# Optimizing a Trainium2 kernel written in Bass

```python
import numpy as np
import jax
import jax.numpy as jnp

def _softmax(x, axis=-1):
    return jax.nn.softmax(x, axis=axis)

def _gelu(x):
    return jax.nn.gelu(x, approximate=True)

def _silu(x):
    return jax.nn.silu(x)

def _sigmoid(x):
    return jax.nn.sigmoid(x)

def _layernorm(x, axis=-1, eps=1e-05):
    m = jnp.mean(x, axis=axis, keepdims=True)
    v = jnp.var(x, axis=axis, keepdims=True)
    return (x - m) / jnp.sqrt(v + eps)

def _scatter_add(tgt, idx, src, axis=0):
    return tgt.at[idx].add(src)

def _segment_sum(src, seg, n):
    return jax.ops.segment_sum(src, seg, n)
kernel_name = 'mk_pixart_resid_d1_seqx_r8_8ba66b'

def setup_inputs(seed: int=0):
    np.random.seed(seed)
    _w = jnp.asarray

    def _rec_inputs():
        import jax
        import jax.numpy as jnp
        _rk = jax.random.key(seed)
        x = -0.0002928 + 1 * jax.random.normal(jax.random.fold_in(_rk, 1), (128, 64, 128), jnp.float32)
        _lenS = 64 - jax.random.randint(jax.random.fold_in(_rk, 7), (128,), 0, max(1, 64 // 4) + 1, jnp.int32)
        _lenS2 = 64 - jax.random.randint(jax.random.fold_in(_rk, 8), (128,), 0, max(1, 64 // 4) + 1, jnp.int32)
        cond_1024 = 0.000887014 + 1.03683 * jax.random.normal(jax.random.fold_in(_rk, 11), (128, 128), jnp.float32)
        _ctx_1024P = jax.random.normal(jax.random.fold_in(_rk, 12), (128, 16, 128), jnp.float32)
        _ctx_1024c = jax.random.dirichlet(jax.random.fold_in(_rk, 512), 0.3 * jnp.ones((16,), jnp.float32), (128, 64))
        _ctx_1024t = jnp.einsum('bsk,bkd->bsd', _ctx_1024c, _ctx_1024P)
        _ctx_1024t = _ctx_1024t * jax.lax.rsqrt(jnp.mean(jnp.square(_ctx_1024t)) + 1e-12) * 0.953939
        ctx_1024 = -0.000761806 + 0.999296 * (_ctx_1024t + 0.3 * jax.random.normal(jax.random.fold_in(_rk, 612), (128, 64, 128), jnp.float32))
        return (x, cond_1024, ctx_1024)
    x, cond_1024, ctx_1024 = _rec_inputs()

    def _L0_xcond_setup():
        import jax, jax.numpy as jnp
        import numpy as np
        import math
        B, S, CTX, D, H, DH = (2, 256, 32, 128, 16, 64)
        INNER = H * DH
        DFF = 4 * D

        def layernorm(x, eps=1e-05):
            m = jnp.mean(x, axis=-1, keepdims=True)
            v = jnp.var(x, axis=-1, keepdims=True)
            return (x - m) * jax.lax.rsqrt(v + eps)

        def adaln(x, t, w, b):
            emb = t @ w + b
            scale, shift = jnp.split(emb, 2, axis=-1)
            return layernorm(x) * (1.0 + scale) + shift

        def mha(xq, ctx, wq, wk, wv, wo, bo):
            b, sq, _ = xq.shape
            sk = ctx.shape[1]
            q = (xq @ wq).reshape(b, sq, H, DH).transpose(0, 2, 1, 3)
            k = (ctx @ wk).reshape(b, sk, H, DH).transpose(0, 2, 1, 3)
            v = (ctx @ wv).reshape(b, sk, H, DH).transpose(0, 2, 1, 3)
            scores = jnp.einsum('bhqd,bhkd->bhqk', q, k) / math.sqrt(DH)
            attn = jax.nn.softmax(scores, axis=-1)
            out = jnp.einsum('bhqk,bhkd->bhqd', attn, v)
            out = out.transpose(0, 2, 1, 3).reshape(b, sq, INNER)
            return out @ wo + bo

        def glu_ff(x, w1, b1, w2, b2):
            u = x @ w1 + b1
            a, gate = jnp.split(u, 2, axis=-1)
            return a * jax.nn.gelu(gate, approximate=False) @ w2 + b2
        key = jax.random.key(seed)
        ks = jax.random.split(key, 24)
        s = 1.0 / math.sqrt(D)

        def n(k, shape, scale=1.0):
            return jax.random.normal(k, shape, dtype=jnp.float32) * scale
        return {'x': n(ks[0], (B, S, D)), 't': n(ks[1], (B, 1, D)), 'context': n(ks[2], (B, CTX, D)), 'attn1_wq': n(ks[3], (D, INNER), s), 'attn1_wk': n(ks[4], (D, INNER), s), 'attn1_wv': n(ks[5], (D, INNER), s), 'attn1_wo': n(ks[6], (INNER, D), s), 'attn1_bo': n(ks[7], (D,), 0.01), 'attn2_wq': n(ks[8], (D, INNER), s), 'attn2_wk': n(ks[9], (D, INNER), s), 'attn2_wv': n(ks[10], (D, INNER), s), 'attn2_wo': n(ks[11], (INNER, D), s), 'attn2_bo': n(ks[12], (D,), 0.01), 'ff_w1': n(ks[13], (D, 2 * DFF), s), 'ff_b1': n(ks[14], (2 * DFF,), 0.01), 'ff_w2': n(ks[15], (DFF, D), 1.0 / math.sqrt(DFF)), 'ff_b2': n(ks[16], (D,), 0.01), 'norm1_w': n(ks[17], (D, 2 * D), s), 'norm1_b': n(ks[18], (2 * D,), 0.01), 'norm2_w': n(ks[19], (D, 2 * D), s), 'norm2_b': n(ks[20], (2 * D,), 0.01), 'norm3_w': n(ks[21], (D, 2 * D), s), 'norm3_b': n(ks[22], (2 * D,), 0.01)}
    _L0_xcond_all = _L0_xcond_setup()
    _L0_xcond_in = {k: v for k, v in _L0_xcond_all.items() if k in ('attn1_wq', 'attn1_wk', 'attn1_wv', 'attn1_wo', 'attn1_bo', 'attn2_wq', 'attn2_wk', 'attn2_wv', 'attn2_wo', 'attn2_bo', 'ff_w1', 'ff_b1', 'ff_w2', 'ff_b2', 'norm1_w', 'norm1_b', 'norm2_w', 'norm2_b', 'norm3_w', 'norm3_b')}
    del _L0_xcond_all

    def _L0_ffn_setup():
        import jax, jax.numpy as jnp
        import numpy as np
        TOP_K = 2
        key = jax.random.key(seed)
        k1, k2, k3, k4 = jax.random.split(key, 4)
        B, S, H, F, E = (2, 256, 128, 352, 8)
        hidden_states = jax.random.normal(k1, (B, S, H), dtype=jnp.float32)
        wqkv = jax.random.normal(k2, (3 * E, H), dtype=jnp.float32) * 0.02
        w1 = jax.random.normal(k3, (E, 2 * F, H), dtype=jnp.float32) * 0.02
        w2 = jax.random.normal(k4, (E, H, F), dtype=jnp.float32) * 0.02
        return {'hidden_states': hidden_states, 'wqkv': wqkv, 'w1': w1, 'w2': w2}
    _L0_ffn_all = _L0_ffn_setup()
    _L0_ffn_in = {k: v for k, v in _L0_ffn_all.items() if k in ('wqkv', 'w1', 'w2')}
    del _L0_ffn_all
    return {'x': x, 'cond_1024': cond_1024, 'ctx_1024': ctx_1024, 'L0_xcond_attn1_wq': _L0_xcond_in['attn1_wq'], 'L0_xcond_attn1_wk': _L0_xcond_in['attn1_wk'], 'L0_xcond_attn1_wv': _L0_xcond_in['attn1_wv'], 'L0_xcond_attn1_wo': _L0_xcond_in['attn1_wo'], 'L0_xcond_attn1_bo': _L0_xcond_in['attn1_bo'], 'L0_xcond_attn2_wq': _L0_xcond_in['attn2_wq'], 'L0_xcond_attn2_wk': _L0_xcond_in['attn2_wk'], 'L0_xcond_attn2_wv': _L0_xcond_in['attn2_wv'], 'L0_xcond_attn2_wo': _L0_xcond_in['attn2_wo'], 'L0_xcond_attn2_bo': _L0_xcond_in['attn2_bo'], 'L0_xcond_ff_w1': _L0_xcond_in['ff_w1'], 'L0_xcond_ff_b1': _L0_xcond_in['ff_b1'], 'L0_xcond_ff_w2': _L0_xcond_in['ff_w2'], 'L0_xcond_ff_b2': _L0_xcond_in['ff_b2'], 'L0_xcond_norm1_w': _L0_xcond_in['norm1_w'], 'L0_xcond_norm1_b': _L0_xcond_in['norm1_b'], 'L0_xcond_norm2_w': _L0_xcond_in['norm2_w'], 'L0_xcond_norm2_b': _L0_xcond_in['norm2_b'], 'L0_xcond_norm3_w': _L0_xcond_in['norm3_w'], 'L0_xcond_norm3_b': _L0_xcond_in['norm3_b'], 'L0_ffn_wqkv': _L0_ffn_in['wqkv'], 'L0_ffn_w1': _L0_ffn_in['w1'], 'L0_ffn_w2': _L0_ffn_in['w2']}

def reference(x, cond_1024, ctx_1024, L0_xcond_attn1_wq, L0_xcond_attn1_wk, L0_xcond_attn1_wv, L0_xcond_attn1_wo, L0_xcond_attn1_bo, L0_xcond_attn2_wq, L0_xcond_attn2_wk, L0_xcond_attn2_wv, L0_xcond_attn2_wo, L0_xcond_attn2_bo, L0_xcond_ff_w1, L0_xcond_ff_b1, L0_xcond_ff_w2, L0_xcond_ff_b2, L0_xcond_norm1_w, L0_xcond_norm1_b, L0_xcond_norm2_w, L0_xcond_norm2_b, L0_xcond_norm3_w, L0_xcond_norm3_b, L0_ffn_wqkv, L0_ffn_w1, L0_ffn_w2):
    import jax
    import jax.numpy as jnp

    def _L0_xcond_ref(x, t, context, attn1_wq, attn1_wk, attn1_wv, attn1_wo, attn1_bo, attn2_wq, attn2_wk, attn2_wv, attn2_wo, attn2_bo, ff_w1, ff_b1, ff_w2, ff_b2, norm1_w, norm1_b, norm2_w, norm2_b, norm3_w, norm3_b):
        import jax, jax.numpy as jnp
        import numpy as np
        import math
        B, S, CTX, D, H, DH = (2, 256, 32, 128, 16, 64)
        INNER = H * DH
        DFF = 4 * D

        def layernorm(x, eps=1e-05):
            m = jnp.mean(x, axis=-1, keepdims=True)
            v = jnp.var(x, axis=-1, keepdims=True)
            return (x - m) * jax.lax.rsqrt(v + eps)

        def adaln(x, t, w, b):
            emb = t @ w + b
            scale, shift = jnp.split(emb, 2, axis=-1)
            return layernorm(x) * (1.0 + scale) + shift

        def mha(xq, ctx, wq, wk, wv, wo, bo):
            b, sq, _ = xq.shape
            sk = ctx.shape[1]
            q = (xq @ wq).reshape(b, sq, H, DH).transpose(0, 2, 1, 3)
            k = (ctx @ wk).reshape(b, sk, H, DH).transpose(0, 2, 1, 3)
            v = (ctx @ wv).reshape(b, sk, H, DH).transpose(0, 2, 1, 3)
            scores = jnp.einsum('bhqd,bhkd->bhqk', q, k) / math.sqrt(DH)
            attn = jax.nn.softmax(scores, axis=-1)
            out = jnp.einsum('bhqk,bhkd->bhqd', attn, v)
            out = out.transpose(0, 2, 1, 3).reshape(b, sq, INNER)
            return out @ wo + bo

        def glu_ff(x, w1, b1, w2, b2):
            u = x @ w1 + b1
            a, gate = jnp.split(u, 2, axis=-1)
            return a * jax.nn.gelu(gate, approximate=False) @ w2 + b2
        h1 = adaln(x, t, norm1_w, norm1_b)
        x = mha(h1, h1, attn1_wq, attn1_wk, attn1_wv, attn1_wo, attn1_bo) + x
        h2 = adaln(x, t, norm2_w, norm2_b)
        x = mha(h2, context, attn2_wq, attn2_wk, attn2_wv, attn2_wo, attn2_bo) + x
        h3 = adaln(x, t, norm3_w, norm3_b)
        x = glu_ff(h3, ff_w1, ff_b1, ff_w2, ff_b2) + x
        return x

    def _L0_ffn_ref(hidden_states, wqkv, w1, w2):
        import jax, jax.numpy as jnp
        import numpy as np
        TOP_K = 2
        b, s, h = hidden_states.shape
        E = w1.shape[0]
        mixed = hidden_states @ wqkv.T
        q, k, v = jnp.split(mixed, 3, axis=-1)
        q = q.astype(jnp.float32)
        k = k.astype(jnp.float32)
        v = v.astype(jnp.float32)
        attn = jax.nn.softmax(q[..., :, None] * k[..., None, :], axis=-1)
        logits = jnp.einsum('bsej,bsj->bse', attn, v).reshape(-1, E)
        top_logits, idx = jax.lax.top_k(logits, TOP_K)
        scores = jax.nn.softmax(top_logits.astype(jnp.float32), axis=-1).astype(hidden_states.dtype)
        N = b * s
        x = hidden_states.reshape(N, h)
        token_ids = jnp.repeat(jnp.arange(N), TOP_K)
        expert_ids = idx.reshape(-1)
        x_rep = x[token_ids]
        out = jnp.zeros_like(x_rep)
        for e in range(E):
            h1 = x_rep @ w1[e].T
            a, g = jnp.split(h1, 2, axis=-1)
            he = jax.nn.silu(a) * g @ w2[e].T
            out = out + jnp.where((expert_ids == e)[:, None], he, jnp.zeros((), out.dtype))
        out = out * scores.reshape(-1, 1)
        combined = out.reshape(N, TOP_K, h).sum(axis=1)
        return combined.reshape(b, s, h)
    x = x + _L0_xcond_ref(_layernorm(x, axis=-1), cond_1024[:, None, :], ctx_1024, L0_xcond_attn1_wq, L0_xcond_attn1_wk, L0_xcond_attn1_wv, L0_xcond_attn1_wo, L0_xcond_attn1_bo, L0_xcond_attn2_wq, L0_xcond_attn2_wk, L0_xcond_attn2_wv, L0_xcond_attn2_wo, L0_xcond_attn2_bo, L0_xcond_ff_w1, L0_xcond_ff_b1, L0_xcond_ff_w2, L0_xcond_ff_b2, L0_xcond_norm1_w, L0_xcond_norm1_b, L0_xcond_norm2_w, L0_xcond_norm2_b, L0_xcond_norm3_w, L0_xcond_norm3_b)
    x = x + _L0_ffn_ref(_layernorm(x, axis=-1), L0_ffn_wqkv, L0_ffn_w1, L0_ffn_w2)
    return x

_drawn_inputs = setup_inputs


def setup_inputs(seed=0):
    import zlib

    import numpy as np

    out = dict(_drawn_inputs(seed))
    spreads = {}
    factors = {'L0_xcond_attn1_bo': 8.0,
     'L0_xcond_attn2_bo': 8.0,
     'L0_xcond_ff_b1': 8.0,
     'L0_xcond_ff_b2': 8.0,
     'L0_xcond_norm1_b': 4.968,
     'L0_xcond_norm2_b': 8.0,
     'L0_xcond_norm3_b': 8.0,
     'L0_ffn_wqkv': 8.0,
     'L0_ffn_w1': 8.0,
     'L0_ffn_w2': 8.0}
    for name, (base, spread) in spreads.items():
        noise = np.random.default_rng([zlib.crc32(name.encode()), seed]).standard_normal(out[name].shape)
        drawn = base * np.exp(spread * noise) if base else spread * noise
        out[name] = jnp.asarray(drawn.astype(out[name].dtype))
    for name, factor in factors.items():
        out[name] = (out[name] * factor).astype(out[name].dtype)
    return out
```

```python
from contextlib import ExitStack

import concourse.bass as bass
from concourse import mybir

F32 = mybir.dt.float32
F32R = mybir.dt.float32r
ALU = mybir.AluOpType
ACT = mybir.ActivationFunctionType
AX_X = mybir.AxisListType.X

P = 128
EPS = 1e-5


def pixart_block_moe(nc, t_in, out):
    x_d, cond_d, ctx_d = t_in["x"], t_in["cond_1024"], t_in["ctx_1024"]
    B, S, D = x_d.shape
    assert D == P and ctx_d.shape[1] == S == 64
    INNER = t_in["L0_xcond_attn1_wq"].shape[1]
    DH = 64
    H = INNER // DH
    HG = 8
    DFF = t_in["L0_xcond_ff_w2"].shape[0]
    FT = DFF // P
    E, F2, _ = t_in["L0_ffn_w1"].shape
    F = F2 // 2
    MT = E * F // P
    assert E * F % P == 0
    CT = 512
    NT = CT // P
    NC = B * S // CT
    SCALE = float(DH) ** -0.5
    UNITS = 2 * H // HG
    assert UNITS == 4

    def segs(j):
        found, r = [], j * P
        while r < (j + 1) * P:
            e = r // F
            end = min((e + 1) * F, (j + 1) * P)
            found.append((e, r - j * P, end - j * P))
            r = end
        return found

    slots = sorted({tuple(segs(j)) for j in range(MT)})
    slot_of = [slots.index(tuple(segs(j))) for j in range(MT)]
    NGL = sum(len(x) for x in slots)

    x_v = x_d.rearrange("(c t s) q d -> c (s q) t d", t=NT, s=2)
    ctx_v = ctx_d.rearrange("(c t s) q d -> c (s q) t d", t=NT, s=2)
    ctx_vs = ctx_d.rearrange("(c t s) q d -> c s q t d", t=NT, s=2)
    out_v = out.rearrange("(c t s) q d -> c (s q) t d", t=NT, s=2)
    emb_s = nc.dram_tensor("emb_s", [B, 6 * D], F32).ap()
    emb_v = emb_s.rearrange("(c t s) (n k) -> c n s t k", t=NT, s=2, n=3)
    x1_s = nc.dram_tensor("x1_s", [NC, P, NT, D], F32).ap()
    n4_s = nc.dram_tensor("n4_s", [NC, 2, P, CT], F32).ap()
    mix_s = nc.dram_tensor("mix_s", [NC, P, NT * 3 * E], F32).ap()
    gate_s = nc.dram_tensor("gate_s", [NC * NT * E, P], F32).ap()
    gate_v = gate_s.rearrange("(c t e) q -> c e t q", t=NT, e=E)

    ctx = ExitStack()
    with ctx:
        def sem(name):
            return ctx.enter_context(nc.semaphore(name))

        def sb(name, shape, dt=F32, where=ctx):
            return where.enter_context(nc.sbuf_tensor(name, shape, dt))

        ident = sb("ident", [P, P])
        half = sb("half", [P, NT])
        eps = sb("eps", [P, NT])
        nothing = sb("nothing", [P, 8])

        with ExitStack() as phase_a:
            def sa(name, shape, dt=F32):
                return sb(name, shape, dt, phase_a)
            Mw = [sa(f"M{a}", [P, 2, H, D], F32R) for a in range(2)]
            Vw = [sa(f"V{a}", [P, 2, H, D], F32R) for a in range(2)]
            W1 = sa("W1", [P, 2, 2 * DFF], F32R)
            W2 = sa("W2", [P, 2, FT, D], F32R)
            WR = sa("WR", [P, 2, 3 * E], F32R)
            b_o = sa("b_o", [P, 2])
            b_1 = sa("b_1", [P, 2 * FT])
            b_2 = sa("b_2", [P, 1])
            with ExitStack() as working:
                def sw(name, shape, dt=F32):
                    return sb(name, shape, dt, working)
                kp = sw("kp", [P, 2, HG, CT], F32R)
                tt = sw("tt", [P, 2, 2, HG // 2, CT], F32R)
                pr = sw("pr", [P, 2, CT])
                pt = sw("pt", [P, 2, CT], F32R)
                hq = [sw(f"hq{k}", [P, 2, NT, 192], F32R) for k in range(2)]
                h3 = sw("h3", [P, 2, CT], F32R)
                cT = sw("cT", [P, 2, CT], F32R)
                h_tm = sw("h_tm", [P, 2, 2, NT, D], F32R)
                c_tm = sw("c_tm", [P, 2, 2, NT, D], F32R)
                x_in = sw("x_in", [P, NT, D])
                c_in = sw("c_in", [P, NT, D])
                modA = sw("modA", [P, NT, 2 * D])
                modB = sw("modB", [P, NT, 2 * D])
                y1 = sw("y1", [P, NT, D])
                y2 = sw("y2", [P, NT, D])
                x_ag = sw("x_ag", [P, NT, D])
                oT = sw("oT", [P, CT])
                htm = sw("htm", [P, NT, D])
                mixed = sw("mixed", [P, NT * 3 * E])
                st = sw("st", [P, NT, 6])
                lv = sw("lv", [P, 12, NT])
                mx = sw("mx", [P, 2, HG])
                sm = sw("sm", [P, 2, HG])
            with ExitStack() as staging:
                def sg(name, shape, dt=F32):
                    return sb(name, shape, dt, staging)
                raw = [[sg(f"raw{a}{k}", [P, INNER]) for k in range(3)] for a in range(2)]
                rawo = [sg(f"rawo{a}", [P, H // 2, D]) for a in range(2)]
                raw1 = sg("raw1", [P, 2 * DFF])
                raw2 = sg("raw2", [P, FT, D])
                rawr = sg("rawr", [3 * E, D])
                rawn = sg("rawn", [P, 3, 2 * D])
                brow = sg("brow", [1, 3, 2 * D])
                rawc = sg("rawc", [B, D])
                wT = [[sg(f"wT{a}{k}", [P, H // 2, P]) for k in range(3)] for a in range(2)]
                condT = sg("condT", [P, B])
                emb = sg("emb", [B, 3, 2 * D])
                ones = sg("ones", [1, P])
        with ExitStack() as phase_b:
            def sbb(name, shape, dt=F32):
                return sb(name, shape, dt, phase_b)
            WE = sbb("WE", [P, 3, 2, MT, P], F32R)
            with ExitStack() as b_work:
                nT = [sb(f"nT{i}", [P, 2, CT], F32R, b_work) for i in range(2)]
                x1b = [sb(f"x1b{i}", [P, NT, D], F32, b_work) for i in range(2)]
                gb = [sb(f"gb{i}", [P, len(slots), CT], F32, b_work) for i in range(2)]
                sil = sb("sil", [P, 2, CT], F32, b_work)
                ug = sb("ug", [P, 4, CT], F32, b_work)
                uu = sb("uu", [P, 4, 2, CT], F32R, b_work)
                oTb = sb("oTb", [P, CT], F32, b_work)
                ob = sb("ob", [P, NT, D], F32, b_work)
            with ExitStack() as b_stage:
                rawe = [sb(f"rawe{k}", [P, MT, P], F32, b_stage) for k in range(3)]
                TT = NC * NT
                mixa = sb("mixa", [P, NC, NT, 3 * E], F32, b_stage)
                qk = sb("qk", [P, TT, E, E], F32, b_stage)
                rr = [sb(f"rr{i}", [P, TT, E], F32, b_stage) for i in range(6)]
                r1 = [sb(f"r1{i}", [P, TT], F32, b_stage) for i in range(4)]
                pri = sb("pri", [P, E], F32, b_stage)
                gT = sb("gT", [P, 4, P], F32, b_stage)

        psum = [ctx.enter_context(nc.psum_tensor(f"ps{i}", [P, CT], F32)) for i in range(8)]
        psS, psK, psT, pst, psO = psum[0:2], psum[2:4], psum[4], psum[5:7], psum[7]

        pads = sem("pads")
        consts, identity = sem("consts"), sem("identity")
        ld_w = [sem(f"ld_w{a}") for a in range(2)]
        ld_m = sem("ld_m")
        ld_b = sem("ld_b")
        su_pe, su_act, su_dve = sem("su_pe"), sem("su_act"), sem("su_dve")
        emb_w = sem("emb_w")
        ld_x, ld_c, ld_mA, ld_mB, ld_xa = sem("ld_x"), sem("ld_c"), sem("ld_mA"), sem("ld_mB"), sem("ld_xa")
        s_done, max_done, sub_done, exp_done = sem("s_done"), sem("max_done"), sem("sub_done"), sem("exp_done")
        sum_done, rec_done, prob_done = sem("sum_done"), sem("rec_done"), sem("prob_done")
        T_done, pt_hi, pt_lo = sem("T_done"), sem("pt_hi"), sem("pt_lo")
        t_done, tt_hi, tt_lo = sem("t_done"), sem("tt_hi"), sem("tt_lo")
        k_done, kp_hi, kp_lo = sem("k_done"), sem("kp_hi"), sem("kp_lo")
        o_done = sem("o_done")
        o_out = sem("o_out")
        back1, back2, backf = sem("back1"), sem("back2"), sem("backf")
        y1_done, y2_done, y3_done, x1_done = sem("y1_done"), sem("y2_done"), sem("y3_done"), sem("x1_done")
        stat = [sem(f"stat{k}") for k in range(4)]
        rstd = [sem(f"rstd{k}") for k in range(4)]
        nrm = [sem(f"nrm{k}") for k in range(4)]
        mods = [sem(f"mods{k}") for k in range(3)]
        hx = [sem(f"hx{k}") for k in range(4)]
        hx_hi = [sem(f"hx_hi{k}") for k in range(4)]
        hx_lo = [sem(f"hx_lo{k}") for k in range(4)]
        tm_hi, tm_lo, tm_sw = sem("tm_hi"), sem("tm_lo"), sem("tm_sw")
        cx, cx_hi, cx_lo = sem("cx"), sem("cx_hi"), sem("cx_lo")
        cm_hi, cm_lo, cm_sw = sem("cm_hi"), sem("cm_lo"), sem("cm_sw")
        ff_done, gel, glu, glu_hi, glu_lo = sem("ff_done"), sem("gel"), sem("glu"), sem("glu_hi"), sem("glu_lo")
        f2_done, f2_out = sem("f2_done"), sem("f2_out")
        rm_done, mix_cp = sem("rm_done"), sem("mix_cp")
        st_x1, st_n4, st_mix = sem("st_x1"), sem("st_n4"), sem("st_mix")

        a_end = sem("a_end")
        ld_e, ld_mx = [sem(f"ld_e{k}") for k in range(3)], sem("ld_mx")
        eu_pe, eu_act, eu_dve = sem("eu_pe"), sem("eu_act"), sem("eu_dve")
        rt, rt_act = sem("rt"), sem("rt_act")
        gt_pe, gt_cp, gt_st = sem("gt_pe"), sem("gt_cp"), sem("gt_st")
        ld_nb, ld_xb, ld_gb = [[sem(f"{n}{i}") for i in range(2)] for n in ("ld_nb", "ld_xb", "ld_gb")]
        ag_done, sil_done, ug_done, uc_done, uh_done, ul_done = (
            sem("ag_done"), sem("sil_done"), sem("ug_done"), sem("uc_done"), sem("uh_done"), sem("ul_done"))
        mo_done, mo_out, mb_done, ob_done = sem("mo_done"), sem("mo_out"), sem("mb_done"), sem("ob_done")
        e_done = sem("e_done")
        st_out = sem("st_out")

        block = ctx.enter_context(nc.Block())

        def mm3(ps, w, m, first=True, last=True, add=False):
            for n, (i, j) in enumerate([(1, 0), (0, 1), (0, 0)]):
                mm = nc.tensor.matmul(ps, w(i), m(j), start=(first and n == 0), stop=(last and n == 2))
            return mm

        def f32(ap):
            return ap.bitcast(F32)

        SR = [psum[i] for i in range(4)]
        tiles = []
        for a in range(2):
            for k in range(3):
                for g in range(H // 8):
                    tiles.append(("T", a, k, g))
            for g in range(H // 4):
                tiles.append(("M", a, g))
            for g in range(H // 4):
                tiles.append(("V", a, g))
        tiles += [("R",), ("C",), ("E", 0), ("E", 1), ("E", 2)]
        NSU = len(tiles)
        t_of = {t: n for n, t in enumerate(tiles)}
        EU = [(k, g) for k in range(3) for g in range((MT + 3) // 4)]
        NEU = len(EU)
        LAG = 3

        NLD = [sum(len(segs(j)) for j in range(MT))] * 2 + [1]
        RT_DIFF = 8 + E + 5 + 1 + 5 + 1
        RT_LAST = RT_DIFF + 6

        def pair(ap):
            return ap.rearrange("p t (b k) -> p t b k", k=64)[:, :, 0:3:2, :]

        @block.sync
        def _(sp):
            for a in range(2):
                for k, n in enumerate(("wq", "wk", "wv")):
                    sp.dma_start(raw[a][k][:], t_in[f"L0_xcond_attn{a + 1}_{n}"]).then_inc(ld_w[a], 16)
                sp.dma_start(rawo[a][:], t_in[f"L0_xcond_attn{a + 1}_wo"].rearrange("(t p) n -> p t n", p=P)).then_inc(ld_w[a], 16)
            sp.dma_start(rawr[:], t_in["L0_ffn_wqkv"]).then_inc(ld_m, 16)
            sp.dma_start(rawc[:], cond_d).then_inc(ld_m, 16)
            for n in range(3):
                sp.dma_start(rawn[:, n, :], t_in[f"L0_xcond_norm{n + 1}_w"]).then_inc(ld_m, 16)
                sp.dma_start(brow[:, n, :], t_in[f"L0_xcond_norm{n + 1}_b"].unsqueeze(0)).then_inc(ld_m, 16)
            sp.dma_start(raw1[:], t_in["L0_xcond_ff_w1"]).then_inc(ld_m, 16)
            sp.dma_start(raw2[:], t_in["L0_xcond_ff_w2"].rearrange("(t p) n -> p t n", p=P)).then_inc(ld_m, 16)
            for a in range(2):
                sp.dma_start(b_o[:, a:a + 1], t_in[f"L0_xcond_attn{a + 1}_bo"].unsqueeze(1)).then_inc(ld_b, 16)
            sp.dma_start(b_1[:], t_in["L0_xcond_ff_b1"].rearrange("(t p) -> p t", p=P), allow_slow_non_contiguous=True).then_inc(ld_b, 16)
            sp.dma_start(b_2[:], t_in["L0_xcond_ff_b2"].unsqueeze(1)).then_inc(ld_b, 16)
            sp.wait_ge(su_act, NSU + 2)
            sp.wait_ge(su_dve, NSU + 2)
            sp.dma_start(emb_s, emb[:].rearrange("p n k -> p (n k)")).then_inc(emb_w, 16)
            sp.wait_ge(emb_w, 16)

            def load_x(c):
                sp.dma_start(x_in[:], x_v[c]).then_inc(ld_x, 16)
                for s in range(2):
                    sp.dma_start(modA[64 * s:64 * s + 64], emb_v[c, 0, s].partition_broadcast(64)).then_inc(ld_mA, 16)

            def load_modB(c, n):
                for s in range(2):
                    sp.dma_start(modB[64 * s:64 * s + 64], emb_v[c, n, s].partition_broadcast(64)).then_inc(ld_mB, 16)

            def swap(src, swapped):
                for k in range(2):
                    for s in range(2):
                        sp.dma_start(f32(src[64 * s:64 * s + 64, k, 1]), f32(src[64 - 64 * s:128 - 64 * s, k, 0])).then_inc(swapped, 16)

            def after_x1(c):
                sp.wait_ge(x1_done, c + 2)
                sp.dma_start(x1_s[c], y2[:]).then_inc(st_x1, 16)
                sp.wait_ge(hx_hi[3], c + 1)
                sp.wait_ge(hx_lo[3], c + 1)
                sp.dma_start(n4_s[c].rearrange("k p n -> p k n"), f32(h3[:])).then_inc(st_n4, 16)
                sp.wait_ge(mix_cp, c + 1)
                sp.dma_start(mix_s[c], mixed[:]).then_inc(st_mix, 16)

            def body(c, first=False, last=False):
                if not first:
                    sp.wait_ge(x1_done, c)
                    sp.dma_start(x_ag[:], x_v[c - 1]).then_inc(ld_xa, 16)
                    sp.wait_ge(cx, c)
                    sp.wait_ge(cm_hi, c)
                    sp.wait_ge(cm_lo, c)
                sp.dma_start(c_in[:], ctx_v[c]).then_inc(ld_c, 16)
                if not first:
                    sp.wait_ge(mods[2], 2 * c)
                load_modB(c, 1)
                sp.wait_ge(cm_hi, c + 1)
                sp.wait_ge(cm_lo, c + 1)
                swap(c_tm, cm_sw)
                if not last:
                    sp.wait_ge(y1_done, c + 1)
                    load_x(c + 1)
                sp.wait_ge(mods[1], 2 * c + 2)
                load_modB(c, 2)
                if not first:
                    after_x1(c - 1)
                if not last:
                    sp.wait_ge(tm_hi, c + 2)
                    sp.wait_ge(tm_lo, c + 2)
                    swap(h_tm, tm_sw)

            load_x(0)
            sp.wait_ge(tm_hi, 1)
            sp.wait_ge(tm_lo, 1)
            swap(h_tm, tm_sw)
            body(0, first=True)
            with sp.Fori(1, NC - 1) as c:
                body(c)
            body(NC - 1, last=True)
            sp.wait_ge(x1_done, NC)
            sp.dma_start(x_ag[:], x_v[NC - 1]).then_inc(ld_xa, 16)
            after_x1(NC - 1)
            sp.wait_ge(st_x1, 16 * (NC + 1))
            sp.wait_ge(st_n4, 16 * (NC + 1))
            sp.wait_ge(st_mix, 16 * (NC + 1))

            sp.wait_ge(a_end, 4)
            sp.dma_start(mixa[:].rearrange("p c t k -> p c (t k)"), mix_s.rearrange("c p k -> p c k")).then_inc(ld_mx, 16)
            w1_ = t_in["L0_ffn_w1"]
            for k in range(2):
                for j in range(MT):
                    for e, p0, p1 in segs(j):
                        f0 = j * P + p0 - e * F + k * F
                        sp.dma_start(rawe[k][p0:p1, j, :], w1_[e, f0:f0 + p1 - p0, :]).then_inc(ld_e[k], 16)
            sp.dma_start(rawe[2][:].rearrange("p a b -> p (a b)").rearrange("p (e f) -> p e f", e=E),
                         t_in["L0_ffn_w2"].rearrange("e o f -> o e f")).then_inc(ld_e[2], 16)
            sp.wait_ge(gt_cp, 1)
            sp.dma_start(gate_s.rearrange("(g p) q -> p g q", p=P), gT[:]).then_inc(gt_st, 16)
            sp.wait_ge(gt_st, 16)
            sp.wait_ge(eu_act, NEU)
            sp.wait_ge(eu_dve, NEU)

            def load_b(c, i):
                sp.dma_start(f32(nT[i][:]), n4_s[c].rearrange("k p n -> p k n")).then_inc(ld_nb[i], 16)
                for n, parts in enumerate(slots):
                    for e, p0, p1 in parts:
                        sp.dma_start(gb[i][p0:p1, n, :].rearrange("p (t q) -> p t q", t=NT),
                                     gate_v[c, e].partition_broadcast(p1 - p0)).then_inc(ld_gb[i], 16)
                sp.dma_start(x1b[i][:], x1_s[c]).then_inc(ld_xb[i], 16)

            load_b(0, 0)
            load_b(1, 1)
            with sp.Fori(0, NC // 2 - 1) as d:
                for i in range(2):
                    sp.wait_ge(ob_done, 2 * d + i + 1)
                    sp.dma_start(out_v[2 * d + i], ob[:]).then_inc(st_out, 16)
                    sp.wait_ge(ag_done, (2 * d + i + 1) * MT)
                    sp.wait_ge(uc_done, (2 * d + i + 1) * MT)
                    load_b(2 * d + i + 2, i)
            for i in range(2):
                sp.wait_ge(ob_done, NC - 1 + i)
                sp.dma_start(out_v[NC - 2 + i], ob[:]).then_inc(st_out, 16)
            sp.wait_ge(st_out, 16 * (NC + 1))

        @block.tensor
        def _(pe):
            pe.wait_ge(consts, 3)
            pe.wait_ge(identity, 2)
            for n, tile in enumerate(tiles):
                ps = SR[n % 4]
                if n >= 4:
                    pe.wait_ge(su_dve, n - 3)
                if tile[0] == "T":
                    _, a, k, g = tile
                    pe.wait_ge(ld_w[a], 64)
                    for i in range(4):
                        mm = nc.tensor.transpose(ps[:, i * P:(i + 1) * P], raw[a][k][:, (4 * g + i) * P:(4 * g + i + 1) * P], ident[:])
                elif tile[0] in "MV":
                    kind, a, g = tile
                    pe.wait_ge(su_dve, t_of[("T", a, 2, 1)] + 1)
                    for i in range(4):
                        h = 8 * (g // 2) + 2 * i + g % 2
                        lo = 64 * (h % 2)
                        w = wT[a][1 if kind == "M" else 2][lo:lo + 64, h // 2, :]
                        m = wT[a][0][lo:lo + 64, h // 2, :] if kind == "M" else rawo[a][lo:lo + 64, h // 2, :]
                        mm = nc.tensor.matmul(ps[:, i * P:(i + 1) * P], w, m, start=True, stop=True)
                elif tile[0] == "R":
                    pe.wait_ge(ld_m, 160)
                    mm = nc.tensor.transpose(ps[:, 0:3 * E], rawr[:], ident[0:3 * E, 0:3 * E])
                elif tile[0] == "C":
                    mm = nc.tensor.transpose(ps[:, 0:B], rawc[:], ident[:])
                else:
                    pe.wait_ge(su_dve, t_of[("C",)] + 1)
                    nc.tensor.matmul(ps[:, 0:2 * D], condT[:], rawn[:, tile[1], :], start=True, stop=False)
                    mm = nc.tensor.matmul(ps[:, 0:2 * D], ones[:], brow[:, tile[1], :], start=False, stop=True)
                mm.then_inc(su_pe, 1)

            def keys(c, u, hs, before=None):
                a, g = divmod(u, 2)
                for h in hs:
                    n = c * 4 * HG + u * HG + h
                    if not (isinstance(n, int) and n < 2):
                        pe.wait_ge(kp_lo, n - 1)
                    src = (lambda k: pair(hq[0][:, k])) if a == 0 else (lambda k: cT[:, k, :])
                    ps = psK[h % 2][:]
                    if a == 0:
                        ps = ps.rearrange("p (t s q) -> p t s q", t=NT, s=2)
                    mm3(ps, lambda k: Mw[a][:, k, g * HG + h, :], src).then_inc(k_done, 1)

            def scores(c, u, p):
                n = c * 16 + u * 4 + p
                if p == 0:
                    pe.wait_ge(kp_lo, c * 4 * HG + (u + 1) * HG)
                if not (isinstance(n, int) and n < 2):
                    pe.wait_ge(sub_done, n - 1)
                for s in range(2):
                    for q, (i, j) in enumerate(((1, 0), (0, 1), (0, 0))):
                        mm = nc.tensor.matmul(psS[p % 2][:].rearrange("p (h k) -> p h k", h=HG),
                                              hq[u // 2][:, i, p, 64 * s:64 * s + P],
                                              kp[:, j, :, p * P + 64 * s:p * P + 64 * s + 64],
                                              start=(s == 0 and q == 0), stop=(s == 1 and q == 2))
                mm.then_inc(s_done, 1)

            def turn(c, u, p, free=None):
                n = c * 16 + u * 4 + p
                if not (isinstance(n, int) and n < 1):
                    pe.wait_ge(pt_lo, n)
                if free:
                    pe.wait_ge(*free)
                pe.wait_ge(prob_done, n + 1)
                for i in range(4):
                    mm = nc.tensor.transpose(psT[:, i * P:(i + 1) * P], pr[:, p % 2, i * P:(i + 1) * P], ident[:])
                mm.then_inc(T_done, 1)

            def weigh(c, u, p):
                n = c * 16 + u * 4 + p
                tm, swapped = (h_tm, tm_sw) if u < 2 else (c_tm, cm_sw)
                if p == 0 and u % 2 == 0:
                    pe.wait_ge(swapped, 64 * (c + 1))
                pe.wait_ge(pt_lo, n + 1)
                if not (isinstance(n, int) and n < 1):
                    pe.wait_ge(tt_lo, 2 * n)
                for s in range(2):
                    for q, (i, j) in enumerate(((1, 0), (0, 1), (0, 0))):
                        for par in range(2):
                            rows = slice(64 * par, 64 * par + 64)
                            mm = nc.tensor.matmul(pst[par][:].rearrange("p (h r k) -> p h r k", h=4, r=2)[:, :, s, :],
                                                  tm[rows, i, (par + s) % 2, p, :],
                                                  pt[rows, j, :].rearrange("p (h r k) -> p h r k", h=4, r=2)[:, :, s, :],
                                                  start=(q == 0), stop=(q == 2))
                            if s == 1 and q == 2:
                                mm.then_inc(t_done, 1)

            def project(c, u):
                a, g = divmod(u, 2)
                pe.wait_ge(tt_lo, 2 * (c * 16 + u * 4 + 4))
                for h in range(HG):
                    mm = mm3(psO[:], lambda k: Vw[a][:, k, g * HG + h, :], lambda k: tt[:, k, h % 2, h // 2, :],
                             first=(g == 0 and h == 0), last=(g == 1 and h == HG - 1))
                mm.then_inc(o_done, 1)

            def turn4(done, src):
                for i in range(4):
                    mm = nc.tensor.transpose(psT[:, i * P:(i + 1) * P], src(i), ident[:])
                mm.then_inc(done, 1)

            def back(done):
                turn4(done, lambda i: oT[:, i * P:(i + 1) * P])

            def ln_turn(k):
                turn4(hx[k], lambda i: htm[:, i, :])

            def glu_up(c, f):
                if f % 2 == 0:
                    ba, bg = psK
                else:
                    ba, bg = psS
                mm3(ba[:], lambda k: W1[:, k, f * P:(f + 1) * P], lambda k: h3[:, k, :])
                mm3(bg[:], lambda k: W1[:, k, DFF + f * P:DFF + (f + 1) * P], lambda k: h3[:, k, :]).then_inc(ff_done, 1)

            def glu_down(c):
                pe.wait_ge(glu_lo, FT * (c + 1))
                pe.wait_ge(glu_hi, FT * (c + 1))
                for f in range(FT):
                    mm = mm3(psO[:], lambda k: W2[:, k, f, :], lambda k: tt[:, k, 0, f, :], first=f == 0, last=f == FT - 1)
                mm.then_inc(f2_done, 1)

            def router(c):
                for t in range(NT):
                    mm = mm3(psT[:, t * 3 * E:(t + 1) * 3 * E], lambda k: h3[:, k, t * P:(t + 1) * P], lambda k: WR[:, k, :])
                mm.then_inc(rm_done, 1)

            def unit(c, u, mid=None, hook_a=None, hook_b=None, free0=None, free1=None, free2=None, nxt=True):
                scores(c, u, 0)
                scores(c, u, 1)
                if mid:
                    mid()
                turn(c, u, 0, free0)
                scores(c, u, 2)
                if hook_a:
                    hook_a()
                weigh(c, u, 0)
                turn(c, u, 1, free1)
                scores(c, u, 3)
                if hook_b:
                    hook_b()
                weigh(c, u, 1)
                turn(c, u, 2, free2)
                un, cn = (u + 1) % 4, c + (u + 1) // 4
                if nxt:
                    if un == 0:
                        pe.wait_ge(hx_lo[0], cn + 1)
                    if un == 2:
                        pe.wait_ge(cx_lo, cn + 1)
                    keys(cn, un, range(0, HG // 2))
                weigh(c, u, 2)
                turn(c, u, 3)
                if nxt:
                    keys(cn, un, range(HG // 2, HG))
                weigh(c, u, 3)

            def body(c, first=False, last=False):
                n = c * 16
                def mid0():
                    project(c - 1, 3)

                def hook0():
                    pe.wait_ge(pt_lo, n + 1)
                    pe.wait_ge(o_out, 2 * c)
                    back(back2)

                pe.wait_ge(hx_lo[0], c + 1)
                if first:
                    unit(c, 0, free0=(hx_lo[0], 1))
                else:
                    unit(c, 0, mid=mid0, hook_a=hook0, free1=(y2_done, c))
                    pe.wait_ge(pt_lo, n + 4)
                    pe.wait_ge(mods[2], 2 * c)
                    ln_turn(2)

                def mid1():
                    if not first:
                        pe.wait_ge(o_out, 2 * c)
                    project(c, 0)

                def hook1():
                    pe.wait_ge(pt_lo, n + 5)
                    pe.wait_ge(ld_c, 16 * (c + 1))
                    turn4(cx, lambda i: c_in[:, i, :])

                unit(c, 1, mid=mid1, hook_a=hook1, free0=None if first else (hx_lo[2], c), free1=(cx_lo, c + 1))
                project(c, 1)
                if not first:
                    pe.wait_ge(hx_lo[2], c)
                    pe.wait_ge(kp_lo, c * 4 * HG + 3 * HG)
                    glu_up(c - 1, 0)
                pe.wait_ge(pt_lo, n + 8)
                pe.wait_ge(o_out, 2 * c + 1)
                back(back1)
                if not first:
                    pe.wait_ge(sub_done, n + 8)
                    glu_up(c - 1, 1)
                    for f in range(2, FT):
                        pe.wait_ge(glu, FT * (c - 1) + f - 1)
                        glu_up(c - 1, f)
                pe.wait_ge(y1_done, c + 1)
                pe.wait_ge(mods[1], 2 * c + 2)
                ln_turn(1)
                pe.wait_ge(hx_lo[1], c + 1)
                if not first:
                    pe.wait_ge(glu, FT * c)

                def mid2():
                    pe.wait_ge(o_out, 2 * c + 1)
                    glu_down(c - 1)

                def hook2():
                    pe.wait_ge(pt_lo, n + 9)
                    pe.wait_ge(f2_out, c)
                    back(backf)

                if first:
                    unit(c, 2, free0=(hx_lo[1], c + 1))
                else:
                    unit(c, 2, mid=mid2, hook_a=hook2, free0=(hx_lo[1], c + 1), free1=(y3_done, c))
                    pe.wait_ge(pt_lo, n + 12)
                    pe.wait_ge(nrm[3], c)
                    ln_turn(3)

                def mid3():
                    if not first:
                        pe.wait_ge(f2_out, c)
                    project(c, 2)

                def hook3():
                    pe.wait_ge(pt_lo, n + 13)
                    pe.wait_ge(mods[0], 2 * c + 4)
                    ln_turn(0)

                def hook3b():
                    pe.wait_ge(pt_lo, n + 14)
                    router(c - 1)

                if not last:
                    pass
                unit(c, 3, mid=mid3, hook_a=None if last else hook3, hook_b=None if first else hook3b,
                     free0=None if first else (hx_lo[3], c), free1=None if last else (hx_lo[0], c + 2),
                     free2=None if first else (mix_cp, c), nxt=not last)

            pe.wait_ge(pads, 2)
            pe.wait_ge(mods[0], 2)
            ln_turn(0)
            pe.wait_ge(hx_lo[0], 1)
            keys(0, 0, range(HG))
            body(0, first=True)
            with pe.Fori(1, NC - 1) as c:
                body(c)
            body(NC - 1, last=True)
            project(NC - 1, 3)
            pe.wait_ge(pt_lo, 16 * NC)
            pe.wait_ge(o_out, 2 * NC)
            back(back2)
            pe.wait_ge(y2_done, NC)
            pe.wait_ge(mods[2], 2 * NC)
            ln_turn(2)
            pe.wait_ge(hx_lo[2], NC)
            pe.wait_ge(sub_done, 16 * NC)
            for f in range(FT):
                if f >= 2:
                    pe.wait_ge(glu, FT * (NC - 1) + f - 1)
                glu_up(NC - 1, f)
            glu_down(NC - 1)
            pe.wait_ge(f2_out, NC)
            back(backf)
            pe.wait_ge(y3_done, NC)
            pe.wait_ge(nrm[3], NC)
            ln_turn(3)
            pe.wait_ge(hx_lo[3], NC)
            router(NC - 1)
            pe.drain().then_inc(a_end, 1)

            pe.wait_ge(mix_cp, NC)
            for n, (k, g) in enumerate(EU):
                if n >= 4:
                    pe.wait_ge(eu_dve, n - 3)
                else:
                    pe.wait_ge(a_end, 4)
                pe.wait_ge(ld_e[k], 16 * NLD[k])
                for i, j in enumerate(range(4 * g, min(4 * g + 4, MT))):
                    mm = nc.tensor.transpose(SR[n % 4][:, i * P:(i + 1) * P], rawe[k][:, j, :], ident[:])
                mm.then_inc(eu_pe, 1)
            pe.wait_ge(rt, RT_LAST)
            for i in range(4):
                mm = nc.tensor.transpose(psum[7][:, i * P:(i + 1) * P], rr[5][:].rearrange("p t e -> p (t e)")[:, i * P:(i + 1) * P], ident[:])
            mm.then_inc(gt_pe, 1)
            pe.wait_ge(eu_act, NEU)
            pe.wait_ge(eu_dve, NEU)
            pe.wait_ge(gt_cp, 1)

            def up(c, i, j, first):
                m = c * MT + j
                if not (first and j < 3):
                    pe.wait_ge(ug_done, m - 1 if i == 0 and j < 2 else m - 2)
                b = (j + i) % 3
                mm3(psum[b][:], lambda k: WE[:, 0, k, j, :], lambda k: nT[i][:, k, :])
                mm3(psum[3 + b][:], lambda k: WE[:, 1, k, j, :], lambda k: nT[i][:, k, :]).then_inc(ag_done, 1)

            def down(c, i, j):
                r = (i * MT + j) % 4
                pe.wait_ge(ul_done, c * MT + j + 1)
                mm = mm3(psum[6][:], lambda k: WE[:, 2, k, j, :], lambda k: uu[:, r, k, :], first=j == 0, last=j == MT - 1)
                mm.then_inc(e_done, 1)

            def back_b(c):
                pe.wait_ge(mo_out, c + 1)
                if not (isinstance(c, int) and c == 0):
                    pe.wait_ge(ob_done, c)
                for t in range(4):
                    mm = nc.tensor.transpose(psum[7][:, t * P:(t + 1) * P], oTb[:, t * P:(t + 1) * P], ident[:])
                mm.then_inc(mb_done, 1)

            def chunk(c, i, first=False):
                for j in range(MT):
                    if j == 0:
                        pass
                    up(c, i, j, first)
                    if j >= LAG:
                        if j == LAG and not first:
                            pe.wait_ge(mo_out, c)
                        down(c, i, j - LAG)
                    elif not first:
                        down(c - 1, 1 - i, MT + j - LAG)
                    if j == LAG + 2 and not first:
                        back_b(c - 1)

            pe.wait_ge(ld_nb[0], 16)
            chunk(0, 0, first=True)
            pe.wait_ge(ld_nb[1], 16)
            chunk(1, 1)
            with pe.Fori(1, NC // 2) as d:
                for i in range(2):
                    pe.wait_ge(ld_nb[i], 16 * d + 16)
                    chunk(2 * d + i, i)
            for j in range(MT - LAG, MT):
                down(NC - 1, 1, j)
            back_b(NC - 1)

        @block.scalar
        def _(act):
            def copy(o, i):
                return nc.scalar.activation(o, i, ACT.Copy)

            for n, tile in enumerate(tiles):
                ps = SR[n % 4]
                act.wait_ge(su_pe, n + 1)
                if tile[0] == "T":
                    _, a, k, g = tile
                    op = copy(wT[a][k][:, 4 * g:4 * g + 2, :].rearrange("p a b -> p (a b)"), ps[:, 0:2 * P])
                elif tile[0] in "MV":
                    kind, a, g = tile
                    dst = (Mw if kind == "M" else Vw)[a]
                    op = copy(dst[:, 0, 8 * (g // 2) + g % 2:8 * (g // 2) + 8:2, :], ps[:].rearrange("p (a b) -> p a b", a=4))
                elif tile[0] == "R":
                    op = copy(WR[:, 0, :], ps[:, 0:3 * E])
                elif tile[0] == "C":
                    op = copy(condT[:, 0:B // 2], ps[:, 0:B // 2])
                else:
                    op = copy(emb[:, tile[1], D:2 * D], ps[:, D:2 * D])
                op.then_inc(su_act, 1)
            act.wait_ge(ld_m, 160)
            copy(W1[:, 0, :], raw1[:]).then_inc(su_act, 1)
            copy(W2[:, 0], raw2[:]).then_inc(su_act, 1)
            act.wait_ge(ld_b, 64)

            def exp(c, u, p):
                act.wait_ge(sub_done, c * 16 + u * 4 + p + 1)
                nc.scalar.activation(pr[:, p % 2, :], pr[:, p % 2, :], ACT.Exp, scale=SCALE).then_inc(exp_done, 1)

            def turn_hi(c, u, p):
                n = c * 16 + u * 4 + p
                act.wait_ge(T_done, n + 1)
                if not (isinstance(n, int) and n < 1):
                    act.wait_ge(t_done, 2 * n)
                copy(pt[:, 0, :], psT[:]).then_inc(pt_hi, 1)

            def tt_out(k, p, s):
                return tt[:, k, s, :, p * P:(p + 1) * P]

            def weigh_hi(c, u, p):
                n = c * 16 + u * 4 + p
                if p == 0:
                    if not (isinstance(n, int) and n < 1):
                        act.wait_ge(o_done, c * 4 + u)
                    if u == 2 and not (isinstance(c, int) and c == 0):
                        act.wait_ge(f2_done, c)
                for s in range(2):
                    act.wait_ge(t_done, 2 * n + s + 1)
                    copy(tt_out(0, p, s), pst[s][:].rearrange("p (h q) -> p h q", h=4)).then_inc(tt_hi, 1)

            def keys_hi(c, u, hs):
                for h in hs:
                    n = c * 4 * HG + u * HG + h
                    act.wait_ge(k_done, n + 1)
                    copy(kp[:, 0, h, :], psK[h % 2][:]).then_inc(kp_hi, 1)

            def out_attn(c, a):
                act.wait_ge(o_done, 4 * c + 2 * a + 2)
                if a == 0:
                    if not (isinstance(c, int) and c == 0):
                        act.wait_ge(back2, c)
                else:
                    act.wait_ge(back1, c + 1)
                    if not (isinstance(c, int) and c == 0):
                        act.wait_ge(backf, c)
                nc.scalar.activation(oT[:], psO[:], ACT.Identity, bias=b_o[:, a:a + 1]).then_inc(o_out, 1)

            def ln_hi(k, c):
                act.wait_ge(hx[k], c + 1)
                src = psT[:]
                if k < 2:
                    dst, src = pair(hq[k][:, 0]), src.rearrange("p (t s q) -> p t s q", t=NT, s=2)
                else:
                    dst = h3[:, 0, :]
                if k == 2:
                    act.wait_ge(st_n4, 16 * (c + 1))
                copy(dst, src).then_inc(hx_hi[k], 1)

            def glu_act(c, f):
                act.wait_ge(ff_done, FT * c + f + 1)
                bg = psK[1] if f % 2 == 0 else psS[1]
                if f < 2:
                    act.wait_ge(T_done, 16 * (c + 1) + GLU_AT[0] if not tail[0] else 16 * NC)
                else:
                    act.wait_ge(glu_lo, FT * c + f - 1)
                nc.scalar.activation(pr[:, f % 2, :], bg[:], ACT.Gelu, bias=b_1[:, FT + f:FT + f + 1]).then_inc(gel, 1)

            def glu_split(c, f):
                act.wait_ge(glu, FT * c + f + 1)
                if f == 0:
                    act.wait_ge(o_done, 4 * (c + 1) + 2 if not tail[0] else 4 * NC)
                copy(tt[:, 0, 0, f, :], pr[:, f % 2, :]).then_inc(glu_hi, 1)

            tail = [False]
            GLU_AT = [8]

            def out_glu(c):
                act.wait_ge(f2_done, c + 1)
                if tail[0]:
                    act.wait_ge(back2, c + 1)
                else:
                    act.wait_ge(back1, c + 2)
                nc.scalar.activation(oT[:], psO[:], ACT.Identity, bias=b_2[:, 0:1]).then_inc(f2_out, 1)

            def mix_out(c):
                act.wait_ge(rm_done, c + 1)
                act.wait_ge(st_mix, 16 * (c + 1))
                copy(mixed[:], psT[:, 0:NT * 3 * E]).then_inc(mix_cp, 1)

            def tm_split(c):
                act.wait_ge(mods[0], 2 * c + 2)
                if not (isinstance(c, int) and c == 0):
                    act.wait_ge(t_done, 32 * (c - 1) + 16)
                copy(h_tm[:, 0, 0], htm[:]).then_inc(tm_hi, 1)

            def unit(c, u, mid=None, hook_a=None, hook_b=None, nxt=True):
                exp(c, u, 0)
                exp(c, u, 1)
                if mid:
                    mid()
                turn_hi(c, u, 0)
                exp(c, u, 2)
                if hook_a:
                    hook_a()
                weigh_hi(c, u, 0)
                turn_hi(c, u, 1)
                exp(c, u, 3)
                if hook_b:
                    hook_b()
                weigh_hi(c, u, 1)
                turn_hi(c, u, 2)
                un, cn = (u + 1) % 4, c + (u + 1) // 4
                if nxt:
                    keys_hi(cn, un, range(0, HG // 2))
                weigh_hi(c, u, 2)
                turn_hi(c, u, 3)
                if nxt:
                    keys_hi(cn, un, range(HG // 2, HG))
                weigh_hi(c, u, 3)

            def context(c):
                act.wait_ge(cx, c + 1)
                copy(cT[:, 0, :], psT[:]).then_inc(cx_hi, 1)
                act.wait_ge(ld_c, 16 * (c + 1))
                if not (isinstance(c, int) and c == 0):
                    act.wait_ge(t_done, 32 * c)
                copy(c_tm[:, 0, 0], c_in[:]).then_inc(cm_hi, 1)

            def next_ln1(c):
                ln_hi(0, c)
                tm_split(c)

            def body(c, first=False, last=False):
                unit(c, 0, mid=None if first else (lambda: out_attn(c - 1, 1)))
                if not first:
                    ln_hi(2, c - 1)
                unit(c, 1, hook_a=lambda: context(c))
                out_attn(c, 0)
                if not first:
                    for f in range(FT):
                        glu_act(c - 1, f)
                        if f >= 1:
                            glu_split(c - 1, f - 1)
                    glu_split(c - 1, FT - 1)
                ln_hi(1, c)
                unit(c, 2, mid=None if first else (lambda: out_glu(c - 1)))
                if not first:
                    ln_hi(3, c - 1)
                unit(c, 3, hook_a=None if last else (lambda: next_ln1(c + 1)),
                     hook_b=None if first else (lambda: mix_out(c - 1)), nxt=not last)

            ln_hi(0, 0)
            tm_split(0)
            keys_hi(0, 0, range(HG))
            body(0, first=True)
            with act.Fori(1, NC - 1) as c:
                body(c)
            body(NC - 1, last=True)
            tail[0] = True
            out_attn(NC - 1, 1)
            ln_hi(2, NC - 1)
            for f in range(FT):
                glu_act(NC - 1, f)
                if f >= 1:
                    glu_split(NC - 1, f - 1)
            glu_split(NC - 1, FT - 1)
            out_glu(NC - 1)
            ln_hi(3, NC - 1)
            mix_out(NC - 1)
            act.drain().then_inc(a_end, 1)

            act.wait_ge(a_end, 4)
            act.wait_ge(rt, 3)
            nc.scalar.activation(qk[:], qk[:], ACT.Exp).then_inc(rt_act, 1)
            for n, (k, g) in enumerate(EU):
                if n == 4:
                    act.wait_ge(rt, RT_DIFF)
                    nc.scalar.activation(r1[3][:], r1[3][:], ACT.Exp).then_inc(rt_act, 1)
                act.wait_ge(eu_pe, n + 1)
                w = min(4, MT - 4 * g)
                copy(WE[:, k, 0, 4 * g:4 * g + w, :].rearrange("p a b -> p (a b)"), SR[n % 4][:, 0:w * P]).then_inc(eu_act, 1)

            def silu(c, i, j, first=False):
                m = c * MT + j
                act.wait_ge(ag_done, m + 1)
                if not (first and j < 2):
                    act.wait_ge(ug_done, m - 1)
                nc.scalar.activation(sil[:, j % 2, :], psum[(j + i) % 3][:], ACT.Silu).then_inc(sil_done, 1)

            def uhi(c, i, j):
                m = c * MT + j
                r = (i * MT + j) % 4
                act.wait_ge(uc_done, m + 1)
                if not (isinstance(m, int) and m < 4):
                    act.wait_ge(e_done, m - 3)
                copy(uu[:, r, 0, :], ug[:, r, :]).then_inc(uh_done, 1)

            def out_b(c):
                act.wait_ge(e_done, (c + 1) * MT)
                if not (isinstance(c, int) and c == 0):
                    act.wait_ge(mb_done, c)
                copy(oTb[:], psum[6][:]).then_inc(mo_out, 1)

            def chunk(c, i, first=False):
                for j in range(MT):
                    silu(c, i, j, first)
                    if j >= 1:
                        uhi(c, i, j - 1)
                    elif not first:
                        uhi(c - 1, 1 - i, MT - 1)
                    if j == LAG and not first:
                        out_b(c - 1)

            chunk(0, 0, first=True)
            chunk(1, 1)
            with act.Fori(1, NC // 2) as d:
                for i in range(2):
                    chunk(2 * d + i, i)
            uhi(NC - 1, 1, MT - 1)
            out_b(NC - 1)

        @block.vector
        def _(dve):
            tensor = nc.vector.tensor_tensor
            nc.vector.memset(half[:], -0.5).then_inc(consts, 1)
            nc.vector.memset(ones[:], 1.0).then_inc(consts, 1)
            nc.vector.memset(nothing[:, 0:1], 0.0).then_inc(x1_done, 1)
            nc.vector.memset(nothing[:, 1:2], 0.0).then_inc(st_x1, 16)
            nc.vector.memset(nothing[:, 2:3], 0.0).then_inc(st_n4, 16)
            nc.vector.memset(nothing[:, 3:4], 0.0).then_inc(st_mix, 16)
            nc.vector.memset(nothing[:, 4:5], 0.0).then_inc(st_out, 16)
            nc.vector.memset(eps[:], EPS).then_inc(consts, 1)
            for n, tile in enumerate(tiles):
                ps = SR[n % 4]
                dve.wait_ge(su_act, n + 1)
                if tile[0] == "T":
                    _, a, k, g = tile
                    op = nc.vector.tensor_copy(wT[a][k][:, 4 * g + 2:4 * g + 4, :].rearrange("p a b -> p (a b)"), ps[:, 2 * P:])
                elif tile[0] in "MV":
                    kind, a, g = tile
                    dst = (Mw if kind == "M" else Vw)[a]
                    hi, lo = (dst[:, k, 8 * (g // 2) + g % 2:8 * (g // 2) + 8:2, :] for k in range(2))
                    op = tensor(lo, ps[:].rearrange("p (a b) -> p a b", a=4), f32(hi), ALU.subtract)
                elif tile[0] == "R":
                    op = tensor(WR[:, 1, :], ps[:, 0:3 * E], f32(WR[:, 0, :]), ALU.subtract)
                elif tile[0] == "C":
                    op = nc.vector.tensor_copy(condT[:, B // 2:], ps[:, B // 2:B])
                else:
                    op = nc.vector.tensor_scalar(emb[:, tile[1], 0:D], ps[:, 0:D], 1.0, None, ALU.add)
                op.then_inc(su_dve, 1)
            dve.wait_ge(su_act, NSU + 1)
            tensor(W1[:, 1, :], raw1[:], f32(W1[:, 0, :]), ALU.subtract).then_inc(su_dve, 1)
            dve.wait_ge(su_act, NSU + 2)
            tensor(W2[:, 1], raw2[:], f32(W2[:, 0]), ALU.subtract).then_inc(su_dve, 1)

            def heads(ap):
                return ap.rearrange("p (h k) -> p h k", h=HG)

            def peak(c, u, p):
                n = c * 16 + u * 4 + p
                dve.wait_ge(s_done, n + 1)
                nc.vector.tensor_reduce(mx[:, p % 2, :], heads(psS[p % 2][:]), AX_X, ALU.max).then_inc(max_done, 1)
                dve.wait_ge(max_done, n + 1)
                if not (isinstance(n, int) and n < 2):
                    dve.wait_ge(T_done, n - 1)
                if p < 2 and u == 2 and not (isinstance(c, int) and c == 0):
                    dve.wait_ge(glu_hi, FT * c)
                    dve.wait_ge(glu_lo, FT * c)
                tensor(heads(pr[:, p % 2, :]), heads(psS[p % 2][:]), mx[:, p % 2, :].unsqueeze(2).broadcast_to([P, HG, 64]), ALU.subtract).then_inc(sub_done, 1)

            def total(c, u, p):
                n = c * 16 + u * 4 + p
                dve.wait_ge(exp_done, n + 1)
                if not (isinstance(n, int) and n < 2):
                    dve.wait_ge(prob_done, n - 1)
                nc.vector.tensor_reduce(sm[:, p % 2, :], heads(pr[:, p % 2, :]), AX_X, ALU.add).then_inc(sum_done, 1)
                dve.wait_ge(sum_done, n + 1)
                nc.vector.reciprocal(sm[:, p % 2, :], sm[:, p % 2, :]).then_inc(rec_done, 1)

            def turn_lo(c, u, p):
                dve.wait_ge(pt_hi, c * 16 + u * 4 + p + 1)
                tensor(pt[:, 1, :], psT[:], f32(pt[:, 0, :]), ALU.subtract).then_inc(pt_lo, 1)

            def weigh_lo(c, u, p):
                for s in range(2):
                    dve.wait_ge(tt_hi, 2 * (c * 16 + u * 4 + p) + s + 1)
                    hi, lo = (tt[:, k, s, :, p * P:(p + 1) * P] for k in range(2))
                    tensor(lo, pst[s][:].rearrange("p (h q) -> p h q", h=4), f32(hi), ALU.subtract).then_inc(tt_lo, 1)

            def keys_lo(c, u, hs):
                for h in hs:
                    dve.wait_ge(kp_hi, c * 4 * HG + u * HG + h + 1)
                    tensor(kp[:, 1, h, :], psK[h % 2][:], f32(kp[:, 0, h, :]), ALU.subtract).then_inc(kp_lo, 1)

            def ln_stats(k, c, src):
                z = 12 * c
                for t in range(NT):
                    nc.vector.bn_stats(st[:, t, :], src[:, t, :]).then_inc(stat[k], 1)
                dve.wait_ge(stat[k], z + 4)
                me, M2e, mo, M2o = st[:, :, 1], st[:, :, 2], st[:, :, 4], st[:, :, 5]
                tensor(lv[:, 0, :], me, mo, ALU.add).then_inc(stat[k], 1)
                tensor(lv[:, 1, :], me, mo, ALU.subtract).then_inc(stat[k], 1)
                tensor(lv[:, 2, :], M2e, M2o, ALU.add).then_inc(stat[k], 1)
                dve.wait_ge(stat[k], z + 7)
                nc.vector.tensor_scalar(lv[:, 4, :], lv[:, 0, :], 0.5, None, ALU.mult).then_inc(stat[k], 1)
                nc.vector.scalar_tensor_tensor(lv[:, 3, :], lv[:, 1, :], D / 4.0, lv[:, 1, :], ALU.mult, ALU.mult).then_inc(stat[k], 1)
                dve.wait_ge(stat[k], z + 9)
                tensor(lv[:, 0, :], lv[:, 2, :], lv[:, 3, :], ALU.add).then_inc(stat[k], 1)
                dve.wait_ge(stat[k], z + 10)
                nc.vector.tensor_scalar(lv[:, 5, :], lv[:, 0, :], 1.0 / D, None, ALU.mult).then_inc(stat[k], 1)
                nc.vector.tensor_scalar(lv[:, 6, :], lv[:, 0, :], 1.0 / D, EPS, ALU.mult, ALU.add).then_inc(stat[k], 1)

            def ln_norm(k, src, dst):
                for t in range(NT):
                    op = nc.vector.tensor_scalar(dst[:, t, :], src[:, t, :], lv[:, 4, t:t + 1], lv[:, 7, t:t + 1], ALU.subtract, ALU.mult)
                op.then_inc(nrm[k], 1)

            def ln1_stats(c):
                dve.wait_ge(ld_x, 16 * (c + 1))
                ln_stats(0, c, x_in)

            def ln1(c, free):
                dve.wait_ge(rstd[0], 5 * c + 5)
                ln_norm(0, x_in, x_in)
                dve.wait_ge(nrm[0], c + 1)
                dve.wait_ge(ld_mA, 32 * (c + 1))
                for w in free:
                    dve.wait_ge(*w)
                for t in range(NT):
                    op = nc.vector.scalar_tensor_tensor(htm[:, t, :], x_in[:, t, :], lv[:, 11, t:t + 1], modA[:, t, 0:D], ALU.mult, ALU.mult)
                op.then_inc(mods[0], 1)
                dve.wait_ge(mods[0], 2 * c + 1)
                tensor(htm[:], htm[:], modA[:, :, D:2 * D], ALU.add).then_inc(mods[0], 1)

            def ln_lo(k, c):
                dve.wait_ge(hx_hi[k], c + 1)
                src = psT[:]
                if k < 2:
                    src = src.rearrange("p (t s q) -> p t s q", t=NT, s=2)
                    tensor(pair(hq[k][:, 1]), src, f32(pair(hq[k][:, 0])), ALU.subtract).then_inc(hx_lo[k], 1)
                else:
                    tensor(h3[:, 1, :], src, f32(h3[:, 0, :]), ALU.subtract).then_inc(hx_lo[k], 1)

            tiles3 = lambda ap: ap.rearrange("p (t d) -> p t d", t=NT)

            def after_attn1(c):
                dve.wait_ge(back1, c + 1)
                tensor(y1[:], tiles3(psT[:]), x_in[:], ALU.add).then_inc(y1_done, 1)
                dve.wait_ge(y1_done, c + 1)
                ln_stats(1, c, y1)

            def norm2(c):
                dve.wait_ge(rstd[1], c + 1)
                if isinstance(c, int) and c == 0:
                    dve.wait_ge(hx[0], 1)
                    dve.wait_ge(tm_hi, 1)
                    dve.wait_ge(tm_lo, 1)
                else:
                    dve.wait_ge(hx[2], c)
                ln_norm(1, y1, htm)

            def after_attn2(c):
                dve.wait_ge(back2, c + 1)
                dve.wait_ge(st_x1, 16 * (c + 1))
                tensor(y2[:], tiles3(psT[:]), y1[:], ALU.add).then_inc(y2_done, 1)
                dve.wait_ge(y2_done, c + 1)
                ln_stats(2, c, y2)

            def norm3(c, free):
                dve.wait_ge(rstd[2], c + 1)
                for w in free:
                    dve.wait_ge(*w)
                ln_norm(2, y2, htm)

            def after_glu(c):
                dve.wait_ge(backf, c + 1)
                tensor(y2[:], tiles3(psT[:]), y2[:], ALU.add).then_inc(y3_done, 1)
                dve.wait_ge(y3_done, c + 1)
                dve.wait_ge(ld_xa, 16 * (c + 1))
                tensor(y2[:], y2[:], x_ag[:], ALU.add).then_inc(x1_done, 1)
                dve.wait_ge(x1_done, c + 2)
                ln_stats(3, c, y2)

            def norm4(c, free):
                dve.wait_ge(rstd[3], c + 1)
                dve.wait_ge(*free)
                ln_norm(3, y2, htm)

            def glu_mul(c, f):
                dve.wait_ge(gel, FT * c + f + 1)
                ba = psK[0] if f % 2 == 0 else psS[0]
                nc.vector.scalar_tensor_tensor(pr[:, f % 2, :], ba[:], b_1[:, f:f + 1], pr[:, f % 2, :], ALU.add, ALU.mult).then_inc(glu, 1)

            def unit(c, u, mid=None, hook_a=None, hook_b=None, nxt=True):
                peak(c, u, 0)
                peak(c, u, 1)
                if mid:
                    mid()
                total(c, u, 0)
                total(c, u, 1)
                turn_lo(c, u, 0)
                peak(c, u, 2)
                if hook_a:
                    hook_a()
                weigh_lo(c, u, 0)
                turn_lo(c, u, 1)
                total(c, u, 2)
                peak(c, u, 3)
                if hook_b:
                    hook_b()
                weigh_lo(c, u, 1)
                turn_lo(c, u, 2)
                total(c, u, 3)
                un, cn = (u + 1) % 4, c + (u + 1) // 4
                if nxt:
                    keys_lo(cn, un, range(0, HG // 2))
                weigh_lo(c, u, 2)
                turn_lo(c, u, 3)
                if nxt:
                    keys_lo(cn, un, range(HG // 2, HG))
                weigh_lo(c, u, 3)

            def context(c):
                dve.wait_ge(cx_hi, c + 1)
                tensor(cT[:, 1, :], psT[:], f32(cT[:, 0, :]), ALU.subtract).then_inc(cx_lo, 1)

            def body(c, first=False, last=False):
                if first:
                    unit(c, 0)
                else:
                    unit(c, 0, hook_a=lambda: after_attn2(c - 1),
                         hook_b=lambda: norm3(c - 1, ((hx[0], c + 1), (tm_hi, c + 1), (tm_lo, c + 1))))
                    ln_lo(2, c - 1)
                unit(c, 1, hook_a=lambda: context(c))
                if not first:
                    glu_mul(c - 1, 0)
                after_attn1(c)
                if not first:
                    glu_mul(c - 1, 1)
                norm2(c)
                if not first:
                    for f in range(2, FT):
                        glu_mul(c - 1, f)
                ln_lo(1, c)
                if first:
                    unit(c, 2)
                else:
                    unit(c, 2, hook_a=lambda: after_glu(c - 1), hook_b=lambda: norm4(c - 1, (hx[1], c + 1)))
                    ln_lo(3, c - 1)
                if not last:
                    ln1_stats(c + 1)
                unit(c, 3, mid=None if last else (lambda: ln1(c + 1, ((hx[1], 1),) if first else ((hx[3], c),))),
                     hook_a=None if last else (lambda: ln_lo(0, c + 1)), nxt=not last)

            dve.wait_ge(pads, 2)
            ln1_stats(0)
            ln1(0, ())
            ln_lo(0, 0)
            keys_lo(0, 0, range(HG))
            body(0, first=True)
            with dve.Fori(1, NC - 1) as c:
                body(c)
            body(NC - 1, last=True)
            after_attn2(NC - 1)
            norm3(NC - 1, ((hx[3], NC - 1),))
            ln_lo(2, NC - 1)
            for f in range(FT):
                glu_mul(NC - 1, f)
            after_glu(NC - 1)
            norm4(NC - 1, (hx[2], NC))
            ln_lo(3, NC - 1)
            dve.drain().then_inc(a_end, 1)

            dve.wait_ge(a_end, 4)
            dve.wait_ge(ld_mx, 16)
            mixt = mixa[:].rearrange("p c t k -> p (c t) k")
            q_, k_, v_ = (mixt[:, :, i * E:(i + 1) * E] for i in range(3))
            TTE, TTEE = [P, TT, E], [P, TT, E, E]

            count = [0]

            def step(op):
                op.then_inc(rt, 1)
                count[0] += 1
                dve.wait_ge(rt, count[0])

            def over(ap):
                return ap.unsqueeze(2).broadcast_to(TTE)

            def pick(logits, mask, eq, top, first_eq):
                step(nc.vector.tensor_reduce(top, logits, AX_X, ALU.max))
                step(tensor(eq, logits, over(top), ALU.is_equal))
                step(tensor(eq, eq, pri[:].unsqueeze(1).broadcast_to(TTE), ALU.mult))
                step(nc.vector.tensor_reduce(first_eq, eq, AX_X, ALU.max))
                step(tensor(mask, eq, over(first_eq), ALU.is_equal))

            step(tensor(qk[:], q_.unsqueeze(3).broadcast_to(TTEE), k_.unsqueeze(2).broadcast_to(TTEE), ALU.mult))
            step(nc.vector.tensor_reduce(rr[0][:], qk[:], AX_X, ALU.max))
            step(tensor(qk[:], qk[:], rr[0][:].unsqueeze(3).broadcast_to(TTEE), ALU.subtract))
            dve.wait_ge(rt_act, 1)
            step(nc.vector.tensor_reduce(rr[1][:], qk[:], AX_X, ALU.add))
            step(tensor(qk[:], qk[:], v_.unsqueeze(2).broadcast_to(TTEE), ALU.mult))
            step(nc.vector.tensor_reduce(rr[2][:], qk[:], AX_X, ALU.add))
            step(nc.vector.reciprocal(rr[1][:], rr[1][:]))
            step(tensor(rr[3][:], rr[2][:], rr[1][:], ALU.mult))
            for e in range(E):
                step(nc.vector.memset(pri[:, e:e + 1], float(E - e)))
            pick(rr[3][:], rr[1][:], rr[0][:], r1[0][:], r1[1][:])
            step(nc.vector.scalar_tensor_tensor(rr[2][:], rr[1][:], -3e38, rr[3][:], ALU.mult, ALU.add))
            pick(rr[2][:], rr[4][:], rr[0][:], r1[2][:], r1[1][:])
            step(tensor(r1[3][:], r1[2][:], r1[0][:], ALU.subtract))
            assert count[0] == RT_DIFF
            dve.wait_ge(rt_act, 2)
            step(nc.vector.tensor_scalar(r1[0][:], r1[3][:], 1.0, None, ALU.add))
            step(nc.vector.reciprocal(r1[0][:], r1[0][:]))
            step(tensor(r1[3][:], r1[3][:], r1[0][:], ALU.mult))
            step(tensor(rr[1][:], rr[1][:], over(r1[0][:]), ALU.mult))
            step(tensor(rr[4][:], rr[4][:], over(r1[3][:]), ALU.mult))
            step(tensor(rr[5][:], rr[1][:], rr[4][:], ALU.add))
            assert count[0] == RT_LAST
            for n, (k, g) in enumerate(EU):
                dve.wait_ge(eu_act, n + 1)
                w = min(4, MT - 4 * g)
                hi, lo = (WE[:, k, i, 4 * g:4 * g + w, :].rearrange("p a b -> p (a b)") for i in range(2))
                tensor(lo, SR[n % 4][:, 0:w * P], f32(hi), ALU.subtract).then_inc(eu_dve, 1)
            dve.wait_ge(gt_pe, 1)
            nc.vector.tensor_copy(gT[:].rearrange("p a b -> p (a b)"), psum[7][:]).then_inc(gt_cp, 1)

            def gate_mul(c, i, j, first=False):
                m = c * MT + j
                r = (i * MT + j) % 4
                dve.wait_ge(sil_done, m + 1)
                if not (first and j < 4):
                    dve.wait_ge(uh_done, m - 3)
                    dve.wait_ge(ul_done, m - 3)
                tensor(ug[:, r, :], psum[3 + (j + i) % 3][:], sil[:, j % 2, :], ALU.mult).then_inc(ug_done, 1)

            def ulo(c, i, j):
                r = (i * MT + j) % 4
                dve.wait_ge(uh_done, c * MT + j + 1)
                tensor(uu[:, r, 1, :], ug[:, r, :], f32(uu[:, r, 0, :]), ALU.subtract).then_inc(ul_done, 1)

            def out_b(c, i):
                dve.wait_ge(mb_done, c + 1)
                dve.wait_ge(ld_xb[i], 16 * (c // 2 + 1) if isinstance(c, int) else 8 * (c - i) + 16)
                dve.wait_ge(st_out, 16 * (c + 1))
                tensor(ob[:], tiles3(psum[7][:]), x1b[i][:], ALU.add).then_inc(ob_done, 1)

            def chunk(c, i, first=False):
                for j in range(MT):
                    gate_mul(c, i, j, first)
                    if j >= 2:
                        ulo(c, i, j - 2)
                    elif not first:
                        ulo(c - 1, 1 - i, MT + j - 2)
                    if j == LAG + 3 and not first:
                        out_b(c - 1, 1 - i)

            dve.wait_ge(gt_st, 16)
            chunk(0, 0, first=True)
            chunk(1, 1)
            with dve.Fori(1, NC // 2) as d:
                for i in range(2):
                    chunk(2 * d + i, i)
            for j in range(MT - 2, MT):
                ulo(NC - 1, 1, j)
            out_b(NC - 1, 1)

        @block.gpsimd
        def _(pool):
            nc.gpsimd.memset(ident[:], 0.0).then_inc(identity, 1)
            pool.wait_ge(identity, 1)
            nc.gpsimd.affine_select(out=ident[:], in_=ident[:], compare_op=ALU.not_equal, fill=1.0, base=0,
                                    pattern=[[-1, P]], channel_multiplier=1).then_inc(identity, 1)
            pool.wait_ge(consts, 3)
            pool.wait_ge(emb_w, 16)
            for k in range(2):
                nc.gpsimd.memset(f32(hq[k][:, :, :, 64:128]), 0.0).then_inc(pads, 1)

            tensor = nc.gpsimd.tensor_tensor

            def prob(c, u, p):
                n = c * 16 + u * 4 + p
                pool.wait_ge(rec_done, n + 1)
                v = pr[:, p % 2, :].rearrange("p (h k) -> p h k", h=HG)
                tensor(v, v, sm[:, p % 2, :].unsqueeze(2).broadcast_to([P, HG, 64]), ALU.mult).then_inc(prob_done, 1)

            def ln_rstd(k, c):
                pool.wait_ge(stat[k], 12 * c + 12)
                tensor(lv[:, 7, :], lv[:, 6, :], half[:], ALU.pow).then_inc(rstd[k], 1)

            def ln1_rstd(c):
                pool.wait_ge(stat[0], 12 * c + 12)
                tensor(lv[:, 7, :], lv[:, 6, :], half[:], ALU.pow).then_inc(rstd[0], 1)
                pool.wait_ge(rstd[0], 5 * c + 1)
                tensor(lv[:, 8, :], lv[:, 5, :], lv[:, 7, :], ALU.mult).then_inc(rstd[0], 1)
                pool.wait_ge(rstd[0], 5 * c + 2)
                tensor(lv[:, 9, :], lv[:, 8, :], lv[:, 7, :], ALU.mult).then_inc(rstd[0], 1)
                pool.wait_ge(rstd[0], 5 * c + 3)
                tensor(lv[:, 10, :], lv[:, 9, :], eps[:], ALU.add).then_inc(rstd[0], 1)
                pool.wait_ge(rstd[0], 5 * c + 4)
                tensor(lv[:, 11, :], lv[:, 10, :], half[:], ALU.pow).then_inc(rstd[0], 1)

            def modulate(k, c, half_):
                pool.wait_ge(nrm[k], c + 1)
                pool.wait_ge(ld_mB, 64 * c + 32 * k)
                tensor(htm[:], htm[:], modB[:, :, 0:D], ALU.mult).then_inc(mods[k], 1)
                pool.wait_ge(mods[k], 2 * c + 1)
                tensor(htm[:], htm[:], modB[:, :, D:2 * D], ALU.add).then_inc(mods[k], 1)

            def tm_lo_(c):
                pool.wait_ge(tm_hi, c + 1)
                tensor(h_tm[:, 1, 0], htm[:], f32(h_tm[:, 0, 0]), ALU.subtract).then_inc(tm_lo, 1)

            def cm_lo_(c):
                pool.wait_ge(cm_hi, c + 1)
                tensor(c_tm[:, 1, 0], c_in[:], f32(c_tm[:, 0, 0]), ALU.subtract).then_inc(cm_lo, 1)

            def glu_lo_(c, f):
                pool.wait_ge(glu_hi, FT * c + f + 1)
                tensor(tt[:, 1, 0, f, :], pr[:, f % 2, :], f32(tt[:, 0, 0, f, :]), ALU.subtract).then_inc(glu_lo, 1)

            def body(c, first=False, last=False):
                prob(c, 0, 0)
                prob(c, 0, 1)
                if not first:
                    ln_rstd(2, c - 1)
                prob(c, 0, 2)
                if not first:
                    modulate(2, c - 1, 1)
                prob(c, 0, 3)
                prob(c, 1, 0)
                prob(c, 1, 1)
                cm_lo_(c)
                prob(c, 1, 2)
                prob(c, 1, 3)
                ln_rstd(1, c)
                if not first:
                    glu_lo_(c - 1, 0)
                modulate(1, c, 0)
                if not first:
                    for f in range(1, FT):
                        glu_lo_(c - 1, f)
                prob(c, 2, 0)
                prob(c, 2, 1)
                if not first:
                    ln_rstd(3, c - 1)
                prob(c, 2, 2)
                prob(c, 2, 3)
                if not last:
                    ln1_rstd(c + 1)
                prob(c, 3, 0)
                prob(c, 3, 1)
                if not last:
                    tm_lo_(c + 1)
                prob(c, 3, 2)
                prob(c, 3, 3)

            ln1_rstd(0)
            tm_lo_(0)
            body(0, first=True)
            with pool.Fori(1, NC - 1) as c:
                body(c)
            body(NC - 1, last=True)
            ln_rstd(2, NC - 1)
            modulate(2, NC - 1, 1)
            for f in range(FT):
                glu_lo_(NC - 1, f)
            ln_rstd(3, NC - 1)
            pool.drain().then_inc(a_end, 1)

            def gate(c, i, j):
                r = (i * MT + j) % 4
                m = c * MT + j
                pool.wait_ge(ug_done, m + 1)
                tensor(ug[:, r, :], ug[:, r, :], gb[i][:, slot_of[j], :], ALU.mult).then_inc(uc_done, 1)

            pool.wait_ge(a_end, 4)
            for i in range(2):
                pool.wait_ge(ld_gb[i], 16 * NGL)
                for j in range(MT):
                    gate(i, i, j)
            with pool.Fori(1, NC // 2) as d:
                for i in range(2):
                    pool.wait_ge(ld_gb[i], 16 * NGL * d + 16 * NGL)
                    for j in range(MT):
                        gate(2 * d + i, i, j)


_INS = ["x", "cond_1024", "ctx_1024", "L0_xcond_attn1_wq", "L0_xcond_attn1_wk", "L0_xcond_attn1_wv",
        "L0_xcond_attn1_wo", "L0_xcond_attn1_bo", "L0_xcond_attn2_wq", "L0_xcond_attn2_wk", "L0_xcond_attn2_wv",
        "L0_xcond_attn2_wo", "L0_xcond_attn2_bo", "L0_xcond_ff_w1", "L0_xcond_ff_b1", "L0_xcond_ff_w2",
        "L0_xcond_ff_b2", "L0_xcond_norm1_w", "L0_xcond_norm1_b", "L0_xcond_norm2_w", "L0_xcond_norm2_b",
        "L0_xcond_norm3_w", "L0_xcond_norm3_b", "L0_ffn_wqkv", "L0_ffn_w1", "L0_ffn_w2"]


def kernel(**inputs):
    import numpy as _np
    import concourse.bacc as _bacc
    from concourse import mybir as _mybir
    from concourse.bass_utils import run_bass_kernel_spmd as _run

    nc = _bacc.Bacc("TRN2", target_bir_lowering=False, num_devices=1)
    arrays, t_in = {}, {}
    for name in _INS:
        a = _np.ascontiguousarray(inputs[name])
        arrays[f"in_{name}_dram"] = a
        t_in[name] = nc.dram_tensor(f"in_{name}_dram", a.shape, _mybir.dt.from_np(a.dtype), kind="ExternalInput").ap()
    out = nc.dram_tensor("out_dram", inputs["x"].shape, _mybir.dt.float32, kind="ExternalOutput").ap()
    pixart_block_moe(nc, t_in, out)
    r = _run(nc, [arrays], core_ids=[0])
    return r.results[0]["out_dram"]
```

```python
from contextlib import ExitStack

import concourse.bass as bass
from concourse import mybir

F32 = mybir.dt.float32
F32R = mybir.dt.float32r
ALU = mybir.AluOpType
ACT = mybir.ActivationFunctionType
AX_X = mybir.AxisListType.X

P = 128
EPS = 1e-5


def pixart_block_moe(nc, t_in, out):
    x_d, cond_d, ctx_d = t_in["x"], t_in["cond_1024"], t_in["ctx_1024"]
    B, S, D = x_d.shape
    assert D == P and ctx_d.shape[1] == S == 64
    INNER = t_in["L0_xcond_attn1_wq"].shape[1]
    DH = 64
    H = INNER // DH
    HG = 8
    DFF = t_in["L0_xcond_ff_w2"].shape[0]
    FT = DFF // P
    E, F2, _ = t_in["L0_ffn_w1"].shape
    F = F2 // 2
    MT = E * F // P
    assert E * F % P == 0 and P % E == 0
    CT = 512
    NT = CT // P
    NC = B * S // CT
    SCALE = float(DH) ** -0.5
    UNITS = 2 * H // HG
    assert UNITS == 4

    EP = P // E
    assert F == EP * MT

    x_v = x_d.rearrange("(c t s) q d -> c (s q) t d", t=NT, s=2)
    ctx_v = ctx_d.rearrange("(c t s) q d -> c (s q) t d", t=NT, s=2)
    ctx_vs = ctx_d.rearrange("(c t s) q d -> c s q t d", t=NT, s=2)
    out_v = out.rearrange("(c t s) q d -> c (s q) t d", t=NT, s=2)
    emb_s = nc.dram_tensor("emb_s", [B, 6 * D], F32).ap()
    emb_v = emb_s.rearrange("(c t s) (n k) -> c n s t k", t=NT, s=2, n=3)
    x1_s = nc.dram_tensor("x1_s", [NC, P, NT, D], F32).ap()
    xn_s = nc.dram_tensor("xn_s", [NC, P, NT, D], F32).ap()
    y1_s = nc.dram_tensor("y1_s", [NC, P, NT, D], F32).ap()
    u_s = nc.dram_tensor("u_s", [NC, P, NT, D], F32).ap()
    n4_s = nc.dram_tensor("n4_s", [NC, 2, P, CT], F32).ap()
    mix_s = nc.dram_tensor("mix_s", [NC, P, NT * 3 * E], F32).ap()
    gate_s = nc.dram_tensor("gate_s", [NC * NT * E, P], F32).ap()
    gate_v = gate_s.rearrange("(c t e) q -> c e t q", t=NT, e=E)

    ctx = ExitStack()
    with ctx:
        def sem(name):
            return ctx.enter_context(nc.semaphore(name))

        def sb(name, shape, dt=F32, where=ctx):
            return where.enter_context(nc.sbuf_tensor(name, shape, dt))

        ident = sb("ident", [P, P])
        half = sb("half", [P, NT])
        eps = sb("eps", [P, NT])
        nothing = sb("nothing", [P, 1])

        with ExitStack() as phase_a:
            def sa(name, shape, dt=F32):
                return sb(name, shape, dt, phase_a)
            Mw = [sa(f"M{a}", [P, 2, H, D], F32R) for a in range(2)]
            Vw = [sa(f"V{a}", [P, 2, H, D], F32R) for a in range(2)]
            W1 = sa("W1", [P, 2, 2 * DFF], F32R)
            W2 = sa("W2", [P, 2, FT, D], F32R)
            WR = sa("WR", [P, 2, 3 * E], F32R)
            b_o = sa("b_o", [P, 2])
            b_1 = sa("b_1", [P, 2 * FT])
            b_2 = sa("b_2", [P, 1])
            with ExitStack() as working:
                def sw(name, shape, dt=F32):
                    return sb(name, shape, dt, working)
                kp = sw("kp", [P, 2, HG, CT], F32R)
                tt = sw("tt", [P, 2, 2, HG // 2, CT], F32R)
                pr = sw("pr", [P, NT, CT])
                pt = sw("pt", [P, 2, 2, CT], F32R)
                hq = [sw(f"hq{k}", [P, 2, NT, 192], F32R) for k in range(2)]
                h3 = sw("h3", [P, 2, CT], F32R)
                cT = sw("cT", [P, 2, CT], F32R)
                h_tm = sw("h_tm", [P, 2, 2, NT, D], F32R)
                c_tm = h_tm
                x_in = sw("x_in", [P, NT, D])
                c_in = sw("c_in", [P, NT, D])
                h1 = sw("h1", [P, NT, D])
                mod = sw("mod", [P, NT, 2 * D])
                tmp = sw("tmp", [P, NT, D])
                res = sw("res", [P, NT, D])
                gl = sw("gl", [P, 2, CT], F32R)
                oT = sw("oT", [P, CT])
                htm = sw("htm", [P, NT, D])
                st = sw("st", [P, NT, 6])
                lv = [sw(f"lv{k}", [P, 8 if k else 12, NT]) for k in range(4)]
                mx = sw("mx", [P, 2, HG])
                sm = sw("sm", [P, NT, HG])
            with ExitStack() as staging:
                def sg(name, shape, dt=F32):
                    return sb(name, shape, dt, staging)
                raw = [[sg(f"raw{a}{k}", [P, INNER]) for k in range(3)] for a in range(2)]
                rawo = [sg(f"rawo{a}", [P, H // 2, D]) for a in range(2)]
                raw1 = sg("raw1", [P, 2 * DFF])
                raw2 = sg("raw2", [P, FT, D])
                rawr = sg("rawr", [3 * E, D])
                rawn = sg("rawn", [P, 3, 2 * D])
                brow = sg("brow", [1, 3, 2 * D])
                rawc = sg("rawc", [B, D])
                wT = [[sg(f"wT{a}{k}", [P, H // 2, P]) for k in range(3)] for a in range(2)]
                condT = sg("condT", [P, B])
                emb = sg("emb", [B, 3, 2 * D])
                ones = sg("ones", [1, P])
        LAG = 4
        UR = 11
        assert 2 * MT % UR == 0 and 2 * MT % 4 == 0 and UR > LAG + 1
        with ExitStack() as phase_b:
            def sbb(name, shape, dt=F32):
                return sb(name, shape, dt, phase_b)
            WE = sbb("WE", [P, 3, 2, MT, P], F32R)
            with ExitStack() as b_work:
                nT = [sb(f"nT{i}", [P, 2, CT], F32R, b_work) for i in range(2)]
                x1b = [sb(f"x1b{i}", [P, NT, D], F32, b_work) for i in range(2)]
                gb = [sb(f"gb{i}", [P, CT], F32, b_work) for i in range(2)]
                sil = sb("sil", [P, 2, CT], F32, b_work)
                ug = sb("ug", [P, 4, CT], F32, b_work)
                uu = sb("uu", [P, UR, 2, CT], F32R, b_work)
                oTb = sb("oTb", [P, CT], F32, b_work)
                ob = sb("ob", [P, NT, D], F32, b_work)
            with ExitStack() as b_stage:
                rawe = [sb(f"rawe{k}", [P, MT, P], F32, b_stage) for k in range(3)]
                TT = NC * NT
                mixa = sb("mixa", [P, NC, NT, 3 * E], F32, b_stage)
                qk = sb("qk", [P, TT, E, E], F32, b_stage)
                rr = [sb(f"rr{i}", [P, TT, E], F32, b_stage) for i in range(6)]
                r1 = [sb(f"r1{i}", [P, TT], F32, b_stage) for i in range(4)]
                pri = sb("pri", [P, E], F32, b_stage)
                gT = sb("gT", [P, 4, P], F32, b_stage)

        psum = [ctx.enter_context(nc.psum_tensor(f"ps{i}", [P, CT], F32)) for i in range(8)]
        psS, psM, psT, psO = psum[0:2], psum[2], psum[4], psum[7]
        pstw = [psum[5:7], psum[2:4]]
        psKey = [psum[5], psum[6], psum[3]]

        def queries(a, k):
            return hq[a][:, k].rearrange("p t (b q) -> p t b q", q=64)[:, :, 0:3:2, :]

        def by_sample(bank):
            return bank[:].rearrange("p (t s q) -> p t s q", t=NT, s=2)


        pads = sem("pads")
        consts, identity = sem("consts"), sem("identity")
        ld_w = [sem(f"ld_w{a}") for a in range(2)]
        ld_m = sem("ld_m")
        ld_b = sem("ld_b")
        su_pe, su_act, su_dve = sem("su_pe"), sem("su_act"), sem("su_dve")
        emb_w = sem("emb_w")
        ld_x, ld_c, ld_xa, ld_xn, ld_y1 = sem("ld_x"), sem("ld_c"), sem("ld_xa"), sem("ld_xn"), sem("ld_y1")
        ld_mod = [sem(f"ld_mod{n}") for n in range(3)]
        s_done, max_done, sub_done, exp_done = sem("s_done"), sem("max_done"), sem("sub_done"), sem("exp_done")
        sum_done, rec_done, prob_done = sem("sum_done"), sem("rec_done"), sem("prob_done")
        T_done, pt_hi, pt_lo = sem("T_done"), sem("pt_hi"), sem("pt_lo")
        t_done, tt_hi, tt_raw = sem("t_done"), sem("tt_hi"), sem("tt_raw")
        tt_lo = [sem(f"tt_lo{s}") for s in range(2)]
        k_done, kp_hi, kp_raw = sem("k_done"), sem("kp_hi"), sem("kp_raw")
        kp_lo = [sem(f"kp_lo{s}") for s in range(2)]
        o_done = sem("o_done")
        o_out = [sem(f"o_out{a}") for a in range(2)]
        back1, back2, backf = sem("back1"), sem("back2"), sem("backf")
        y1_done, y2_done, u_done, x1_done = sem("y1_done"), sem("y2_done"), sem("u_done"), sem("x1_done")
        stat = [sem(f"stat{k}") for k in range(4)]
        rstd = [sem(f"rstd{k}") for k in range(4)]
        nrm = [sem(f"nrm{k}") for k in range(4)]
        mods = [sem(f"mods{k}") for k in range(3)]
        hx = [sem(f"hx{k}") for k in range(4)]
        hx_hi = [sem(f"hx_hi{k}") for k in range(4)]
        hx_lo = [sem(f"hx_lo{k}") for k in range(4)]
        tm_hi, tm_lo, tm_sw = sem("tm_hi"), sem("tm_lo"), sem("tm_sw")
        cx, cx_hi, cx_lo = sem("cx"), sem("cx_hi"), sem("cx_lo")
        cm_hi, cm_lo, cm_sw = sem("cm_hi"), sem("cm_lo"), sem("cm_sw")
        ff_done, gel, glu, glu_hi, glu_lo = sem("ff_done"), sem("gel"), sem("glu"), sem("glu_hi"), sem("glu_lo")
        f2_done, f2_out = sem("f2_done"), sem("f2_out")
        rm_done, mix_cp = sem("rm_done"), sem("mix_cp")
        st_x1, st_n4, st_mix, st_xn, st_y1 = sem("st_x1"), sem("st_n4"), sem("st_mix"), sem("st_xn"), sem("st_y1")
        ld_u, st_u = sem("ld_u"), sem("st_u")

        a_end = sem("a_end")
        ld_e, ld_mx = [sem(f"ld_e{k}") for k in range(3)], sem("ld_mx")
        eu_pe, eu_act, eu_dve = sem("eu_pe"), sem("eu_act"), sem("eu_dve")
        rt, rt_act = sem("rt"), sem("rt_act")
        gt_pe, gt_cp, gt_st = sem("gt_pe"), sem("gt_cp"), sem("gt_st")
        ld_nb, ld_xb, ld_gb = [[sem(f"{n}{i}") for i in range(2)] for n in ("ld_nb", "ld_xb", "ld_gb")]
        ag_done, sil_done, ug_done, uc_done, uh_done, ul_done = (
            sem("ag_done"), sem("sil_done"), sem("ug_done"), sem("uc_done"), sem("uh_done"), sem("ul_done"))
        mo_done, mo_out, mb_done, ob_done = sem("mo_done"), sem("mo_out"), sem("mb_done"), sem("ob_done")
        e_done = sem("e_done")
        st_out = sem("st_out")

        block = ctx.enter_context(nc.Block())

        def mm3(ps, w, m, first=True, last=True, add=False):
            for n, (i, j) in enumerate([(1, 0), (0, 1), (0, 0)]):
                mm = nc.tensor.matmul(ps, w(i), m(j), start=(first and n == 0), stop=(last and n == 2))
            return mm

        def f32(ap):
            return ap.bitcast(F32)

        SR = [psum[i] for i in range(4)]
        tiles = []
        for a in range(2):
            for k in range(3):
                for g in range(H // 8):
                    tiles.append(("T", a, k, g))
            for g in range(H // 4):
                tiles.append(("M", a, g))
            for g in range(H // 4):
                tiles.append(("V", a, g))
        tiles += [("R",), ("C",), ("E", 0), ("E", 1), ("E", 2)]
        NSU = len(tiles)
        t_of = {t: n for n, t in enumerate(tiles)}
        EU = [(k, g) for k in range(3) for g in range((MT + 3) // 4)]
        NEU = len(EU)

        RT_DIFF = 8 + E + 5 + 1 + 5 + 1
        RT_LAST = RT_DIFF + 6

        def ok(c):
            return not isinstance(c, int) or 0 <= c < NC

        def first(c):
            return isinstance(c, int) and c == 0

        def c_last(c):
            return isinstance(c, int) and c == NC - 1

        def live(i, u):
            return ok(i) if u < 2 else ok(i - 1)

        def before(i, u):
            return (i, u - 1) if u else (i - 1, 3)

        def after(i, u):
            return (i, u + 1) if u < 3 else (i + 1, 0)

        def seq(i, u):
            if first(i):
                return u
            if isinstance(i, int) and i == NC:
                return 4 * NC - 4 + u
            return 4 * i - 2 + u

        def rounds(engine, body):
            for i in range(3):
                body(i)
            with engine.Fori(3, NC - 1) as i:
                body(i)
            for i in range(NC - 1, NC + 3):
                body(i)

        POOL_KEYS = ()
        KEYS_LAST = (HG - 1,)

        def k_count(i, u, h, pool_):
            kind = [k for k in range(HG) if (k in POOL_KEYS) == pool_]
            return len(kind) * seq(i, u) + sum(k <= h for k in kind)

        def k_free(i, u, h):
            return (kp_raw, k_count(i, u, h, True)) if h in POOL_KEYS else (kp_lo[0], k_count(i, u, h, False))

        def k_ready(i, u, h):
            pool_ = h in POOL_KEYS
            return kp_lo[int(pool_)], k_count(i, u, h, pool_)

        POOL_TILES = (0, 2)

        def t_count(i, u, p, pool_):
            each = [int(k in POOL_TILES) if pool_ else 2 - (k in POOL_TILES) for k in range(NT)]
            return sum(each) * seq(i, u) + sum(each[:p + 1])

        def t_free(i, u, p):
            return [(tt_lo[0], t_count(i, u, p, False))] + ([(tt_raw, t_count(i, u, p, True))] if p in POOL_TILES else [])

        STAGES = (((1, 1, "ln2", hx_lo[1]), (3, 1, "context", cx_lo), (5, 3, "backf", x1_done)),
                  ((1, 2, "back2", y2_done), (3, 3, "ln4", hx_lo[3]), (6, 3, "router", mix_cp)),
                  ((1, 2, "ln3", hx_lo[2]), (6, -1, "ln1", hx_lo[0])),
                  ((1, 0, "back1", y1_done),))

        def misc_free(i, u):
            return [(done, i - lag + 1) for _, lag, _, done in STAGES[u] if ok(i - lag)]

        mixed = oT[:, 0:NT * 3 * E]
        tmp2 = tmp[:].rearrange("p t d -> p (t d)")

        def tmp_free(i, u):
            if u == 0 and ok(i - 3):
                return [(glu_lo, FT * (i - 2))]
            if u == 1 and ok(i - 3):
                return [(st_x1, 16 * (i - 2)), (nrm[3], i - 2)]
            if u == 2 and ok(i - 2):
                return [(st_u, 16 * (i - 1))]
            if u == 3 and ok(i - 2):
                return [(glu_lo, FT * (i - 2) + 1)]
            return []

        def tmp_split(i, u):
            li, lu = before(i, u)
            return [(tt_lo[1], t_count(li, lu, 3, True))] if live(li, lu) else []

        def tt_tile(k, p, s):
            return tt[:, k, s, :, p * P:(p + 1) * P]

        def heads4(bank):
            return (bank if bank is tmp2 else bank[:]).rearrange("p (h q) -> p h q", h=4)

        @block.sync
        def _(sp):
            for a in range(2):
                for k, n in enumerate(("wq", "wk", "wv")):
                    sp.dma_start(raw[a][k][:], t_in[f"L0_xcond_attn{a + 1}_{n}"]).then_inc(ld_w[a], 16)
                sp.dma_start(rawo[a][:], t_in[f"L0_xcond_attn{a + 1}_wo"].rearrange("(t p) n -> p t n", p=P)).then_inc(ld_w[a], 16)
            sp.dma_start(rawr[:], t_in["L0_ffn_wqkv"]).then_inc(ld_m, 16)
            sp.dma_start(rawc[:], cond_d).then_inc(ld_m, 16)
            for n in range(3):
                sp.dma_start(rawn[:, n, :], t_in[f"L0_xcond_norm{n + 1}_w"]).then_inc(ld_m, 16)
                sp.dma_start(brow[:, n, :], t_in[f"L0_xcond_norm{n + 1}_b"].unsqueeze(0)).then_inc(ld_m, 16)
            sp.dma_start(raw1[:], t_in["L0_xcond_ff_w1"]).then_inc(ld_m, 16)
            sp.dma_start(raw2[:], t_in["L0_xcond_ff_w2"].rearrange("(t p) n -> p t n", p=P)).then_inc(ld_m, 16)
            for a in range(2):
                sp.dma_start(b_o[:, a:a + 1], t_in[f"L0_xcond_attn{a + 1}_bo"].unsqueeze(1)).then_inc(ld_b, 16)
            sp.dma_start(b_1[:], t_in["L0_xcond_ff_b1"].rearrange("(t p) -> p t", p=P), allow_slow_non_contiguous=True).then_inc(ld_b, 16)
            sp.dma_start(b_2[:], t_in["L0_xcond_ff_b2"].unsqueeze(1)).then_inc(ld_b, 16)
            sp.wait_ge(su_act, NSU + 2)
            sp.wait_ge(su_dve, NSU + 2)
            sp.dma_start(emb_s, emb[:].rearrange("p n k -> p (n k)")).then_inc(emb_w, 16)
            sp.wait_ge(emb_w, 16)

            def load_mod(c, n):
                for s in range(2):
                    sp.dma_start(mod[64 * s:64 * s + 64], emb_v[c, n, s].partition_broadcast(64)).then_inc(ld_mod[n], 16)

            def swap(src, swapped):
                for k in range(2):
                    for s in range(2):
                        sp.dma_start(f32(src[64 * s:64 * s + 64, k, 1]), f32(src[64 - 64 * s:128 - 64 * s, k, 0])).then_inc(swapped, 16)

            def new_x(c):
                if not first(c):
                    sp.wait_ge(st_xn, 16 * c)
                sp.dma_start(x_in[:], x_v[c]).then_inc(ld_x, 16)

            def ln_x(c):
                sp.wait_ge(nrm[0], c + 1)
                sp.dma_start(xn_s[c], x_in[:]).then_inc(st_xn, 16)
                sp.wait_ge(mods[0], 2 * c + 2)
                if not first(c):
                    load_mod(c - 1, 1)

            def round_(i):
                if ok(i - 1):
                    sp.wait_ge(mods[1], 2 * i)
                if ok(i - 2):
                    load_mod(i - 2, 2)
                if ok(i - 3) and isinstance(i, int):
                    sp.wait_ge(st_u, 16 * (i - 2))
                if ok(i - 3):
                    sp.wait_ge(st_y1, 16 * i if ok(i - 1) else 16 * NC)
                    sp.dma_start(res[:], u_s[i - 3]).then_inc(ld_u, 16)
                if ok(i + 1):
                    new_x(i + 1)
                if ok(i):
                    sp.wait_ge(tm_hi, i + 1)
                    sp.wait_ge(tm_lo, i + 1)
                    swap(h_tm, tm_sw)
                if ok(i - 3):
                    sp.wait_ge(x1_done, i - 2)
                    sp.dma_start(x1_s[i - 3], tmp[:]).then_inc(st_x1, 16)
                if ok(i - 2):
                    if isinstance(i, int):
                        sp.wait_ge(st_y1, 16 * min(i, NC))
                    sp.dma_start(res[:], y1_s[i - 2]).then_inc(ld_y1, 16)
                    sp.wait_ge(y2_done, i - 1)
                    sp.dma_start(res[:], x_v[i - 2]).then_inc(ld_xa, 16)
                elif ok(i - 1):
                    sp.wait_ge(st_y1, 16 * i)
                if ok(i - 3):
                    sp.wait_ge(hx_hi[3], i - 2)
                    sp.wait_ge(hx_lo[3], i - 2)
                    sp.dma_start(n4_s[i - 3].rearrange("k p n -> p k n"), f32(h3[:])).then_inc(st_n4, 16)
                if ok(i - 2):
                    sp.wait_ge(u_done, i - 1)
                    sp.dma_start(u_s[i - 2], tmp[:]).then_inc(st_u, 16)
                if ok(i):
                    sp.dma_start(res[:], xn_s[i]).then_inc(ld_xn, 16)
                if ok(i - 3):
                    sp.wait_ge(mix_cp, i - 2)
                    sp.dma_start(mix_s[i - 3], mixed).then_inc(st_mix, 16)
                if ok(i - 2):
                    sp.wait_ge(mods[2], 2 * i - 2)
                if ok(i + 1):
                    load_mod(i + 1, 0)
                    ln_x(i + 1)
                elif ok(i):
                    load_mod(i, 1)
                if ok(i - 1):
                    sp.wait_ge(cm_hi, i)
                    sp.wait_ge(cm_lo, i)
                    swap(c_tm, cm_sw)
                if ok(i):
                    sp.dma_start(c_in[:], ctx_v[i]).then_inc(ld_c, 16)
                if ok(i - 2) and not isinstance(i, int):
                    sp.wait_ge(st_u, 16 * i - 16)
                if ok(i):
                    sp.wait_ge(y1_done, i + 1)
                    sp.dma_start(y1_s[i], res[:]).then_inc(st_y1, 16)

            new_x(0)
            load_mod(0, 0)
            ln_x(0)
            rounds(sp, round_)
            sp.wait_ge(st_x1, 16 * NC)
            sp.wait_ge(st_n4, 16 * NC)
            sp.wait_ge(st_mix, 16 * NC)

            sp.wait_ge(a_end, 4)
            sp.dma_start(mixa[:].rearrange("p c t k -> p c (t k)"), mix_s.rearrange("c p k -> p c k")).then_inc(ld_mx, 16)
            for k in range(2):
                for e in range(E):
                    sp.dma_start(rawe[k][EP * e:EP * e + EP], t_in["L0_ffn_w1"][e, k * F:k * F + F, :].rearrange("(q j) n -> q j n", j=MT)).then_inc(ld_e[k], 16)
            sp.dma_start(rawe[2][:].rearrange("p a b -> p (a b)").rearrange("p (e f) -> p e f", e=E),
                         t_in["L0_ffn_w2"].rearrange("e o f -> o e f")).then_inc(ld_e[2], 16)
            sp.wait_ge(gt_cp, 1)
            sp.dma_start(gate_s.rearrange("(g p) q -> p g q", p=P), gT[:]).then_inc(gt_st, 16)
            sp.wait_ge(gt_st, 16)
            sp.wait_ge(eu_act, NEU)
            sp.wait_ge(eu_dve, NEU)

            def load_b(c, i):
                sp.dma_start(f32(nT[i][:]), n4_s[c].rearrange("k p n -> p k n")).then_inc(ld_nb[i], 16)
                for e in range(E):
                    sp.dma_start(gb[i][EP * e:EP * e + EP, :].rearrange("p (t q) -> p t q", t=NT),
                                 gate_v[c, e].partition_broadcast(EP)).then_inc(ld_gb[i], 16)
                sp.dma_start(x1b[i][:], x1_s[c]).then_inc(ld_xb[i], 16)

            load_b(0, 0)
            load_b(1, 1)
            with sp.Fori(0, NC // 2 - 1) as d:
                for i in range(2):
                    sp.wait_ge(ob_done, 2 * d + i + 1)
                    sp.dma_start(out_v[2 * d + i], ob[:]).then_inc(st_out, 16)
                    sp.wait_ge(ag_done, (2 * d + i + 1) * MT)
                    sp.wait_ge(uc_done, (2 * d + i + 1) * MT)
                    load_b(2 * d + i + 2, i)
            for i in range(2):
                sp.wait_ge(ob_done, NC - 1 + i)
                sp.dma_start(out_v[NC - 2 + i], ob[:]).then_inc(st_out, 16)
            sp.wait_ge(st_out, 16 * (NC + 1))

        @block.tensor
        def _(pe):
            pe.wait_ge(consts, 3)
            pe.wait_ge(identity, 2)
            for n, tile in enumerate(tiles):
                ps = SR[n % 4]
                if n >= 4:
                    pe.wait_ge(su_dve, n - 3)
                if tile[0] == "T":
                    _, a, k, g = tile
                    pe.wait_ge(ld_w[a], 64)
                    for i in range(4):
                        mm = nc.tensor.transpose(ps[:, i * P:(i + 1) * P], raw[a][k][:, (4 * g + i) * P:(4 * g + i + 1) * P], ident[:])
                elif tile[0] in "MV":
                    kind, a, g = tile
                    pe.wait_ge(su_dve, t_of[("T", a, 2, 1)] + 1)
                    for i in range(4):
                        h = 8 * (g // 2) + 2 * i + g % 2
                        lo = 64 * (h % 2)
                        w = wT[a][1 if kind == "M" else 2][lo:lo + 64, h // 2, :]
                        m = wT[a][0][lo:lo + 64, h // 2, :] if kind == "M" else rawo[a][lo:lo + 64, h // 2, :]
                        mm = nc.tensor.matmul(ps[:, i * P:(i + 1) * P], w, m, start=True, stop=True)
                elif tile[0] == "R":
                    pe.wait_ge(ld_m, 160)
                    mm = nc.tensor.transpose(ps[:, 0:3 * E], rawr[:], ident[0:3 * E, 0:3 * E])
                elif tile[0] == "C":
                    mm = nc.tensor.transpose(ps[:, 0:B], rawc[:], ident[:])
                else:
                    pe.wait_ge(su_dve, t_of[("C",)] + 1)
                    nc.tensor.matmul(ps[:, 0:2 * D], condT[:], rawn[:, tile[1], :], start=True, stop=False)
                    mm = nc.tensor.matmul(ps[:, 0:2 * D], ones[:], brow[:, tile[1], :], start=False, stop=True)
                mm.then_inc(su_pe, 1)

            def wait(w):
                pe.wait_ge(*w)

            def keys(i, u, h):
                a, g = divmod(u, 2)
                if a == 0:
                    pe.wait_ge(hx_lo[0], i + 1)
                else:
                    pe.wait_ge(cx_lo, i)
                if h >= 3:
                    wait(k_free(i, u, h - 3))
                src = (lambda k: queries(0, k)) if a == 0 else (lambda k: cT[:, k, :])
                bank = psKey[h % 3]
                mm3(by_sample(bank) if a == 0 else bank[:], lambda k: Mw[a][:, k, g * HG + h, :], src).then_inc(k_done, 1)

            def scores(i, u, p):
                n = 4 * seq(i, u) + p
                if p == 0:
                    for h in KEYS_LAST:
                        wait(k_ready(i, u, h))
                    if u == 2:
                        pe.wait_ge(hx_lo[1], i)
                if not (isinstance(n, int) and n < 2):
                    pe.wait_ge(sub_done, n - 1)
                for s in range(2):
                    for q, (k, j) in enumerate(((1, 0), (0, 1), (0, 0))):
                        mm = nc.tensor.matmul(psS[p % 2][:].rearrange("p (h k) -> p h k", h=HG), hq[u // 2][:, k, p, 64 * s:64 * s + P],
                                              kp[:, j, :, p * P + 64 * s:p * P + 64 * s + 64],
                                              start=(s == 0 and q == 0), stop=(s == 1 and q == 2))
                mm.then_inc(s_done, 1)

            def turn(i, u, p):
                n = 4 * seq(i, u) + p
                if not (isinstance(n, int) and n < 1):
                    pe.wait_ge(pt_lo, n)
                pe.wait_ge(prob_done, n + 1)
                for k in range(4):
                    mm = nc.tensor.transpose(psT[:, k * P:(k + 1) * P], pr[:, p, k * P:(k + 1) * P], ident[:])
                mm.then_inc(T_done, 1)

            def weigh(i, u, p):
                n = 4 * seq(i, u) + p
                tm, swapped = (h_tm, tm_sw) if u < 2 else (c_tm, cm_sw)
                if p == 0 and u % 2 == 0:
                    pe.wait_ge(swapped, 64 * ((i if u < 2 else i - 1) + 1))
                pe.wait_ge(pt_lo, n + 1)
                if p >= 2:
                    for w in t_free(i, u, p - 2):
                        wait(w)
                pst = pstw[p % 2]
                for s in range(2):
                    for q, (k, j) in enumerate(((1, 0), (0, 1), (0, 0))):
                        for par in range(2):
                            rows = slice(64 * par, 64 * par + 64)
                            mm = nc.tensor.matmul(pst[par][:].rearrange("p (h r k) -> p h r k", h=4, r=2)[:, :, s, :],
                                                  tm[rows, k, (par + s) % 2, p, :],
                                                  pt[rows, p % 2, j, :].rearrange("p (h r k) -> p h r k", h=4, r=2)[:, :, s, :],
                                                  start=(q == 0), stop=(q == 2))
                            if s == 1 and q == 2:
                                mm.then_inc(t_done, 1)

            def project(i, u, h):
                a, g = divmod(u, 2)
                if h == 0:
                    pe.wait_ge(tt_lo[0], t_count(i, u, 3, False))
                    pe.wait_ge(tt_lo[1], t_count(i, u, 3, True))
                if h == 0 and g == 0:
                    if a == 0 and ok(i - 2):
                        pe.wait_ge(o_out[1], i - 1)
                    if a == 1:
                        pe.wait_ge(o_out[0], i + 1 if ok(i) else NC)
                mm = mm3(psO[:], lambda k: Vw[a][:, k, g * HG + h, :], lambda k: tt[:, k, h % 2, h // 2, :],
                         first=(g == 0 and h == 0), last=(g == 1 and h == HG - 1))
                if h == HG - 1:
                    mm.then_inc(o_done, 1)

            def turn4(bank, done, src):
                for k in range(4):
                    mm = nc.tensor.transpose(bank[:, k * P:(k + 1) * P], src(k), ident[:])
                mm.then_inc(done, 1)

            def back(c, ready, done):
                pe.wait_ge(ready, c + 1)
                turn4(psM, done, lambda k: oT[:, k * P:(k + 1) * P])

            def ln_turn(c, k):
                pe.wait_ge(*((nrm[3], c + 1) if k == 3 else (mods[k], 2 * c + 2)))
                turn4(psM, hx[k], lambda t: (h1 if k == 0 else htm)[:, t, :])

            def glu_up(c, f):
                n = FT * c + f
                if not (isinstance(n, int) and n < 1):
                    pe.wait_ge(glu, n)
                for bank, col in ((psS[0], f * P), (psS[1], DFF + f * P)):
                    mm = mm3(bank[:], lambda k: W1[:, k, col:col + P], lambda k: h3[:, k, :])
                mm.then_inc(ff_done, 1)

            def glu_down(c, f, turned):
                pe.wait_ge(glu_lo, FT * c + f + 1)
                if f == 0:
                    pe.wait_ge(pt_lo, turned)
                mm3(psT[:], lambda k: W2[:, k, f, :], lambda k: gl[:, k, :], first=f == 0, last=f == FT - 1).then_inc(f2_done, 1)

            def router(c):
                for t in range(NT):
                    mm = mm3(psM[:, t * 3 * E:(t + 1) * 3 * E], lambda k: h3[:, k, t * P:(t + 1) * P], lambda k: WR[:, k, :])
                mm.then_inc(rm_done, 1)

            def slot(i, u):
                here, last, then = live(i, u), live(*before(i, u)), live(*after(i, u))
                li, lu = before(i, u)
                for p in range(NT):
                    if last:
                        if u == 0 and p == 0 and ok(i - 3):
                            pe.wait_ge(f2_out, i - 2)
                        turn(li, lu, p)
                    if p >= 1 and last:
                        if p == 2:
                            for w in misc_free(li, lu):
                                wait(w)
                        weigh(li, lu, p - 1)
                    if here:
                        if p == 0 and u == 3 and ok(i - 2):
                            pe.wait_ge(glu, FT * (i - 2) + 1)
                        if p == 0 and u == 0 and ok(i - 3):
                            pe.wait_ge(glu, FT * (i - 2))
                        scores(i, u, p)
                if last:
                    weigh(li, lu, 3)

                def misc(lag, stage, evacuated=None):
                    if ok(i - lag):
                        if last and evacuated is None:
                            for w in t_free(li, lu, 3):
                                wait(w)
                        for w in misc_free(i, u)[:evacuated] if evacuated else misc_free(li, lu):
                            wait(w)
                        stage(i - lag)

                def turn_context(c):
                    pe.wait_ge(ld_c, 16 * (c + 1))
                    turn4(psM, cx, lambda k: c_in[:, k, :])

                glu_here = u == 3 and ok(i - 2)
                if glu_here and here:
                    pe.wait_ge(sub_done, 4 * seq(i, u) + 4)
                stages = STAGES[u]
                if glu_here:
                    glu_down(i - 2, 0, 4 * seq(li, lu) + 4 if last else 16 * NC)
                    glu_up(i - 2, 1)
                for h in range(HG):
                    if then:
                        if h < 3 and last:
                            for w in t_free(li, lu, 3 if h == 2 else 2):
                                wait(w)
                        keys(*after(i, u), h)
                    for k, (at, lag, name, _) in enumerate(stages):
                        if at == h:
                            misc(lag, {"ln1": lambda c: ln_turn(c, 0), "ln2": lambda c: ln_turn(c, 1),
                                       "ln3": lambda c: ln_turn(c, 2), "ln4": lambda c: ln_turn(c, 3),
                                       "context": turn_context, "router": router,
                                       "back1": lambda c: back(c, o_out[0], back1),
                                       "back2": lambda c: back(c, o_out[1], back2),
                                       "backf": lambda c: back(c, f2_out, backf)}[name],
                                 None if not any(ok(i - l) for _, l, _, _ in stages[:k]) else sum(ok(i - l) for _, l, _, _ in stages[:k]))
                    if last and h >= 1:
                        project(li, lu, h - 1)
                    if u == 2 and h == 3 and ok(i - 2):
                        if here:
                            pe.wait_ge(sub_done, 4 * seq(i, u) + 4)
                        pe.wait_ge(hx_lo[2], i - 1)
                        glu_up(i - 2, 0)
                    if glu_here and h in (2, 4):
                        glu_up(i - 2, h // 2 + 1)
                    if glu_here and h in (3, 5, 7):
                        glu_down(i - 2, h // 2, None)
                if last:
                    project(li, lu, HG - 1)
            pe.wait_ge(pads, 2)
            pe.wait_ge(mods[0], 2)
            turn4(psM, hx[0], lambda t: h1[:, t, :])
            for h in range(HG):
                keys(0, 0, h)
            rounds(pe, lambda i: [slot(i, u) for u in range(4)])
            pe.drain().then_inc(a_end, 1)

            pe.wait_ge(mix_cp, NC)
            for n, (k, g) in enumerate(EU):
                if n >= 4:
                    pe.wait_ge(eu_dve, n - 3)
                else:
                    pe.wait_ge(a_end, 4)
                pe.wait_ge(ld_e[k], 16 * (E if k < 2 else 1))
                for i, j in enumerate(range(4 * g, min(4 * g + 4, MT))):
                    src = rawe[k][:, j, :] if k < 2 else rawe[2][:].rearrange("p a b -> p (a b)").rearrange("p (q j) -> p j q", j=MT)[:, j, :]
                    mm = nc.tensor.transpose(SR[n % 4][:, i * P:(i + 1) * P], src, ident[:])
                mm.then_inc(eu_pe, 1)
            pe.wait_ge(rt, RT_LAST)
            for i in range(4):
                mm = nc.tensor.transpose(psum[7][:, i * P:(i + 1) * P], rr[5][:].rearrange("p t e -> p (t e)")[:, i * P:(i + 1) * P], ident[:])
            mm.then_inc(gt_pe, 1)
            pe.wait_ge(eu_act, NEU)
            pe.wait_ge(eu_dve, NEU)
            pe.wait_ge(gt_cp, 1)

            def up(c, i, j, first):
                m = c * MT + j
                if not (first and j < 3):
                    pe.wait_ge(ug_done, m - 1 if i == 0 and j < 2 else m - 2)
                b = (j + i) % 3
                mm3(psum[b][:], lambda k: WE[:, 0, k, j, :], lambda k: nT[i][:, k, :])
                mm3(psum[3 + b][:], lambda k: WE[:, 1, k, j, :], lambda k: nT[i][:, k, :]).then_inc(ag_done, 1)

            def down(c, i, j):
                r = (i * MT + j) % UR
                pe.wait_ge(ul_done, c * MT + j + 1)
                mm = mm3(psum[6 + i][:], lambda k: WE[:, 2, k, j, :], lambda k: uu[:, r, k, :], first=j == 0, last=j == MT - 1)
                mm.then_inc(e_done, 1)

            def back_b(c, i):
                pe.wait_ge(mo_out, c + 1)
                for t in range(4):
                    mm = nc.tensor.transpose(psum[6 + i][:, t * P:(t + 1) * P], oTb[:, t * P:(t + 1) * P], ident[:])
                mm.then_inc(mb_done, 1)

            def chunk(c, i, first=False):
                for j in range(MT):
                    up(c, i, j, first)
                    if j >= LAG:
                        if j == LAG and not (isinstance(c, int) and c < 2):
                            pe.wait_ge(ob_done, c - 1)
                        down(c, i, j - LAG)
                    elif not first:
                        down(c - 1, 1 - i, MT + j - LAG)
                    if j == LAG + 2 and not first:
                        back_b(c - 1, 1 - i)

            pe.wait_ge(ld_nb[0], 16)
            chunk(0, 0, first=True)
            pe.wait_ge(ld_nb[1], 16)
            chunk(1, 1)
            with pe.Fori(1, NC // 2) as d:
                for i in range(2):
                    pe.wait_ge(ld_nb[i], 16 * d + 16)
                    chunk(2 * d + i, i)
            for j in range(MT - LAG, MT):
                down(NC - 1, 1, j)
            back_b(NC - 1, 1)

        @block.scalar
        def _(act):
            def copy(o, i):
                return nc.scalar.activation(o, i, ACT.Copy)

            for n, tile in enumerate(tiles):
                ps = SR[n % 4]
                act.wait_ge(su_pe, n + 1)
                if tile[0] == "T":
                    _, a, k, g = tile
                    op = copy(wT[a][k][:, 4 * g:4 * g + 2, :].rearrange("p a b -> p (a b)"), ps[:, 0:2 * P])
                elif tile[0] in "MV":
                    kind, a, g = tile
                    dst = (Mw if kind == "M" else Vw)[a]
                    op = copy(dst[:, 0, 8 * (g // 2) + g % 2:8 * (g // 2) + 8:2, :], ps[:].rearrange("p (a b) -> p a b", a=4))
                elif tile[0] == "R":
                    op = copy(WR[:, 0, :], ps[:, 0:3 * E])
                elif tile[0] == "C":
                    op = copy(condT[:, 0:B // 2], ps[:, 0:B // 2])
                else:
                    op = copy(emb[:, tile[1], D:2 * D], ps[:, D:2 * D])
                op.then_inc(su_act, 1)
            act.wait_ge(ld_m, 160)
            copy(W1[:, 0, :], raw1[:]).then_inc(su_act, 1)
            copy(W2[:, 0], raw2[:]).then_inc(su_act, 1)
            act.wait_ge(ld_b, 64)

            def exp(i, u, p):
                act.wait_ge(sub_done, 4 * seq(i, u) + p + 1)
                nc.scalar.activation(pr[:, p, :], pr[:, p, :], ACT.Exp, scale=SCALE).then_inc(exp_done, 1)

            def turn_hi(i, u, p):
                n = 4 * seq(i, u) + p
                act.wait_ge(T_done, n + 1)
                if not (isinstance(n, int) and n < 2):
                    act.wait_ge(t_done, 2 * n - 2)
                copy(pt[:, p % 2, 0, :], psT[:]).then_inc(pt_hi, 1)

            def weigh_hi(i, u, p):
                n = 4 * seq(i, u) + p
                if p == 0 and not (isinstance(n, int) and n < 1):
                    act.wait_ge(o_done, seq(i, u))
                pst = pstw[p % 2]
                act.wait_ge(t_done, 2 * n + 1)
                copy(tt_tile(0, p, 0), heads4(pst[0])).then_inc(tt_hi, 1)
                act.wait_ge(t_done, 2 * n + 2)
                op = copy(tt_tile(0, p, 1), heads4(pst[1]))
                if p in POOL_TILES:
                    for w in (tmp_free(*after(i, u)) if p == POOL_TILES[0] else [(tt_lo[1], t_count(i, u, p, True) - 1)]):
                        act.wait_ge(*w)
                    copy(heads4(tmp2), heads4(pst[1])).then_inc(tt_raw, 1)
                else:
                    op.then_inc(tt_hi, 1)

            def keys_hi(i, u, h):
                act.wait_ge(k_done, HG * seq(i, u) + h + 1)
                bank = psKey[h % 3][:]
                op = copy(kp[:, 0, h, :], bank)
                if h in POOL_KEYS:
                    copy(f32(kp[:, 1, h, :]), bank).then_inc(kp_raw, 1)
                else:
                    op.then_inc(kp_hi, 1)

            def out_attn(c, a):
                act.wait_ge(o_done, seq(c + 1 if a else c, 2 * a + 1) + 1)
                if a == 0:
                    if ok(c - 3):
                        act.wait_ge(st_mix, 16 * (c - 2))
                    if ok(c - 2):
                        act.wait_ge(back2, c - 1)
                else:
                    if ok(c - 1):
                        act.wait_ge(backf, c)
                    act.wait_ge(back1, c + 2 if ok(c + 1) else NC)
                nc.scalar.activation(oT[:], psO[:], ACT.Identity, bias=b_o[:, a:a + 1]).then_inc(o_out[a], 1)

            def ln_hi(c, k):
                act.wait_ge(hx[k], c + 1)
                if k == 2 and not first(c):
                    act.wait_ge(st_n4, 16 * c)
                    act.wait_ge(rm_done, c)
                dst, src = (queries(k, 0), by_sample(psM)) if k < 2 else (h3[:, 0, :], psM[:])
                copy(dst, src).then_inc(hx_hi[k], 1)

            def glu_act(c, f):
                n = FT * c + f
                if f < 2:
                    for w in tmp_split(c + 2, 2 + f) + (tmp_free(c + 2, 2) if f == 0 else []):
                        act.wait_ge(*w)
                act.wait_ge(ff_done, n + 1)
                if not (isinstance(n, int) and n < 1):
                    act.wait_ge(f2_done, n)
                nc.scalar.activation(tmp2, psS[1][:], ACT.Gelu, bias=b_1[:, FT + f:FT + f + 1]).then_inc(gel, 1)

            def glu_split(c, f):
                act.wait_ge(glu, FT * c + f + 1)
                copy(gl[:, 0, :], tmp2).then_inc(glu_hi, 1)

            def out_glu(c):
                act.wait_ge(f2_done, FT * c + FT)
                act.wait_ge(back1, c + 3 if ok(c + 2) else NC)
                if c_last(c):
                    act.wait_ge(back2, c + 1)
                if not ok(c + 2):
                    act.wait_ge(st_mix, 16 * c)
                nc.scalar.activation(oT[:], psT[:], ACT.Identity, bias=b_2[:, 0:1]).then_inc(f2_out, 1)

            def mix_out(c):
                act.wait_ge(rm_done, c + 1)
                copy(mixed, psM[:, 0:NT * 3 * E]).then_inc(mix_cp, 1)

            def tm_split(c):
                act.wait_ge(mods[0], 2 * c + 2)
                if not first(c):
                    act.wait_ge(t_done, 8 * seq(c, 0))
                copy(h_tm[:, 0, 0], h1[:]).then_inc(tm_hi, 1)

            def context(c):
                act.wait_ge(cx, c + 1)
                copy(cT[:, 0, :], psM[:]).then_inc(cx_hi, 1)

            def cm_split(c):
                act.wait_ge(t_done, 8 * seq(c + 1, 2))
                copy(c_tm[:, 0, 0], c_in[:]).then_inc(cm_hi, 1)

            def slot(i, u):
                here, last, then = live(i, u), live(*before(i, u)), live(*after(i, u))
                li, lu = before(i, u)
                for p in range(NT):
                    if last:
                        turn_hi(li, lu, p)
                    if p >= 1 and last:
                        weigh_hi(li, lu, p - 1)
                    if p >= 1 and here:
                        exp(i, u, p - 1)
                if here:
                    exp(i, u, 3)
                if last:
                    weigh_hi(li, lu, 3)
                hooks = {0: ((1, 0, tm_split), (2, 1, lambda c: ln_hi(c, 1)), (4, 1, context)),
                         1: ((4, 3, lambda c: ln_hi(c, 3)), (7, 3, mix_out)),
                         2: ((2, 2, lambda c: ln_hi(c, 2)), (5, 2, lambda c: glu_act(c, 0)), (6, 2, lambda c: glu_split(c, 0)),
                             (1, 1, cm_split), (8, -1, lambda c: ln_hi(c, 0))),
                         3: ()}[u]
                for h in range(HG + 1):
                    for at, lag, stage in hooks:
                        if at == h and ok(i - lag):
                            stage(i - lag)
                    if u == 3 and ok(i - 2):
                        if h in (1, 3, 5):
                            glu_act(i - 2, h // 2 + 1)
                        if h in (2, 4, 6):
                            glu_split(i - 2, h // 2)
                    if h < HG and then:
                        keys_hi(*after(i, u), h)
                if last and lu == 1:
                    out_attn(li, 0)
                if last and lu == 3:
                    out_attn(li - 1, 1)
                if u == 3 and ok(i - 2):
                    out_glu(i - 2)

            ln_hi(0, 0)
            for h in range(HG):
                keys_hi(0, 0, h)
            rounds(act, lambda i: [slot(i, u) for u in range(4)])
            act.drain().then_inc(a_end, 1)

            act.wait_ge(a_end, 4)
            act.wait_ge(rt, 3)
            nc.scalar.activation(qk[:], qk[:], ACT.Exp).then_inc(rt_act, 1)
            for n, (k, g) in enumerate(EU):
                if n == 4:
                    act.wait_ge(rt, RT_DIFF)
                    nc.scalar.activation(r1[3][:], r1[3][:], ACT.Exp).then_inc(rt_act, 1)
                act.wait_ge(eu_pe, n + 1)
                w = min(4, MT - 4 * g)
                copy(WE[:, k, 0, 4 * g:4 * g + w, :].rearrange("p a b -> p (a b)"), SR[n % 4][:, 0:w * P]).then_inc(eu_act, 1)

            def silu(c, i, j, first=False):
                m = c * MT + j
                act.wait_ge(ag_done, m + 1)
                if not (first and j < 2):
                    act.wait_ge(ug_done, m - 1)
                nc.scalar.activation(sil[:, j % 2, :], psum[(j + i) % 3][:], ACT.Silu).then_inc(sil_done, 1)

            def uhi(c, i, j):
                m = c * MT + j
                act.wait_ge(uc_done, m + 1)
                if not (isinstance(m, int) and m < UR):
                    act.wait_ge(e_done, m - UR + 1)
                copy(uu[:, (i * MT + j) % UR, 0, :], ug[:, (i * MT + j) % 4, :]).then_inc(uh_done, 1)

            def out_b(c, i):
                act.wait_ge(e_done, (c + 1) * MT)
                if not (isinstance(c, int) and c == 0):
                    act.wait_ge(mb_done, c)
                copy(oTb[:], psum[6 + i][:]).then_inc(mo_out, 1)

            def chunk(c, i, first=False):
                for j in range(MT):
                    silu(c, i, j, first)
                    if j >= 2:
                        uhi(c, i, j - 2)
                    elif not first:
                        uhi(c - 1, 1 - i, MT + j - 2)
                    if j == LAG and not first:
                        out_b(c - 1, 1 - i)

            chunk(0, 0, first=True)
            chunk(1, 1)
            with act.Fori(1, NC // 2) as d:
                for i in range(2):
                    chunk(2 * d + i, i)
            for j in range(MT - 2, MT):
                uhi(NC - 1, 1, j)
            out_b(NC - 1, 1)

        @block.vector
        def _(dve):
            tensor = nc.vector.tensor_tensor
            nc.vector.memset(half[:], -0.5).then_inc(consts, 1)
            nc.vector.memset(ones[:], 1.0).then_inc(consts, 1)
            nc.vector.memset(nothing[:], 0.0).then_inc(st_out, 16)
            nc.vector.memset(eps[:], EPS).then_inc(consts, 1)
            for n, tile in enumerate(tiles):
                ps = SR[n % 4]
                dve.wait_ge(su_act, n + 1)
                if tile[0] == "T":
                    _, a, k, g = tile
                    op = nc.vector.tensor_copy(wT[a][k][:, 4 * g + 2:4 * g + 4, :].rearrange("p a b -> p (a b)"), ps[:, 2 * P:])
                elif tile[0] in "MV":
                    kind, a, g = tile
                    dst = (Mw if kind == "M" else Vw)[a]
                    hi, lo = (dst[:, k, 8 * (g // 2) + g % 2:8 * (g // 2) + 8:2, :] for k in range(2))
                    op = tensor(lo, ps[:].rearrange("p (a b) -> p a b", a=4), f32(hi), ALU.subtract)
                elif tile[0] == "R":
                    op = tensor(WR[:, 1, :], ps[:, 0:3 * E], f32(WR[:, 0, :]), ALU.subtract)
                elif tile[0] == "C":
                    op = nc.vector.tensor_copy(condT[:, B // 2:], ps[:, B // 2:B])
                else:
                    op = nc.vector.tensor_scalar(emb[:, tile[1], 0:D], ps[:, 0:D], 1.0, None, ALU.add)
                op.then_inc(su_dve, 1)
            dve.wait_ge(su_act, NSU + 1)
            tensor(W1[:, 1, :], raw1[:], f32(W1[:, 0, :]), ALU.subtract).then_inc(su_dve, 1)
            dve.wait_ge(su_act, NSU + 2)
            tensor(W2[:, 1], raw2[:], f32(W2[:, 0]), ALU.subtract).then_inc(su_dve, 1)

            def heads(ap):
                return ap.rearrange("p (h k) -> p h k", h=HG)

            def peak(i, u, p):
                n = 4 * seq(i, u) + p
                dve.wait_ge(s_done, n + 1)
                nc.vector.tensor_reduce(mx[:, p % 2, :], heads(psS[p % 2][:]), AX_X, ALU.max).then_inc(max_done, 1)
                dve.wait_ge(max_done, n + 1)
                tensor(heads(pr[:, p, :]), heads(psS[p % 2][:]), mx[:, p % 2, :].unsqueeze(2).broadcast_to([P, HG, 64]), ALU.subtract).then_inc(sub_done, 1)

            def total(i, u, p):
                n = 4 * seq(i, u) + p
                dve.wait_ge(exp_done, n + 1)
                nc.vector.tensor_reduce(sm[:, p, :], heads(pr[:, p, :]), AX_X, ALU.add).then_inc(sum_done, 1)
                dve.wait_ge(sum_done, n + 1)
                nc.vector.reciprocal(sm[:, p, :], sm[:, p, :]).then_inc(rec_done, 1)

            def turn_lo(i, u, p):
                dve.wait_ge(pt_hi, 4 * seq(i, u) + p + 1)
                tensor(pt[:, p % 2, 1, :], psT[:], f32(pt[:, p % 2, 0, :]), ALU.subtract).then_inc(pt_lo, 1)

            def weigh_lo(i, u, p):
                for par in range(1 if p in POOL_TILES else 2):
                    dve.wait_ge(tt_hi, t_count(i, u, p, False) - (par == 0 and p not in POOL_TILES))
                    tensor(tt_tile(1, p, par), heads4(pstw[p % 2][par]), f32(tt_tile(0, p, par)), ALU.subtract).then_inc(tt_lo[0], 1)

            def keys_lo(i, u, h):
                if h not in POOL_KEYS:
                    dve.wait_ge(kp_hi, k_count(i, u, h, False))
                    tensor(kp[:, 1, h, :], psKey[h % 3][:], f32(kp[:, 0, h, :]), ALU.subtract).then_inc(kp_lo[0], 1)

            def ln_stats(k, c, src):
                z, v, s = 12 * c, lv[k], st
                for t in range(NT):
                    nc.vector.bn_stats(s[:, t, :], src[:, t, :]).then_inc(stat[k], 1)
                dve.wait_ge(stat[k], z + 4)
                me, M2e, mo, M2o = s[:, :, 1], s[:, :, 2], s[:, :, 4], s[:, :, 5]
                tensor(v[:, 0, :], me, mo, ALU.add).then_inc(stat[k], 1)
                tensor(v[:, 1, :], me, mo, ALU.subtract).then_inc(stat[k], 1)
                tensor(v[:, 2, :], M2e, M2o, ALU.add).then_inc(stat[k], 1)
                dve.wait_ge(stat[k], z + 7)
                nc.vector.tensor_scalar(v[:, 4, :], v[:, 0, :], 0.5, None, ALU.mult).then_inc(stat[k], 1)
                nc.vector.scalar_tensor_tensor(v[:, 3, :], v[:, 1, :], D / 4.0, v[:, 1, :], ALU.mult, ALU.mult).then_inc(stat[k], 1)
                dve.wait_ge(stat[k], z + 9)
                tensor(v[:, 0, :], v[:, 2, :], v[:, 3, :], ALU.add).then_inc(stat[k], 1)
                dve.wait_ge(stat[k], z + 10)
                nc.vector.tensor_scalar(v[:, 5, :], v[:, 0, :], 1.0 / D, None, ALU.mult).then_inc(stat[k], 1)
                nc.vector.tensor_scalar(v[:, 6, :], v[:, 0, :], 1.0 / D, EPS, ALU.mult, ALU.add).then_inc(stat[k], 1)

            def ln_norm(k, src, dst):
                v = lv[k]
                for t in range(NT):
                    op = nc.vector.tensor_scalar(dst[:, t, :], src[:, t, :], v[:, 4, t:t + 1], v[:, 7, t:t + 1], ALU.subtract, ALU.mult)
                op.then_inc(nrm[k], 1)

            def ln1_stats(c):
                dve.wait_ge(ld_x, 16 * (c + 1))
                ln_stats(0, c, x_in)

            def ln1(c):
                dve.wait_ge(rstd[0], 5 * c + 5)
                ln_norm(0, x_in, x_in)
                dve.wait_ge(nrm[0], c + 1)
                dve.wait_ge(ld_mod[0], 32 * c + 32)
                if not first(c):
                    dve.wait_ge(hx[0], c)
                    dve.wait_ge(tm_hi, c)
                    dve.wait_ge(tm_lo, c)
                for t in range(NT):
                    op = nc.vector.scalar_tensor_tensor(h1[:, t, :], x_in[:, t, :], lv[0][:, 11, t:t + 1], mod[:, t, 0:D], ALU.mult, ALU.mult)
                op.then_inc(mods[0], 1)
                dve.wait_ge(mods[0], 2 * c + 1)
                tensor(h1[:], h1[:], mod[:, :, D:2 * D], ALU.add).then_inc(mods[0], 1)

            def ln_lo(c, k):
                dve.wait_ge(hx_hi[k], c + 1)
                if k < 2:
                    tensor(queries(k, 1), by_sample(psM), f32(queries(k, 0)), ALU.subtract).then_inc(hx_lo[k], 1)
                else:
                    tensor(h3[:, 1, :], psM[:], f32(h3[:, 0, :]), ALU.subtract).then_inc(hx_lo[k], 1)

            tiles3 = lambda ap: ap.rearrange("p (t d) -> p t d", t=NT)

            def after_attn1(c):
                dve.wait_ge(back1, c + 1)
                dve.wait_ge(ld_xn, 16 * c + 16)
                tensor(res[:], tiles3(psM[:]), res[:], ALU.add).then_inc(y1_done, 1)

            def norm2(c):
                dve.wait_ge(rstd[1], c + 1)
                if ok(c - 2):
                    dve.wait_ge(hx[2], c - 1)
                elif c == 1:
                    dve.wait_ge(hx[1], 1)
                ln_norm(1, res, htm)
                dve.wait_ge(nrm[1], c + 1)
                dve.wait_ge(ld_mod[1], 32 * c + 32)
                tensor(htm[:], htm[:], mod[:, :, 0:D], ALU.mult).then_inc(mods[1], 1)
                dve.wait_ge(mods[1], 2 * c + 1)
                tensor(htm[:], htm[:], mod[:, :, D:2 * D], ALU.add).then_inc(mods[1], 1)

            def after_attn2(c):
                dve.wait_ge(back2, c + 1)
                dve.wait_ge(ld_y1, 16 * c + 16)
                for w in tmp_free(c + 2, 1) + tmp_split(c + 2, 1):
                    dve.wait_ge(*w)
                tensor(tmp[:], tiles3(psM[:]), res[:], ALU.add).then_inc(y2_done, 1)

            def norm3(c):
                dve.wait_ge(rstd[2], c + 1)
                if ok(c - 1):
                    dve.wait_ge(hx[3], c)
                elif ok(c + 1):
                    dve.wait_ge(hx[1], c + 2)
                ln_norm(2, tmp, htm)

            def add_x(c):
                dve.wait_ge(nrm[2], c + 1)
                dve.wait_ge(ld_xa, 16 * c + 16)
                tensor(tmp[:], tmp[:], res[:], ALU.add).then_inc(u_done, 1)

            def after_glu(c):
                dve.wait_ge(backf, c + 1)
                dve.wait_ge(ld_u, 16 * (c + 1))
                for w in tmp_free(c + 3, 0) + tmp_split(c + 3, 0):
                    dve.wait_ge(*w)
                tensor(tmp[:], tiles3(psM[:]), res[:], ALU.add).then_inc(x1_done, 1)
                dve.wait_ge(x1_done, c + 1)
                ln_stats(3, c, tmp)

            def norm4(c):
                dve.wait_ge(rstd[3], c + 1)
                if ok(c + 2):
                    dve.wait_ge(hx[1], c + 3)
                elif ok(c + 1):
                    dve.wait_ge(hx[2], c + 1)
                else:
                    dve.wait_ge(hx[2], c + 1)
                ln_norm(3, tmp, htm)

            def glu_mul(c, f):
                dve.wait_ge(gel, FT * c + f + 1)
                nc.vector.scalar_tensor_tensor(tmp2, psS[0][:], b_1[:, f:f + 1], tmp2, ALU.add, ALU.mult).then_inc(glu, 1)

            def context(c):
                dve.wait_ge(cx_hi, c + 1)
                tensor(cT[:, 1, :], psM[:], f32(cT[:, 0, :]), ALU.subtract).then_inc(cx_lo, 1)

            def slot(i, u):
                here, last, then = live(i, u), live(*before(i, u)), live(*after(i, u))
                li, lu = before(i, u)
                for p in range(NT):
                    if last:
                        turn_lo(li, lu, p)
                    if here:
                        peak(i, u, p)
                    if p >= 1 and last:
                        weigh_lo(li, lu, p - 1)
                if last:
                    weigh_lo(li, lu, 3)

                def stats2(c):
                    dve.wait_ge(y1_done, c + 1)
                    ln_stats(1, c, res)

                def stats3(c):
                    dve.wait_ge(y2_done, c + 1)
                    ln_stats(2, c, tmp)

                hooks = {0: ((2, 1, lambda c: ln_lo(c, 1)), (4, 1, context), (6, 3, after_glu), (8, 3, norm4)),
                         1: ((2, 2, after_attn2), (3, 2, stats3), (4, 3, lambda c: ln_lo(c, 3)), (6, 2, norm3), (7, 2, add_x), (8, -1, ln1_stats)),
                         2: ((2, 2, lambda c: ln_lo(c, 2)), (3, -1, ln1), (6, 2, lambda c: glu_mul(c, 0)), (8, -1, lambda c: ln_lo(c, 0))),
                         3: ((2, 0, after_attn1), (3, 0, stats2), (7, 0, norm2))}[u]
                for h in range(HG + 1):
                    if u == 3 and ok(i - 2) and h in (2, 4, 6):
                        glu_mul(i - 2, h // 2)
                    for at, lag, stage in hooks:
                        if at == h and ok(i - lag):
                            stage(i - lag)
                    if h < NT and here:
                        total(i, u, h)
                    if h < HG and then:
                        keys_lo(*after(i, u), h)

            ln1_stats(0)
            ln1(0)
            ln_lo(0, 0)
            for h in range(HG):
                keys_lo(0, 0, h)
            rounds(dve, lambda i: [slot(i, u) for u in range(4)])
            dve.drain().then_inc(a_end, 1)

            dve.wait_ge(a_end, 4)
            dve.wait_ge(ld_mx, 16)
            mixt = mixa[:].rearrange("p c t k -> p (c t) k")
            q_, k_, v_ = (mixt[:, :, i * E:(i + 1) * E] for i in range(3))
            TTE, TTEE = [P, TT, E], [P, TT, E, E]

            count = [0]

            def step(op):
                op.then_inc(rt, 1)
                count[0] += 1
                dve.wait_ge(rt, count[0])

            def over(ap):
                return ap.unsqueeze(2).broadcast_to(TTE)

            def pick(logits, mask, eq, top, first_eq):
                step(nc.vector.tensor_reduce(top, logits, AX_X, ALU.max))
                step(tensor(eq, logits, over(top), ALU.is_equal))
                step(tensor(eq, eq, pri[:].unsqueeze(1).broadcast_to(TTE), ALU.mult))
                step(nc.vector.tensor_reduce(first_eq, eq, AX_X, ALU.max))
                step(tensor(mask, eq, over(first_eq), ALU.is_equal))

            step(tensor(qk[:], q_.unsqueeze(3).broadcast_to(TTEE), k_.unsqueeze(2).broadcast_to(TTEE), ALU.mult))
            step(nc.vector.tensor_reduce(rr[0][:], qk[:], AX_X, ALU.max))
            step(tensor(qk[:], qk[:], rr[0][:].unsqueeze(3).broadcast_to(TTEE), ALU.subtract))
            dve.wait_ge(rt_act, 1)
            step(nc.vector.tensor_reduce(rr[1][:], qk[:], AX_X, ALU.add))
            step(tensor(qk[:], qk[:], v_.unsqueeze(2).broadcast_to(TTEE), ALU.mult))
            step(nc.vector.tensor_reduce(rr[2][:], qk[:], AX_X, ALU.add))
            step(nc.vector.reciprocal(rr[1][:], rr[1][:]))
            step(tensor(rr[3][:], rr[2][:], rr[1][:], ALU.mult))
            for e in range(E):
                step(nc.vector.memset(pri[:, e:e + 1], float(E - e)))
            pick(rr[3][:], rr[1][:], rr[0][:], r1[0][:], r1[1][:])
            step(nc.vector.scalar_tensor_tensor(rr[2][:], rr[1][:], -3e38, rr[3][:], ALU.mult, ALU.add))
            pick(rr[2][:], rr[4][:], rr[0][:], r1[2][:], r1[1][:])
            step(tensor(r1[3][:], r1[2][:], r1[0][:], ALU.subtract))
            assert count[0] == RT_DIFF
            dve.wait_ge(rt_act, 2)
            step(nc.vector.tensor_scalar(r1[0][:], r1[3][:], 1.0, None, ALU.add))
            step(nc.vector.reciprocal(r1[0][:], r1[0][:]))
            step(tensor(r1[3][:], r1[3][:], r1[0][:], ALU.mult))
            step(tensor(rr[1][:], rr[1][:], over(r1[0][:]), ALU.mult))
            step(tensor(rr[4][:], rr[4][:], over(r1[3][:]), ALU.mult))
            step(tensor(rr[5][:], rr[1][:], rr[4][:], ALU.add))
            assert count[0] == RT_LAST
            for n, (k, g) in enumerate(EU):
                dve.wait_ge(eu_act, n + 1)
                w = min(4, MT - 4 * g)
                hi, lo = (WE[:, k, i, 4 * g:4 * g + w, :].rearrange("p a b -> p (a b)") for i in range(2))
                tensor(lo, SR[n % 4][:, 0:w * P], f32(hi), ALU.subtract).then_inc(eu_dve, 1)
            dve.wait_ge(gt_pe, 1)
            nc.vector.tensor_copy(gT[:].rearrange("p a b -> p (a b)"), psum[7][:]).then_inc(gt_cp, 1)

            def gate_mul(c, i, j, first=False):
                m = c * MT + j
                r = (i * MT + j) % 4
                dve.wait_ge(sil_done, m + 1)
                if not (first and j < 4):
                    dve.wait_ge(uh_done, m - 3)
                    dve.wait_ge(ul_done, m - 3)
                tensor(ug[:, r, :], psum[3 + (j + i) % 3][:], sil[:, j % 2, :], ALU.mult).then_inc(ug_done, 1)

            def ulo(c, i, j):
                r = (i * MT + j) % UR
                dve.wait_ge(uh_done, c * MT + j + 1)
                tensor(uu[:, r, 1, :], ug[:, (i * MT + j) % 4, :], f32(uu[:, r, 0, :]), ALU.subtract).then_inc(ul_done, 1)

            def out_b(c, i):
                dve.wait_ge(mb_done, c + 1)
                dve.wait_ge(ld_xb[i], 16 * (c // 2 + 1) if isinstance(c, int) else 8 * (c - i) + 16)
                dve.wait_ge(st_out, 16 * (c + 1))
                tensor(ob[:], tiles3(psum[6 + i][:]), x1b[i][:], ALU.add).then_inc(ob_done, 1)

            def chunk(c, i, first=False):
                for j in range(MT):
                    gate_mul(c, i, j, first)
                    if j >= 2:
                        ulo(c, i, j - 2)
                    elif not first:
                        ulo(c - 1, 1 - i, MT + j - 2)
                    if j == LAG + 3 and not first:
                        out_b(c - 1, 1 - i)

            dve.wait_ge(gt_st, 16)
            chunk(0, 0, first=True)
            chunk(1, 1)
            with dve.Fori(1, NC // 2) as d:
                for i in range(2):
                    chunk(2 * d + i, i)
            for j in range(MT - 2, MT):
                ulo(NC - 1, 1, j)
            out_b(NC - 1, 1)

        @block.gpsimd
        def _(pool):
            nc.gpsimd.memset(ident[:], 0.0).then_inc(identity, 1)
            pool.wait_ge(identity, 1)
            nc.gpsimd.affine_select(out=ident[:], in_=ident[:], compare_op=ALU.not_equal, fill=1.0, base=0,
                                    pattern=[[-1, P]], channel_multiplier=1).then_inc(identity, 1)
            pool.wait_ge(consts, 3)
            pool.wait_ge(emb_w, 16)
            for a in range(2):
                nc.gpsimd.memset(f32(hq[a][:, :, :, 64:128]), 0.0).then_inc(pads, 1)
            tensor = nc.gpsimd.tensor_tensor

            def prob(i, u, p):
                pool.wait_ge(rec_done, 4 * seq(i, u) + p + 1)
                v = pr[:, p, :].rearrange("p (h k) -> p h k", h=HG)
                tensor(v, v, sm[:, p, :].unsqueeze(2).broadcast_to([P, HG, 64]), ALU.mult).then_inc(prob_done, 1)

            def weigh_lo(i, u, p):
                if p in POOL_TILES:
                    pool.wait_ge(tt_raw, t_count(i, u, p, True))
                    tensor(tt_tile(1, p, 1), heads4(tmp2), f32(tt_tile(0, p, 1)), ALU.subtract).then_inc(tt_lo[1], 1)

            def keys_lo(i, u, h):
                if h in POOL_KEYS:
                    pool.wait_ge(kp_raw, k_count(i, u, h, True))
                    tensor(kp[:, 1, h, :], f32(kp[:, 1, h, :]), f32(kp[:, 0, h, :]), ALU.subtract).then_inc(kp_lo[1], 1)

            def ln_rstd(k, c):
                pool.wait_ge(stat[k], 12 * c + 12)
                tensor(lv[k][:, 7, :], lv[k][:, 6, :], half[:], ALU.pow).then_inc(rstd[k], 1)

            def ln1_rstd(c):
                v = lv[0]
                pool.wait_ge(stat[0], 12 * c + 12)
                tensor(v[:, 7, :], v[:, 6, :], half[:], ALU.pow).then_inc(rstd[0], 1)
                pool.wait_ge(rstd[0], 5 * c + 1)
                tensor(v[:, 8, :], v[:, 5, :], v[:, 7, :], ALU.mult).then_inc(rstd[0], 1)
                pool.wait_ge(rstd[0], 5 * c + 2)
                tensor(v[:, 9, :], v[:, 8, :], v[:, 7, :], ALU.mult).then_inc(rstd[0], 1)
                pool.wait_ge(rstd[0], 5 * c + 3)
                tensor(v[:, 10, :], v[:, 9, :], eps[:], ALU.add).then_inc(rstd[0], 1)
                pool.wait_ge(rstd[0], 5 * c + 4)
                tensor(v[:, 11, :], v[:, 10, :], half[:], ALU.pow).then_inc(rstd[0], 1)

            def modulate(c):
                pool.wait_ge(nrm[2], c + 1)
                pool.wait_ge(ld_mod[2], 32 * c + 32)
                tensor(htm[:], htm[:], mod[:, :, 0:D], ALU.mult).then_inc(mods[2], 1)
                pool.wait_ge(mods[2], 2 * c + 1)
                tensor(htm[:], htm[:], mod[:, :, D:2 * D], ALU.add).then_inc(mods[2], 1)

            def tm_lo_(c):
                pool.wait_ge(tm_hi, c + 1)
                tensor(h_tm[:, 1, 0], h1[:], f32(h_tm[:, 0, 0]), ALU.subtract).then_inc(tm_lo, 1)

            def cm_lo_(c):
                pool.wait_ge(cm_hi, c + 1)
                tensor(c_tm[:, 1, 0], c_in[:], f32(c_tm[:, 0, 0]), ALU.subtract).then_inc(cm_lo, 1)

            def glu_lo_(c, f):
                pool.wait_ge(glu_hi, FT * c + f + 1)
                tensor(gl[:, 1, :], tmp2, f32(gl[:, 0, :]), ALU.subtract).then_inc(glu_lo, 1)

            def slot(i, u):
                here, last, then = live(i, u), live(*before(i, u)), live(*after(i, u))
                li, lu = before(i, u)
                if last:
                    for p in range(NT):
                        weigh_lo(li, lu, p)
                hooks = {0: ((2, 0, tm_lo_), (8, 3, lambda c: ln_rstd(3, c))),
                         1: ((4, 2, lambda c: ln_rstd(2, c)), (7, 2, modulate), (8, -1, ln1_rstd)),
                         2: ((2, 1, cm_lo_), (7, 2, lambda c: glu_lo_(c, 0))),
                         3: ((5, 0, lambda c: ln_rstd(1, c)),)}[u]
                for h in range(HG + 1):
                    if h < NT and here:
                        prob(i, u, h)
                    if u == 3 and ok(i - 2) and h in (2, 4, 6):
                        glu_lo_(i - 2, h // 2)
                    if h < HG and then:
                        keys_lo(*after(i, u), h)
                    for at, lag, stage in hooks:
                        if at == h and ok(i - lag):
                            stage(i - lag)

            ln1_rstd(0)
            for h in range(HG):
                keys_lo(0, 0, h)
            rounds(pool, lambda i: [slot(i, u) for u in range(4)])
            pool.drain().then_inc(a_end, 1)

            def gate(c, i, j):
                r = (i * MT + j) % 4
                m = c * MT + j
                pool.wait_ge(ug_done, m + 1)
                tensor(ug[:, r, :], ug[:, r, :], gb[i][:], ALU.mult).then_inc(uc_done, 1)

            pool.wait_ge(a_end, 4)
            for i in range(2):
                pool.wait_ge(ld_gb[i], 16 * E)
                for j in range(MT):
                    gate(i, i, j)
            with pool.Fori(1, NC // 2) as d:
                for i in range(2):
                    pool.wait_ge(ld_gb[i], 16 * E * d + 16 * E)
                    for j in range(MT):
                        gate(2 * d + i, i, j)


_INS = ["x", "cond_1024", "ctx_1024", "L0_xcond_attn1_wq", "L0_xcond_attn1_wk", "L0_xcond_attn1_wv",
        "L0_xcond_attn1_wo", "L0_xcond_attn1_bo", "L0_xcond_attn2_wq", "L0_xcond_attn2_wk", "L0_xcond_attn2_wv",
        "L0_xcond_attn2_wo", "L0_xcond_attn2_bo", "L0_xcond_ff_w1", "L0_xcond_ff_b1", "L0_xcond_ff_w2",
        "L0_xcond_ff_b2", "L0_xcond_norm1_w", "L0_xcond_norm1_b", "L0_xcond_norm2_w", "L0_xcond_norm2_b",
        "L0_xcond_norm3_w", "L0_xcond_norm3_b", "L0_ffn_wqkv", "L0_ffn_w1", "L0_ffn_w2"]


def kernel(**inputs):
    import numpy as _np
    import concourse.bacc as _bacc
    from concourse import mybir as _mybir
    from concourse.bass_utils import run_bass_kernel_spmd as _run

    nc = _bacc.Bacc("TRN2", target_bir_lowering=False, num_devices=1)
    arrays, t_in = {}, {}
    for name in _INS:
        a = _np.ascontiguousarray(inputs[name])
        arrays[f"in_{name}_dram"] = a
        t_in[name] = nc.dram_tensor(f"in_{name}_dram", a.shape, _mybir.dt.from_np(a.dtype), kind="ExternalInput").ap()
    out = nc.dram_tensor("out_dram", inputs["x"].shape, _mybir.dt.float32, kind="ExternalOutput").ap()
    pixart_block_moe(nc, t_in, out)
    r = _run(nc, [arrays], core_ids=[0])
    return r.results[0]["out_dram"]
```

```python
from contextlib import ExitStack

import concourse.bass as bass
from concourse import mybir

F32 = mybir.dt.float32
F32R = mybir.dt.float32r
ALU = mybir.AluOpType
ACT = mybir.ActivationFunctionType
AX_X = mybir.AxisListType.X

P = 128
EPS = 1e-5


def pixart_block_moe(nc, t_in, out):
    x_d, cond_d, ctx_d = t_in["x"], t_in["cond_1024"], t_in["ctx_1024"]
    B, S, D = x_d.shape
    assert D == P and ctx_d.shape[1] == S == 64
    INNER = t_in["L0_xcond_attn1_wq"].shape[1]
    DH = 64
    H = INNER // DH
    HG = 8
    DFF = t_in["L0_xcond_ff_w2"].shape[0]
    FT = DFF // P
    E, F2, _ = t_in["L0_ffn_w1"].shape
    F = F2 // 2
    MT = E * F // P
    assert E * F % P == 0 and P % E == 0
    CT = 512
    NT = CT // P
    NC = B * S // CT
    SCALE = float(DH) ** -0.5
    UNITS = 2 * H // HG
    assert UNITS == 4

    EP = P // E
    assert F == EP * MT

    x_v = x_d.rearrange("(c t s) q d -> c (s q) t d", t=NT, s=2)
    ctx_v = ctx_d.rearrange("(c t s) q d -> c (s q) t d", t=NT, s=2)
    ctx_vs = ctx_d.rearrange("(c t s) q d -> c s q t d", t=NT, s=2)
    out_v = out.rearrange("(c t s) q d -> c (s q) t d", t=NT, s=2)
    emb_s = nc.dram_tensor("emb_s", [B, 6 * D], F32).ap()
    emb_v = emb_s.rearrange("(c t s) (n k) -> c n s t k", t=NT, s=2, n=3)
    x1_s = nc.dram_tensor("x1_s", [NC, P, NT, D], F32).ap()
    xn_s = nc.dram_tensor("xn_s", [NC, P, NT, D], F32).ap()
    y1_s = nc.dram_tensor("y1_s", [NC, P, NT, D], F32).ap()
    u_s = nc.dram_tensor("u_s", [NC, P, NT, D], F32).ap()
    n4_s = nc.dram_tensor("n4_s", [NC, 2, P, CT], F32).ap()
    mix_s = nc.dram_tensor("mix_s", [NC, P, NT * E], F32).ap()
    gate_s = nc.dram_tensor("gate_s", [NC * NT * E, P], F32).ap()
    gate_v = gate_s.rearrange("(c t e) q -> c e t q", t=NT, e=E)

    ctx = ExitStack()
    with ctx:
        def sem(name):
            return ctx.enter_context(nc.semaphore(name))

        def sb(name, shape, dt=F32, where=ctx):
            return where.enter_context(nc.sbuf_tensor(name, shape, dt))

        ident = sb("ident", [P, P])
        half = sb("half", [P, NT])
        eps = sb("eps", [P, NT])
        nothing = sb("nothing", [P, 1])

        with ExitStack() as phase_a:
            def sa(name, shape, dt=F32):
                return sb(name, shape, dt, phase_a)
            Mw = [sa(f"M{a}", [P, 2, H, D], F32R) for a in range(2)]
            Vw = [sa(f"V{a}", [P, 2, H, D], F32R) for a in range(2)]
            W1 = sa("W1", [P, 2, 2 * DFF], F32R)
            W2 = sa("W2", [P, 2, FT, D], F32R)
            WR = sa("WR", [P, 2, 3 * E], F32R)
            b_o = sa("b_o", [P, 2])
            b_1 = sa("b_1", [P, 2 * FT])
            b_2 = sa("b_2", [P, 1])
            with ExitStack() as working:
                def sw(name, shape, dt=F32):
                    return sb(name, shape, dt, working)
                kp = sw("kp", [P, 2, HG, CT], F32R)
                tt = sw("tt", [P, 2, 2, HG // 2, CT], F32R)
                pr = sw("pr", [P, NT, CT])
                pt = sw("pt", [P, 2, 2, CT], F32R)
                hq = [sw(f"hq{k}", [P, 2, NT, 192], F32R) for k in range(2)]
                h3 = sw("h3", [P, 2, CT], F32R)
                cT = sw("cT", [P, 2, CT], F32R)
                h_tm = sw("h_tm", [P, 2, 2, NT, D], F32R)
                c_tm = h_tm
                x_in = sw("x_in", [P, NT, D])
                c_in = sw("c_in", [P, NT, D])
                h1 = sw("h1", [P, NT, D])
                mod = sw("mod", [P, NT, 2 * D])
                tmp = sw("tmp", [P, NT, D])
                res = sw("res", [P, NT, D])
                gl = sw("gl", [P, 2, CT], F32R)
                oT = sw("oT", [P, CT])
                htm = sw("htm", [P, NT, D])
                st = sw("st", [P, NT, 6])
                lv = [sw(f"lv{k}", [P, 8 if k else 12, NT]) for k in range(4)]
                rt_o = sw("rt_o", [P, NT, E])
                mx = sw("mx", [P, 2, HG])
                sm = sw("sm", [P, NT, HG])
            with ExitStack() as staging:
                def sg(name, shape, dt=F32):
                    return sb(name, shape, dt, staging)
                raw = [[sg(f"raw{a}{k}", [P, INNER]) for k in range(3)] for a in range(2)]
                rawo = [sg(f"rawo{a}", [P, H // 2, D]) for a in range(2)]
                raw1 = sg("raw1", [P, 2 * DFF])
                raw2 = sg("raw2", [P, FT, D])
                rawr = sg("rawr", [3 * E, D])
                rawn = sg("rawn", [P, 3, 2 * D])
                brow = sg("brow", [1, 3, 2 * D])
                rawc = sg("rawc", [B, D])
                wT = [[sg(f"wT{a}{k}", [P, H // 2, P]) for k in range(3)] for a in range(2)]
                condT = sg("condT", [P, B])
                emb = sg("emb", [B, 3, 2 * D])
                ones = sg("ones", [1, P])
        LAG = 4
        UR = 11
        assert 2 * MT % UR == 0 and 2 * MT % 4 == 0 and UR > LAG + 1
        with ExitStack() as phase_b:
            def sbb(name, shape, dt=F32):
                return sb(name, shape, dt, phase_b)
            WE = sbb("WE", [P, 3, 2, MT, P], F32R)
            with ExitStack() as b_work:
                nT = [sb(f"nT{i}", [P, 2, CT], F32R, b_work) for i in range(2)]
                x1b = [sb(f"x1b{i}", [P, NT, D], F32, b_work) for i in range(2)]
                gb = [sb(f"gb{i}", [P, CT], F32, b_work) for i in range(2)]
                sil = sb("sil", [P, 2, CT], F32, b_work)
                ug = sb("ug", [P, 4, CT], F32, b_work)
                uu = sb("uu", [P, UR, 2, CT], F32R, b_work)
                oTb = sb("oTb", [P, CT], F32, b_work)
                ob = sb("ob", [P, NT, D], F32, b_work)
            with ExitStack() as b_stage:
                rawe = [sb(f"rawe{k}", [P, MT, P], F32, b_stage) for k in range(3)]
                TT = NC * NT
                rr = [sb(f"rr{i}", [P, TT, E], F32, b_stage) for i in range(6)]
                r1 = [sb(f"r1{i}", [P, TT], F32, b_stage) for i in range(4)]
                pri = sb("pri", [P, E], F32, b_stage)
                gT = sb("gT", [P, 4, P], F32, b_stage)

        psum = [ctx.enter_context(nc.psum_tensor(f"ps{i}", [P, CT], F32)) for i in range(8)]
        psS, psM, psT, psO = psum[0:2], psum[2], psum[4], psum[7]
        pstw = [psum[5:7], psum[2:4]]
        psH = psum[3]
        RINGS = ([*psum[5:7], psT, psH, *psS], [*psum[5:7], psT, psH, *psS], [*psum[5:7], psT, psH], [*psum[5:7], psH])

        def ring(u):
            return RINGS[(u - 1) % 4]

        def key_bank(u, h):
            return ring(u)[h % len(ring(u))]

        def queries(a, k):
            return hq[a][:, k].rearrange("p t (b q) -> p t b q", q=64)[:, :, 0:3:2, :]

        def by_sample(bank):
            return bank[:].rearrange("p (t s q) -> p t s q", t=NT, s=2)


        pads = sem("pads")
        consts, identity = sem("consts"), sem("identity")
        ld_w = [sem(f"ld_w{a}") for a in range(2)]
        ld_m = sem("ld_m")
        ld_b = sem("ld_b")
        su_pe, su_act, su_dve = sem("su_pe"), sem("su_act"), sem("su_dve")
        emb_w = sem("emb_w")
        ld_x, ld_c, ld_xa, ld_xn, ld_y1 = sem("ld_x"), sem("ld_c"), sem("ld_xa"), sem("ld_xn"), sem("ld_y1")
        ld_mod = [sem(f"ld_mod{n}") for n in range(3)]
        s_done, max_done, sub_done, exp_done = sem("s_done"), sem("max_done"), sem("sub_done"), sem("exp_done")
        sum_done, rec_done, prob_done = sem("sum_done"), sem("rec_done"), sem("prob_done")
        T_done, pt_hi, pt_lo = sem("T_done"), sem("pt_hi"), sem("pt_lo")
        t_done, tt_hi, tt_raw = sem("t_done"), sem("tt_hi"), sem("tt_raw")
        tt_lo = [sem(f"tt_lo{s}") for s in range(2)]
        k_done, kp_hi, kp_lo = sem("k_done"), sem("kp_hi"), sem("kp_lo")
        o_done = sem("o_done")
        o_out = [sem(f"o_out{a}") for a in range(2)]
        back1, back2, backf = sem("back1"), sem("back2"), sem("backf")
        y1_done, y2_done, u_done, x1_done = sem("y1_done"), sem("y2_done"), sem("u_done"), sem("x1_done")
        stat = [sem(f"stat{k}") for k in range(4)]
        rstd = [sem(f"rstd{k}") for k in range(4)]
        nrm = [sem(f"nrm{k}") for k in range(4)]
        mods = [sem(f"mods{k}") for k in range(3)]
        hx = [sem(f"hx{k}") for k in range(4)]
        hx_hi = [sem(f"hx_hi{k}") for k in range(4)]
        hx_lo = [sem(f"hx_lo{k}") for k in range(4)]
        tm_hi, tm_lo, tm_sw = sem("tm_hi"), sem("tm_lo"), sem("tm_sw")
        cx, cx_hi, cx_lo = sem("cx"), sem("cx_hi"), sem("cx_lo")
        cm_hi, cm_lo, cm_sw = sem("cm_hi"), sem("cm_lo"), sem("cm_sw")
        ff_done, gel, glu, glu_hi, glu_lo = sem("ff_done"), sem("gel"), sem("glu"), sem("glu_hi"), sem("glu_lo")
        f2_done, f2_out = sem("f2_done"), sem("f2_out")
        rm_done, mix_cp = sem("rm_done"), sem("mix_cp")
        rt_qk, rt_peak, rt_sub, rt_exp = sem("rt_qk"), sem("rt_peak"), sem("rt_sub"), sem("rt_exp")
        rt_tot, rt_mul, rt_dotted, rt_rec, rt_done = sem("rt_tot"), sem("rt_mul"), sem("rt_dotted"), sem("rt_rec"), sem("rt_done")
        st_x1, st_n4, st_mix, st_xn, st_y1 = sem("st_x1"), sem("st_n4"), sem("st_mix"), sem("st_xn"), sem("st_y1")
        ld_u, st_u = sem("ld_u"), sem("st_u")

        a_end = sem("a_end")
        ld_e, ld_mx = [sem(f"ld_e{k}") for k in range(3)], sem("ld_mx")
        eu_pe, eu_act, eu_dve = sem("eu_pe"), sem("eu_act"), sem("eu_dve")
        rt, rt_act = sem("rt"), sem("rt_act")
        gt_pe, gt_cp, gt_st = sem("gt_pe"), sem("gt_cp"), sem("gt_st")
        ld_nb, ld_xb, ld_gb = [[sem(f"{n}{i}") for i in range(2)] for n in ("ld_nb", "ld_xb", "ld_gb")]
        ag_done, sil_done, ug_done, uc_done, uh_done, ul_done = (
            sem("ag_done"), sem("sil_done"), sem("ug_done"), sem("uc_done"), sem("uh_done"), sem("ul_done"))
        mo_out, mb_done, ob_done = sem("mo_out"), sem("mb_done"), sem("ob_done")
        e_done = sem("e_done")
        st_out = sem("st_out")

        block = ctx.enter_context(nc.Block())

        def mm3(ps, w, m, first=True, last=True, add=False):
            for n, (i, j) in enumerate([(1, 0), (0, 1), (0, 0)]):
                mm = nc.tensor.matmul(ps, w(i), m(j), start=(first and n == 0), stop=(last and n == 2))
            return mm

        def f32(ap):
            return ap.bitcast(F32)

        SR = [psum[i] for i in range(4)]
        tiles = []
        for a in range(2):
            for k in range(3):
                for g in range(H // 8):
                    tiles.append(("T", a, k, g))
            for g in range(H // 4):
                tiles.append(("M", a, g))
            for g in range(H // 4):
                tiles.append(("V", a, g))
        tiles += [("R",), ("C",), ("E", 0), ("E", 1), ("E", 2)]
        NSU = len(tiles)
        t_of = {t: n for n, t in enumerate(tiles)}
        EU = [(k, g) for k in range(3) for g in range((MT + 3) // 4)]
        NEU = len(EU)

        RT_DIFF = E + 5 + 1 + 5 + 1
        RT_LAST = RT_DIFF + 6

        def ok(c):
            return not isinstance(c, int) or 0 <= c < NC

        def first(c):
            return isinstance(c, int) and c == 0

        def c_last(c):
            return isinstance(c, int) and c == NC - 1

        def live(i, u):
            return ok(i) if u < 2 else ok(i - 1)

        def before(i, u):
            return (i, u - 1) if u else (i - 1, 3)

        def after(i, u):
            return (i, u + 1) if u < 3 else (i + 1, 0)

        def seq(i, u):
            if first(i):
                return u
            if isinstance(i, int) and i == NC:
                return 4 * NC - 4 + u
            return 4 * i - 2 + u

        def rounds(engine, body):
            for i in range(3):
                body(i)
            with engine.Fori(3, NC - 1) as i:
                body(i)
            for i in range(NC - 1, NC + 3):
                body(i)

        def k_count(i, u, h):
            return HG * seq(i, u) + h + 1

        EARLY = 2
        POOL_TILES = (0, 1, 2, 3)

        def t_count(i, u, p, pool_):
            each = [int(k in POOL_TILES) if pool_ else 2 - (k in POOL_TILES) for k in range(NT)]
            return sum(each) * seq(i, u) + sum(each[:p + 1])

        def t_free(i, u, p):
            return [(tt_lo[0], t_count(i, u, p, False))] + ([(tt_raw, t_count(i, u, p, True))] if p in POOL_TILES else [])

        STAGES = (((2, 1, "ln2", hx_lo[1]), (4, 1, "context", cx_lo), (6, 3, "backf", x1_done)),
                  ((2, 2, "back2", y2_done), (4, 3, "ln4", hx_lo[3]), (7, 3, "router", mix_cp)),
                  ((2, 2, "ln3", hx_lo[2]), (6, -1, "ln1", hx_lo[0])),
                  ((None, 2, "glu", f2_out),))

        def misc_free(i, u):
            return [(done, i - lag + 1) for _, lag, _, done in STAGES[u] if ok(i - lag)]

        parts, room = [], 0
        for n in (3 * E, E * E, E, E, E):
            parts.append(oT[:, room:room + NT * n].rearrange("p (t n) -> p t n", t=NT))
            room += NT * n
        assert room <= CT
        mixed, qk4, rt_max, rt_sum, rt_dot = parts
        qk4 = qk4.rearrange("p t (a b) -> p t a b", a=E)
        tmp2 = tmp[:].rearrange("p t d -> p (t d)")

        def tmp_free(i, u):
            if u == 0 and ok(i - 3):
                return [(glu_lo, FT * (i - 2))]
            if u == 1 and ok(i - 3):
                return [(st_x1, 16 * (i - 2)), (nrm[3], i - 2)]
            if u == 2 and ok(i - 2):
                return [(st_u, 16 * (i - 1))]
            if u == 3 and ok(i - 2):
                return [(glu_lo, FT * (i - 2) + 1)]
            return []

        def tmp_split(i, u):
            li, lu = before(i, u)
            return [(tt_lo[1], t_count(li, lu, 3, True))] if live(li, lu) else []

        def tt_tile(k, p, s):
            return tt[:, k, s, :, p * P:(p + 1) * P]

        def heads4(bank):
            return (bank if bank is tmp2 else bank[:]).rearrange("p (h q) -> p h q", h=4)

        @block.sync
        def _(sp):
            for a in range(2):
                for k, n in enumerate(("wq", "wk", "wv")):
                    sp.dma_start(raw[a][k][:], t_in[f"L0_xcond_attn{a + 1}_{n}"]).then_inc(ld_w[a], 16)
                sp.dma_start(rawo[a][:], t_in[f"L0_xcond_attn{a + 1}_wo"].rearrange("(t p) n -> p t n", p=P)).then_inc(ld_w[a], 16)
            sp.dma_start(rawr[:], t_in["L0_ffn_wqkv"]).then_inc(ld_m, 16)
            sp.dma_start(rawc[:], cond_d).then_inc(ld_m, 16)
            for n in range(3):
                sp.dma_start(rawn[:, n, :], t_in[f"L0_xcond_norm{n + 1}_w"]).then_inc(ld_m, 16)
                sp.dma_start(brow[:, n, :], t_in[f"L0_xcond_norm{n + 1}_b"].unsqueeze(0)).then_inc(ld_m, 16)
            sp.dma_start(raw1[:], t_in["L0_xcond_ff_w1"]).then_inc(ld_m, 16)
            sp.dma_start(raw2[:], t_in["L0_xcond_ff_w2"].rearrange("(t p) n -> p t n", p=P)).then_inc(ld_m, 16)
            for a in range(2):
                sp.dma_start(b_o[:, a:a + 1], t_in[f"L0_xcond_attn{a + 1}_bo"].unsqueeze(1)).then_inc(ld_b, 16)
            sp.dma_start(b_1[:], t_in["L0_xcond_ff_b1"].rearrange("(t p) -> p t", p=P), allow_slow_non_contiguous=True).then_inc(ld_b, 16)
            sp.dma_start(b_2[:], t_in["L0_xcond_ff_b2"].unsqueeze(1)).then_inc(ld_b, 16)
            sp.wait_ge(su_act, NSU + 2)
            sp.wait_ge(su_dve, NSU + 2)
            sp.dma_start(emb_s, emb[:].rearrange("p n k -> p (n k)")).then_inc(emb_w, 16)
            sp.wait_ge(emb_w, 16)

            def load_mod(c, n):
                for s in range(2):
                    sp.dma_start(mod[64 * s:64 * s + 64], emb_v[c, n, s].partition_broadcast(64)).then_inc(ld_mod[n], 16)

            def swap(src, swapped):
                for k in range(2):
                    for s in range(2):
                        sp.dma_start(f32(src[64 * s:64 * s + 64, k, 1]), f32(src[64 - 64 * s:128 - 64 * s, k, 0])).then_inc(swapped, 16)

            def new_x(c):
                if not first(c):
                    sp.wait_ge(st_xn, 16 * c)
                sp.dma_start(x_in[:], x_v[c]).then_inc(ld_x, 16)

            def ln_x(c):
                sp.wait_ge(nrm[0], c + 1)
                sp.dma_start(xn_s[c], x_in[:]).then_inc(st_xn, 16)
                sp.wait_ge(mods[0], 2 * c + 2)
                if not first(c):
                    load_mod(c - 1, 1)

            def round_(i):
                if ok(i - 1):
                    sp.wait_ge(mods[1], 2 * i)
                if ok(i - 2):
                    load_mod(i - 2, 2)
                if ok(i - 3) and isinstance(i, int):
                    sp.wait_ge(st_u, 16 * (i - 2))
                if ok(i - 3):
                    sp.wait_ge(st_y1, 16 * i if ok(i - 1) else 16 * NC)
                    sp.dma_start(res[:], u_s[i - 3]).then_inc(ld_u, 16)
                if ok(i + 1):
                    new_x(i + 1)
                if ok(i):
                    sp.wait_ge(tm_hi, i + 1)
                    sp.wait_ge(tm_lo, i + 1)
                    swap(h_tm, tm_sw)
                if ok(i - 3):
                    sp.wait_ge(x1_done, i - 2)
                    sp.dma_start(x1_s[i - 3], tmp[:]).then_inc(st_x1, 16)
                if ok(i - 2):
                    if isinstance(i, int):
                        sp.wait_ge(st_y1, 16 * min(i, NC))
                    sp.dma_start(res[:], y1_s[i - 2]).then_inc(ld_y1, 16)
                    sp.wait_ge(y2_done, i - 1)
                    sp.dma_start(res[:], x_v[i - 2]).then_inc(ld_xa, 16)
                elif ok(i - 1):
                    sp.wait_ge(st_y1, 16 * i)
                if ok(i - 3):
                    sp.wait_ge(hx_hi[3], i - 2)
                    sp.wait_ge(hx_lo[3], i - 2)
                    sp.dma_start(n4_s[i - 3].rearrange("k p n -> p k n"), f32(h3[:])).then_inc(st_n4, 16)
                if ok(i - 2):
                    sp.wait_ge(u_done, i - 1)
                    sp.dma_start(u_s[i - 2], tmp[:]).then_inc(st_u, 16)
                if ok(i):
                    sp.dma_start(res[:], xn_s[i]).then_inc(ld_xn, 16)
                if ok(i - 2):
                    sp.wait_ge(mods[2], 2 * i - 2)
                if ok(i + 1):
                    load_mod(i + 1, 0)
                    ln_x(i + 1)
                elif ok(i):
                    load_mod(i, 1)
                if ok(i - 1):
                    sp.wait_ge(cm_hi, i)
                    sp.wait_ge(cm_lo, i)
                    swap(c_tm, cm_sw)
                if ok(i):
                    sp.dma_start(c_in[:], ctx_v[i]).then_inc(ld_c, 16)
                if ok(i - 3):
                    sp.wait_ge(rt_done, i - 2)
                    sp.dma_start(mix_s[i - 3], rt_o[:].rearrange("p t e -> p (t e)")).then_inc(st_mix, 16)
                if ok(i - 2) and not isinstance(i, int):
                    sp.wait_ge(st_u, 16 * i - 16)
                if ok(i):
                    sp.wait_ge(y1_done, i + 1)
                    sp.dma_start(y1_s[i], res[:]).then_inc(st_y1, 16)

            new_x(0)
            load_mod(0, 0)
            ln_x(0)
            rounds(sp, round_)
            sp.wait_ge(st_x1, 16 * NC)
            sp.wait_ge(st_n4, 16 * NC)
            sp.wait_ge(st_mix, 16 * NC)

            sp.wait_ge(a_end, 4)
            sp.dma_start(rr[3][:].rearrange("p (c t) e -> p c (t e)", c=NC), mix_s.rearrange("c p k -> p c k")).then_inc(ld_mx, 16)
            for k in range(2):
                for e in range(E):
                    sp.dma_start(rawe[k][EP * e:EP * e + EP], t_in["L0_ffn_w1"][e, k * F:k * F + F, :].rearrange("(q j) n -> q j n", j=MT)).then_inc(ld_e[k], 16)
            sp.dma_start(rawe[2][:].rearrange("p a b -> p (a b)").rearrange("p (e f) -> p e f", e=E),
                         t_in["L0_ffn_w2"].rearrange("e o f -> o e f")).then_inc(ld_e[2], 16)
            sp.wait_ge(gt_cp, 1)
            sp.dma_start(gate_s.rearrange("(g p) q -> p g q", p=P), gT[:]).then_inc(gt_st, 16)
            sp.wait_ge(gt_st, 16)
            sp.wait_ge(eu_act, NEU)
            sp.wait_ge(eu_dve, NEU)

            def load_b(c, i):
                sp.dma_start(f32(nT[i][:]), n4_s[c].rearrange("k p n -> p k n")).then_inc(ld_nb[i], 16)
                for e in range(E):
                    sp.dma_start(gb[i][EP * e:EP * e + EP, :].rearrange("p (t q) -> p t q", t=NT),
                                 gate_v[c, e].partition_broadcast(EP)).then_inc(ld_gb[i], 16)
                sp.dma_start(x1b[i][:], x1_s[c]).then_inc(ld_xb[i], 16)

            load_b(0, 0)
            load_b(1, 1)
            with sp.Fori(0, NC // 2 - 1) as d:
                for i in range(2):
                    sp.wait_ge(ob_done, 2 * d + i + 1)
                    sp.dma_start(out_v[2 * d + i], ob[:]).then_inc(st_out, 16)
                    sp.wait_ge(ag_done, (2 * d + i + 1) * MT)
                    sp.wait_ge(uc_done, (2 * d + i + 1) * MT)
                    load_b(2 * d + i + 2, i)
            for i in range(2):
                sp.wait_ge(ob_done, NC - 1 + i)
                sp.dma_start(out_v[NC - 2 + i], ob[:]).then_inc(st_out, 16)
            sp.wait_ge(st_out, 16 * (NC + 1))

        @block.tensor
        def _(pe):
            pe.wait_ge(consts, 3)
            pe.wait_ge(identity, 2)
            for n, tile in enumerate(tiles):
                ps = SR[n % 4]
                if n >= 4:
                    pe.wait_ge(su_dve, n - 3)
                if tile[0] == "T":
                    _, a, k, g = tile
                    pe.wait_ge(ld_w[a], 64)
                    for i in range(4):
                        mm = nc.tensor.transpose(ps[:, i * P:(i + 1) * P], raw[a][k][:, (4 * g + i) * P:(4 * g + i + 1) * P], ident[:])
                elif tile[0] in "MV":
                    kind, a, g = tile
                    pe.wait_ge(su_dve, t_of[("T", a, 2, 1)] + 1)
                    for i in range(4):
                        h = 8 * (g // 2) + 2 * i + g % 2
                        lo = 64 * (h % 2)
                        w = wT[a][1 if kind == "M" else 2][lo:lo + 64, h // 2, :]
                        m = wT[a][0][lo:lo + 64, h // 2, :] if kind == "M" else rawo[a][lo:lo + 64, h // 2, :]
                        mm = nc.tensor.matmul(ps[:, i * P:(i + 1) * P], w, m, start=True, stop=True)
                elif tile[0] == "R":
                    pe.wait_ge(ld_m, 160)
                    mm = nc.tensor.transpose(ps[:, 0:3 * E], rawr[:], ident[0:3 * E, 0:3 * E])
                elif tile[0] == "C":
                    mm = nc.tensor.transpose(ps[:, 0:B], rawc[:], ident[:])
                else:
                    pe.wait_ge(su_dve, t_of[("C",)] + 1)
                    nc.tensor.matmul(ps[:, 0:2 * D], condT[:], rawn[:, tile[1], :], start=True, stop=False)
                    mm = nc.tensor.matmul(ps[:, 0:2 * D], ones[:], brow[:, tile[1], :], start=False, stop=True)
                mm.then_inc(su_pe, 1)

            def wait(w):
                pe.wait_ge(*w)

            def keys(i, u, h):
                a, g = divmod(u, 2)
                if a == 0:
                    pe.wait_ge(hx_lo[0], i + 1)
                else:
                    pe.wait_ge(cx_lo, i)
                if h >= len(ring(u)):
                    pe.wait_ge(kp_lo, k_count(i, u, h - len(ring(u))))
                src = (lambda k: queries(0, k)) if a == 0 else (lambda k: cT[:, k, :])
                bank = key_bank(u, h)
                mm3(by_sample(bank) if a == 0 else bank[:], lambda k: Mw[a][:, k, g * HG + h, :], src).then_inc(k_done, 1)

            def scores(i, u, p):
                n = 4 * seq(i, u) + p
                if p == 0:
                    pe.wait_ge(kp_lo, k_count(i, u, HG - 1))
                    if u == 2:
                        pe.wait_ge(hx_lo[1], i)
                if not (isinstance(n, int) and n < 2):
                    pe.wait_ge(sub_done, n - 1)
                for s in range(2):
                    for q, (k, j) in enumerate(((1, 0), (0, 1), (0, 0))):
                        mm = nc.tensor.matmul(psS[p % 2][:].rearrange("p (h k) -> p h k", h=HG), hq[u // 2][:, k, p, 64 * s:64 * s + P],
                                              kp[:, j, :, p * P + 64 * s:p * P + 64 * s + 64],
                                              start=(s == 0 and q == 0), stop=(s == 1 and q == 2))
                mm.then_inc(s_done, 1)

            def turn(i, u, p):
                n = 4 * seq(i, u) + p
                if not (isinstance(n, int) and n < 1):
                    pe.wait_ge(pt_lo, n)
                pe.wait_ge(prob_done, n + 1)
                for k in range(4):
                    mm = nc.tensor.transpose(psT[:, k * P:(k + 1) * P], pr[:, p, k * P:(k + 1) * P], ident[:])
                mm.then_inc(T_done, 1)

            def weigh(i, u, p):
                n = 4 * seq(i, u) + p
                tm, swapped = (h_tm, tm_sw) if u < 2 else (c_tm, cm_sw)
                if p == 0 and u % 2 == 0:
                    pe.wait_ge(swapped, 64 * ((i if u < 2 else i - 1) + 1))
                pe.wait_ge(pt_lo, n + 1)
                if p >= 2:
                    for w in t_free(i, u, p - 2):
                        wait(w)
                pst = pstw[p % 2]
                for s in range(2):
                    for q, (k, j) in enumerate(((1, 0), (0, 1), (0, 0))):
                        for par in range(2):
                            rows = slice(64 * par, 64 * par + 64)
                            mm = nc.tensor.matmul(pst[par][:].rearrange("p (h r k) -> p h r k", h=4, r=2)[:, :, s, :],
                                                  tm[rows, k, (par + s) % 2, p, :],
                                                  pt[rows, p % 2, j, :].rearrange("p (h r k) -> p h r k", h=4, r=2)[:, :, s, :],
                                                  start=(q == 0), stop=(q == 2))
                            if s == 1 and q == 2:
                                mm.then_inc(t_done, 1)

            def project(i, u, h):
                a, g = divmod(u, 2)
                if h == 0:
                    pe.wait_ge(tt_lo[0], t_count(i, u, 3, False))
                    pe.wait_ge(tt_lo[1], t_count(i, u, 3, True))
                if h == 0 and g == 0:
                    if a == 0 and ok(i - 2):
                        pe.wait_ge(o_out[1], i - 1)
                    if a == 1:
                        pe.wait_ge(o_out[0], i + 1 if ok(i) else NC)
                mm = mm3(psO[:], lambda k: Vw[a][:, k, g * HG + h, :], lambda k: tt[:, k, h % 2, h // 2, :],
                         first=(g == 0 and h == 0), last=(g == 1 and h == HG - 1))
                if h == HG - 1:
                    mm.then_inc(o_done, 1)

            def turn4(bank, done, src):
                for k in range(4):
                    mm = nc.tensor.transpose(bank[:, k * P:(k + 1) * P], src(k), ident[:])
                mm.then_inc(done, 1)

            def back(c, ready, done):
                pe.wait_ge(ready, c + 1)
                turn4(psM, done, lambda k: oT[:, k * P:(k + 1) * P])

            def ln_turn(c, k):
                pe.wait_ge(*((nrm[3], c + 1) if k == 3 else (mods[k], 2 * c + 2)))
                turn4(psM, hx[k], lambda t: (h1 if k == 0 else htm)[:, t, :])

            def glu_up(c, f):
                n = FT * c + f
                if not (isinstance(n, int) and n < 1):
                    pe.wait_ge(glu, n)
                for bank, col in ((psS[0], f * P), (psS[1], DFF + f * P)):
                    mm = mm3(bank[:], lambda k: W1[:, k, col:col + P], lambda k: h3[:, k, :])
                mm.then_inc(ff_done, 1)

            def glu_down(c, f):
                pe.wait_ge(glu_lo, FT * c + f + 1)
                mm3(psM[:], lambda k: W2[:, k, f, :], lambda k: gl[:, k, :], first=f == 0, last=f == FT - 1).then_inc(f2_done, 1)

            def router(c):
                for t in range(NT):
                    mm = mm3(psM[:, t * 3 * E:(t + 1) * 3 * E], lambda k: h3[:, k, t * P:(t + 1) * P], lambda k: WR[:, k, :])
                mm.then_inc(rm_done, 1)

            def slot(i, u):
                here, last, then = live(i, u), live(*before(i, u)), live(*after(i, u))
                li, lu = before(i, u)
                for p in range(NT):
                    if last:
                        if u == 0 and p == 0 and ok(i - 1):
                            pe.wait_ge(y1_done, i)
                        if p == 0 and here and u > 0:
                            pe.wait_ge(kp_lo, k_count(i, u, max(h for h in range(HG) if key_bank(u, h) is psT)))
                        turn(li, lu, p)
                    if p >= 1 and last:
                        if p == 2:
                            for w in misc_free(li, lu):
                                wait(w)
                        weigh(li, lu, p - 1)
                    if here:
                        if p == 0 and u == 3 and ok(i - 2):
                            pe.wait_ge(glu, FT * (i - 2) + 1)
                        if p == 0 and u == 0 and ok(i - 3):
                            pe.wait_ge(glu, FT * (i - 2))
                        scores(i, u, p)
                    if p == 0 and u == 0 and ok(i - 3):
                        glu_down(i - 3, FT - 1)
                def next_key(h):
                    if h < len(RINGS[u]):
                        bank = RINGS[u][h]
                        if last:
                            for w in [(pt_lo, 4 * seq(li, lu) + 4)] if bank is psT else [] if bank in psS else t_free(li, lu, 3 if bank is psH else 2):
                                wait(w)
                        if here and bank in psS:
                            pe.wait_ge(sub_done, 4 * seq(i, u) + 4)
                    keys(*after(i, u), h)

                if last:
                    weigh(li, lu, 3)

                def misc(lag, stage, evacuated=None):
                    if ok(i - lag):
                        if last and evacuated is None:
                            for w in t_free(li, lu, 3):
                                wait(w)
                        for w in misc_free(i, u)[:evacuated] if evacuated else misc_free(li, lu):
                            wait(w)
                        stage(i - lag)

                def turn_context(c):
                    pe.wait_ge(ld_c, 16 * (c + 1))
                    turn4(psM, cx, lambda k: c_in[:, k, :])

                glu_here = u == 3 and ok(i - 2)
                if glu_here and here:
                    pe.wait_ge(sub_done, 4 * seq(i, u) + 4)
                stages = STAGES[u]
                if u == 3 and not glu_here and ok(i):
                    pe.wait_ge(o_out[0], i + 1)
                    if last:
                        pe.wait_ge(pt_lo, 4 * seq(li, lu) + 4)
                    turn4(psT, back1, lambda k: oT[:, k * P:(k + 1) * P])
                for h in range(HG):
                    if then:
                        next_key(h)
                    if glu_here and h == 2:
                        for w in (t_free(li, lu, 3) if last else []) + misc_free(li, lu):
                            wait(w)
                        glu_down(i - 2, 0)
                        if ok(i):
                            pe.wait_ge(o_out[0], i + 1)
                            if last:
                                pe.wait_ge(pt_lo, 4 * seq(li, lu) + 4)
                            turn4(psT, back1, lambda k: oT[:, k * P:(k + 1) * P])
                    for k, (at, lag, name, _) in enumerate(stages):
                        if at == h:
                            misc(lag, {"ln1": lambda c: ln_turn(c, 0), "ln2": lambda c: ln_turn(c, 1),
                                       "ln3": lambda c: ln_turn(c, 2), "ln4": lambda c: ln_turn(c, 3),
                                       "context": turn_context, "router": router,
                                       "back2": lambda c: back(c, o_out[1], back2),
                                       "backf": lambda c: back(c, f2_out, backf)}[name],
                                 None if not any(ok(i - l) for _, l, _, _ in stages[:k]) else sum(ok(i - l) for _, l, _, _ in stages[:k]))
                    if last and h >= 2:
                        project(li, lu, h - 2)
                    if u == 2 and h == 3 and ok(i - 2):
                        if here:
                            pe.wait_ge(sub_done, 4 * seq(i, u) + 4)
                        pe.wait_ge(hx_lo[2], i - 1)
                        glu_up(i - 2, 0)
                    if glu_here and h in (1, 3, 5):
                        glu_up(i - 2, h // 2 + 1)
                    if glu_here and h in (4, 6):
                        glu_down(i - 2, h // 2 - 1)
                if last:
                    project(li, lu, HG - 2)
                    project(li, lu, HG - 1)
            pe.wait_ge(pads, 2)
            pe.wait_ge(mods[0], 2)
            turn4(psM, hx[0], lambda t: h1[:, t, :])
            for h in range(HG):
                keys(0, 0, h)
            rounds(pe, lambda i: [slot(i, u) for u in range(4)])
            pe.drain().then_inc(a_end, 1)

            pe.wait_ge(mix_cp, NC)
            for n, (k, g) in enumerate(EU):
                if n >= 4:
                    pe.wait_ge(eu_dve, n - 3)
                else:
                    pe.wait_ge(a_end, 4)
                pe.wait_ge(ld_e[k], 16 * (E if k < 2 else 1))
                for i, j in enumerate(range(4 * g, min(4 * g + 4, MT))):
                    src = rawe[k][:, j, :] if k < 2 else rawe[2][:].rearrange("p a b -> p (a b)").rearrange("p (q j) -> p j q", j=MT)[:, j, :]
                    mm = nc.tensor.transpose(SR[n % 4][:, i * P:(i + 1) * P], src, ident[:])
                mm.then_inc(eu_pe, 1)
            pe.wait_ge(rt, RT_LAST)
            for i in range(4):
                mm = nc.tensor.transpose(psum[7][:, i * P:(i + 1) * P], rr[5][:].rearrange("p t e -> p (t e)")[:, i * P:(i + 1) * P], ident[:])
            mm.then_inc(gt_pe, 1)
            pe.wait_ge(eu_act, NEU)
            pe.wait_ge(eu_dve, NEU)
            pe.wait_ge(gt_cp, 1)

            def up(c, i, j, first):
                m = c * MT + j
                if not (first and j < 3):
                    pe.wait_ge(ug_done, m - 1 if i == 0 and j < 2 else m - 2)
                b = (j + i) % 3
                mm3(psum[b][:], lambda k: WE[:, 0, k, j, :], lambda k: nT[i][:, k, :])
                mm3(psum[3 + b][:], lambda k: WE[:, 1, k, j, :], lambda k: nT[i][:, k, :]).then_inc(ag_done, 1)

            def down(c, i, j):
                r = (i * MT + j) % UR
                pe.wait_ge(ul_done, c * MT + j + 1)
                mm = mm3(psum[6 + i][:], lambda k: WE[:, 2, k, j, :], lambda k: uu[:, r, k, :], first=j == 0, last=j == MT - 1)
                mm.then_inc(e_done, 1)

            def back_b(c, i):
                pe.wait_ge(mo_out, c + 1)
                for t in range(4):
                    mm = nc.tensor.transpose(psum[6 + i][:, t * P:(t + 1) * P], oTb[:, t * P:(t + 1) * P], ident[:])
                mm.then_inc(mb_done, 1)

            def chunk(c, i, first=False):
                for j in range(MT):
                    up(c, i, j, first)
                    if j >= LAG:
                        if j == LAG and not (isinstance(c, int) and c < 2):
                            pe.wait_ge(ob_done, c - 1)
                        down(c, i, j - LAG)
                    elif not first:
                        down(c - 1, 1 - i, MT + j - LAG)
                    if j == LAG + 2 and not first:
                        back_b(c - 1, 1 - i)

            pe.wait_ge(ld_nb[0], 16)
            chunk(0, 0, first=True)
            pe.wait_ge(ld_nb[1], 16)
            chunk(1, 1)
            with pe.Fori(1, NC // 2) as d:
                for i in range(2):
                    pe.wait_ge(ld_nb[i], 16 * d + 16)
                    chunk(2 * d + i, i)
            for j in range(MT - LAG, MT):
                down(NC - 1, 1, j)
            back_b(NC - 1, 1)

        @block.scalar
        def _(act):
            def copy(o, i):
                return nc.scalar.activation(o, i, ACT.Copy)

            for n, tile in enumerate(tiles):
                ps = SR[n % 4]
                act.wait_ge(su_pe, n + 1)
                if tile[0] == "T":
                    _, a, k, g = tile
                    op = copy(wT[a][k][:, 4 * g:4 * g + 2, :].rearrange("p a b -> p (a b)"), ps[:, 0:2 * P])
                elif tile[0] in "MV":
                    kind, a, g = tile
                    dst = (Mw if kind == "M" else Vw)[a]
                    op = copy(dst[:, 0, 8 * (g // 2) + g % 2:8 * (g // 2) + 8:2, :], ps[:].rearrange("p (a b) -> p a b", a=4))
                elif tile[0] == "R":
                    op = copy(WR[:, 0, :], ps[:, 0:3 * E])
                elif tile[0] == "C":
                    op = copy(condT[:, 0:B // 2], ps[:, 0:B // 2])
                else:
                    op = copy(emb[:, tile[1], D:2 * D], ps[:, D:2 * D])
                op.then_inc(su_act, 1)
            act.wait_ge(ld_m, 160)
            copy(W1[:, 0, :], raw1[:]).then_inc(su_act, 1)
            copy(W2[:, 0], raw2[:]).then_inc(su_act, 1)
            act.wait_ge(ld_b, 64)

            def exp(i, u, p):
                act.wait_ge(sub_done, 4 * seq(i, u) + p + 1)
                nc.scalar.activation(pr[:, p, :], pr[:, p, :], ACT.Exp, scale=SCALE).then_inc(exp_done, 1)

            def turn_hi(i, u, p):
                n = 4 * seq(i, u) + p
                act.wait_ge(T_done, n + 1)
                if not (isinstance(n, int) and n < 2):
                    act.wait_ge(t_done, 2 * n - 2)
                copy(pt[:, p % 2, 0, :], psT[:]).then_inc(pt_hi, 1)

            def weigh_hi(i, u, p):
                n = 4 * seq(i, u) + p
                if p == 0 and not (isinstance(n, int) and n < 1):
                    act.wait_ge(o_done, seq(i, u))
                pst = pstw[p % 2]
                act.wait_ge(t_done, 2 * n + 1)
                copy(tt_tile(0, p, 0), heads4(pst[0])).then_inc(tt_hi, 1)
                act.wait_ge(t_done, 2 * n + 2)
                op = copy(tt_tile(0, p, 1), heads4(pst[1]))
                if p in POOL_TILES:
                    for w in (tmp_free(*after(i, u)) if p == POOL_TILES[0] else [(tt_lo[1], t_count(i, u, p, True) - 1)]):
                        act.wait_ge(*w)
                    copy(heads4(tmp2), heads4(pst[1])).then_inc(tt_raw, 1)
                else:
                    op.then_inc(tt_hi, 1)

            def keys_hi(i, u, h):
                act.wait_ge(k_done, k_count(i, u, h))
                copy(kp[:, 0, h, :], key_bank(u, h)[:]).then_inc(kp_hi, 1)

            def out_attn(c, a):
                act.wait_ge(o_done, seq(c + 1 if a else c, 2 * a + 1) + 1)
                if a == 0:
                    if ok(c - 3):
                        act.wait_ge(rt_done, c - 2)
                    if ok(c - 2):
                        act.wait_ge(back2, c - 1)
                else:
                    if ok(c - 1):
                        act.wait_ge(backf, c)
                    act.wait_ge(back1, c + 2 if ok(c + 1) else NC)
                nc.scalar.activation(oT[:], psO[:], ACT.Identity, bias=b_o[:, a:a + 1]).then_inc(o_out[a], 1)

            def ln_hi(c, k):
                act.wait_ge(hx[k], c + 1)
                if k == 2 and not first(c):
                    act.wait_ge(st_n4, 16 * c)
                    act.wait_ge(rm_done, c)
                dst, src = (queries(k, 0), by_sample(psM)) if k < 2 else (h3[:, 0, :], psM[:])
                copy(dst, src).then_inc(hx_hi[k], 1)

            def glu_act(c, f):
                n = FT * c + f
                if f < 2:
                    for w in tmp_split(c + 2, 2 + f) + (tmp_free(c + 2, 2) if f == 0 else []):
                        act.wait_ge(*w)
                if f > 0:
                    act.wait_ge(glu_lo, n)
                act.wait_ge(ff_done, n + 1)
                nc.scalar.activation(tmp2, psS[1][:], ACT.Gelu, bias=b_1[:, FT + f:FT + f + 1]).then_inc(gel, 1)

            def glu_split(c, f):
                n = FT * c + f
                act.wait_ge(glu, n + 1)
                if not (isinstance(n, int) and n < 1):
                    act.wait_ge(f2_done, n)
                copy(gl[:, 0, :], tmp2).then_inc(glu_hi, 1)

            def out_glu(c):
                act.wait_ge(f2_done, FT * c + FT)
                act.wait_ge(back1, c + 3 if ok(c + 2) else NC)
                if c_last(c):
                    act.wait_ge(back2, c + 1)
                if not ok(c + 2):
                    act.wait_ge(rt_done, c)
                nc.scalar.activation(oT[:], psM[:], ACT.Identity, bias=b_2[:, 0:1]).then_inc(f2_out, 1)

            def mix_out(c):
                act.wait_ge(rm_done, c + 1)
                copy(oT[:, 0:NT * 3 * E], psM[:, 0:NT * 3 * E]).then_inc(mix_cp, 1)

            def router_exp(c):
                act.wait_ge(rt_sub, c + 1)
                nc.scalar.activation(qk4, qk4, ACT.Exp).then_inc(rt_exp, 1)

            def tm_split(c):
                act.wait_ge(mods[0], 2 * c + 2)
                if not first(c):
                    act.wait_ge(t_done, 8 * seq(c, 0))
                copy(h_tm[:, 0, 0], h1[:]).then_inc(tm_hi, 1)

            def context(c):
                act.wait_ge(cx, c + 1)
                copy(cT[:, 0, :], psM[:]).then_inc(cx_hi, 1)

            def cm_split(c):
                act.wait_ge(t_done, 8 * seq(c + 1, 2))
                copy(c_tm[:, 0, 0], c_in[:]).then_inc(cm_hi, 1)

            def slot(i, u):
                here, last, then = live(i, u), live(*before(i, u)), live(*after(i, u))
                li, lu = before(i, u)
                for p in range(NT):
                    if last:
                        turn_hi(li, lu, p)
                    if u == 0 and p == 0 and ok(i - 3):
                        out_glu(i - 3)
                    if p >= 1 and here:
                        exp(i, u, p - 1)
                    if p >= 1 and last:
                        weigh_hi(li, lu, p - 1)
                if here:
                    exp(i, u, 3)
                if last:
                    weigh_hi(li, lu, 3)
                hooks = {0: ((1, 0, tm_split), (3, 1, lambda c: ln_hi(c, 1)), (5, 1, context)),
                         1: ((5, 3, lambda c: ln_hi(c, 3)), (8, 3, mix_out)),
                         2: ((3, 2, lambda c: ln_hi(c, 2)), (5, 2, lambda c: glu_act(c, 0)), (6, 2, lambda c: glu_split(c, 0)),
                             (0, 3, router_exp), (1, 1, cm_split), (8, -1, lambda c: ln_hi(c, 0))),
                         3: ()}[u]
                for h in range(HG + 1):
                    for at, lag, stage in hooks:
                        if at == h and ok(i - lag):
                            stage(i - lag)
                    if u == 3 and ok(i - 2):
                        if h in (2, 4, 6):
                            glu_act(i - 2, h // 2)
                        if h in (3, 5, 7):
                            glu_split(i - 2, h // 2)
                    if h < HG and then:
                        keys_hi(*after(i, u), h)
                if last and lu == 1:
                    out_attn(li, 0)
                if last and lu == 3:
                    out_attn(li - 1, 1)
            ln_hi(0, 0)
            for h in range(HG):
                keys_hi(0, 0, h)
            rounds(act, lambda i: [slot(i, u) for u in range(4)])
            act.drain().then_inc(a_end, 1)

            act.wait_ge(a_end, 4)
            for n, (k, g) in enumerate(EU):
                if n == 4:
                    act.wait_ge(rt, RT_DIFF)
                    nc.scalar.activation(r1[3][:], r1[3][:], ACT.Exp).then_inc(rt_act, 1)
                act.wait_ge(eu_pe, n + 1)
                w = min(4, MT - 4 * g)
                copy(WE[:, k, 0, 4 * g:4 * g + w, :].rearrange("p a b -> p (a b)"), SR[n % 4][:, 0:w * P]).then_inc(eu_act, 1)

            def silu(c, i, j, first=False):
                m = c * MT + j
                act.wait_ge(ag_done, m + 1)
                if not (first and j < 2):
                    act.wait_ge(ug_done, m - 1)
                nc.scalar.activation(sil[:, j % 2, :], psum[(j + i) % 3][:], ACT.Silu).then_inc(sil_done, 1)

            def uhi(c, i, j):
                m = c * MT + j
                act.wait_ge(uc_done, m + 1)
                if not (isinstance(m, int) and m < UR):
                    act.wait_ge(e_done, m - UR + 1)
                copy(uu[:, (i * MT + j) % UR, 0, :], ug[:, (i * MT + j) % 4, :]).then_inc(uh_done, 1)

            def out_b(c, i):
                act.wait_ge(e_done, (c + 1) * MT)
                if not (isinstance(c, int) and c == 0):
                    act.wait_ge(mb_done, c)
                copy(oTb[:], psum[6 + i][:]).then_inc(mo_out, 1)

            def chunk(c, i, first=False):
                for j in range(MT):
                    silu(c, i, j, first)
                    if j >= 2:
                        uhi(c, i, j - 2)
                    elif not first:
                        uhi(c - 1, 1 - i, MT + j - 2)
                    if j == LAG and not first:
                        out_b(c - 1, 1 - i)

            chunk(0, 0, first=True)
            chunk(1, 1)
            with act.Fori(1, NC // 2) as d:
                for i in range(2):
                    chunk(2 * d + i, i)
            for j in range(MT - 2, MT):
                uhi(NC - 1, 1, j)
            out_b(NC - 1, 1)

        @block.vector
        def _(dve):
            tensor = nc.vector.tensor_tensor
            nc.vector.memset(half[:], -0.5).then_inc(consts, 1)
            nc.vector.memset(ones[:], 1.0).then_inc(consts, 1)
            nc.vector.memset(nothing[:], 0.0).then_inc(st_out, 16)
            nc.vector.memset(eps[:], EPS).then_inc(consts, 1)
            for n, tile in enumerate(tiles):
                ps = SR[n % 4]
                dve.wait_ge(su_act, n + 1)
                if tile[0] == "T":
                    _, a, k, g = tile
                    op = nc.vector.tensor_copy(wT[a][k][:, 4 * g + 2:4 * g + 4, :].rearrange("p a b -> p (a b)"), ps[:, 2 * P:])
                elif tile[0] in "MV":
                    kind, a, g = tile
                    dst = (Mw if kind == "M" else Vw)[a]
                    hi, lo = (dst[:, k, 8 * (g // 2) + g % 2:8 * (g // 2) + 8:2, :] for k in range(2))
                    op = tensor(lo, ps[:].rearrange("p (a b) -> p a b", a=4), f32(hi), ALU.subtract)
                elif tile[0] == "R":
                    op = tensor(WR[:, 1, :], ps[:, 0:3 * E], f32(WR[:, 0, :]), ALU.subtract)
                elif tile[0] == "C":
                    op = nc.vector.tensor_copy(condT[:, B // 2:], ps[:, B // 2:B])
                else:
                    op = nc.vector.tensor_scalar(emb[:, tile[1], 0:D], ps[:, 0:D], 1.0, None, ALU.add)
                op.then_inc(su_dve, 1)
            dve.wait_ge(su_act, NSU + 1)
            tensor(W1[:, 1, :], raw1[:], f32(W1[:, 0, :]), ALU.subtract).then_inc(su_dve, 1)
            dve.wait_ge(su_act, NSU + 2)
            tensor(W2[:, 1], raw2[:], f32(W2[:, 0]), ALU.subtract).then_inc(su_dve, 1)

            def heads(ap):
                return ap.rearrange("p (h k) -> p h k", h=HG)

            def peak(i, u, p):
                n = 4 * seq(i, u) + p
                dve.wait_ge(s_done, n + 1)
                nc.vector.tensor_reduce(mx[:, p % 2, :], heads(psS[p % 2][:]), AX_X, ALU.max).then_inc(max_done, 1)
                dve.wait_ge(max_done, n + 1)
                tensor(heads(pr[:, p, :]), heads(psS[p % 2][:]), mx[:, p % 2, :].unsqueeze(2).broadcast_to([P, HG, 64]), ALU.subtract).then_inc(sub_done, 1)

            def total(i, u, p):
                n = 4 * seq(i, u) + p
                dve.wait_ge(exp_done, n + 1)
                nc.vector.tensor_reduce(sm[:, p, :], heads(pr[:, p, :]), AX_X, ALU.add).then_inc(sum_done, 1)
                dve.wait_ge(sum_done, n + 1)
                nc.vector.reciprocal(sm[:, p, :], sm[:, p, :]).then_inc(rec_done, 1)

            def turn_lo(i, u, p):
                dve.wait_ge(pt_hi, 4 * seq(i, u) + p + 1)
                tensor(pt[:, p % 2, 1, :], psT[:], f32(pt[:, p % 2, 0, :]), ALU.subtract).then_inc(pt_lo, 1)

            def weigh_lo(i, u, p):
                for par in range(1 if p in POOL_TILES else 2):
                    dve.wait_ge(tt_hi, t_count(i, u, p, False) - (par == 0 and p not in POOL_TILES))
                    tensor(tt_tile(1, p, par), heads4(pstw[p % 2][par]), f32(tt_tile(0, p, par)), ALU.subtract).then_inc(tt_lo[0], 1)

            def keys_lo(i, u, h):
                dve.wait_ge(kp_hi, k_count(i, u, h))
                tensor(kp[:, 1, h, :], key_bank(u, h)[:], f32(kp[:, 0, h, :]), ALU.subtract).then_inc(kp_lo, 1)

            def ln_stats(k, c, src):
                z, v, s = 12 * c, lv[k], st
                for t in range(NT):
                    nc.vector.bn_stats(s[:, t, :], src[:, t, :]).then_inc(stat[k], 1)
                dve.wait_ge(stat[k], z + 4)
                me, M2e, mo, M2o = s[:, :, 1], s[:, :, 2], s[:, :, 4], s[:, :, 5]
                tensor(v[:, 0, :], me, mo, ALU.add).then_inc(stat[k], 1)
                tensor(v[:, 1, :], me, mo, ALU.subtract).then_inc(stat[k], 1)
                tensor(v[:, 2, :], M2e, M2o, ALU.add).then_inc(stat[k], 1)
                dve.wait_ge(stat[k], z + 7)
                nc.vector.tensor_scalar(v[:, 4, :], v[:, 0, :], 0.5, None, ALU.mult).then_inc(stat[k], 1)
                nc.vector.scalar_tensor_tensor(v[:, 3, :], v[:, 1, :], D / 4.0, v[:, 1, :], ALU.mult, ALU.mult).then_inc(stat[k], 1)
                dve.wait_ge(stat[k], z + 9)
                tensor(v[:, 0, :], v[:, 2, :], v[:, 3, :], ALU.add).then_inc(stat[k], 1)
                dve.wait_ge(stat[k], z + 10)
                nc.vector.tensor_scalar(v[:, 5, :], v[:, 0, :], 1.0 / D, None, ALU.mult).then_inc(stat[k], 1)
                nc.vector.tensor_scalar(v[:, 6, :], v[:, 0, :], 1.0 / D, EPS, ALU.mult, ALU.add).then_inc(stat[k], 1)

            def ln_norm(k, src, dst):
                v = lv[k]
                for t in range(NT):
                    op = nc.vector.tensor_scalar(dst[:, t, :], src[:, t, :], v[:, 4, t:t + 1], v[:, 7, t:t + 1], ALU.subtract, ALU.mult)
                op.then_inc(nrm[k], 1)

            def ln1_stats(c):
                dve.wait_ge(ld_x, 16 * (c + 1))
                ln_stats(0, c, x_in)

            def ln1(c):
                dve.wait_ge(rstd[0], 5 * c + 5)
                ln_norm(0, x_in, x_in)
                dve.wait_ge(nrm[0], c + 1)
                dve.wait_ge(ld_mod[0], 32 * c + 32)
                if not first(c):
                    dve.wait_ge(hx[0], c)
                    dve.wait_ge(tm_hi, c)
                    dve.wait_ge(tm_lo, c)
                for t in range(NT):
                    op = nc.vector.scalar_tensor_tensor(h1[:, t, :], x_in[:, t, :], lv[0][:, 11, t:t + 1], mod[:, t, 0:D], ALU.mult, ALU.mult)
                op.then_inc(mods[0], 1)
                dve.wait_ge(mods[0], 2 * c + 1)
                tensor(h1[:], h1[:], mod[:, :, D:2 * D], ALU.add).then_inc(mods[0], 1)

            def ln_lo(c, k):
                dve.wait_ge(hx_hi[k], c + 1)
                if k < 2:
                    tensor(queries(k, 1), by_sample(psM), f32(queries(k, 0)), ALU.subtract).then_inc(hx_lo[k], 1)
                else:
                    tensor(h3[:, 1, :], psM[:], f32(h3[:, 0, :]), ALU.subtract).then_inc(hx_lo[k], 1)

            tiles3 = lambda ap: ap.rearrange("p (t d) -> p t d", t=NT)

            def after_attn1(c):
                dve.wait_ge(back1, c + 1)
                dve.wait_ge(ld_xn, 16 * c + 16)
                tensor(res[:], tiles3(psT[:]), res[:], ALU.add).then_inc(y1_done, 1)

            def norm2(c):
                dve.wait_ge(rstd[1], c + 1)
                if ok(c - 2):
                    dve.wait_ge(hx[2], c - 1)
                elif c == 1:
                    dve.wait_ge(hx[1], 1)
                ln_norm(1, res, htm)

            def after_attn2(c):
                dve.wait_ge(back2, c + 1)
                dve.wait_ge(ld_y1, 16 * c + 16)
                for w in tmp_free(c + 2, 1) + tmp_split(c + 2, 1):
                    dve.wait_ge(*w)
                tensor(tmp[:], tiles3(psM[:]), res[:], ALU.add).then_inc(y2_done, 1)

            def norm3(c):
                dve.wait_ge(rstd[2], c + 1)
                if ok(c - 1):
                    dve.wait_ge(hx[3], c)
                elif ok(c + 1):
                    dve.wait_ge(hx[1], c + 2)
                ln_norm(2, tmp, htm)

            def after_glu(c):
                dve.wait_ge(backf, c + 1)
                dve.wait_ge(ld_u, 16 * (c + 1))
                for w in tmp_free(c + 3, 0) + tmp_split(c + 3, 0):
                    dve.wait_ge(*w)
                tensor(tmp[:], tiles3(psM[:]), res[:], ALU.add).then_inc(x1_done, 1)
                dve.wait_ge(x1_done, c + 1)
                ln_stats(3, c, tmp)

            def norm4(c):
                dve.wait_ge(rstd[3], c + 1)
                if ok(c + 2):
                    dve.wait_ge(hx[1], c + 3)
                elif ok(c + 1):
                    dve.wait_ge(hx[2], c + 1)
                else:
                    dve.wait_ge(hx[2], c + 1)
                ln_norm(3, tmp, htm)

            def glu_mul(c, f):
                dve.wait_ge(gel, FT * c + f + 1)
                nc.vector.scalar_tensor_tensor(tmp2, psS[0][:], b_1[:, f:f + 1], tmp2, ALU.add, ALU.mult).then_inc(glu, 1)

            def glu_split_lo(c, f):
                dve.wait_ge(glu_hi, FT * c + f + 1)
                tensor(gl[:, 1, :], tmp2, f32(gl[:, 0, :]), ALU.subtract).then_inc(glu_lo, 1)

            def context(c):
                dve.wait_ge(cx_hi, c + 1)
                tensor(cT[:, 1, :], psM[:], f32(cT[:, 0, :]), ALU.subtract).then_inc(cx_lo, 1)

            def router_peak(c):
                dve.wait_ge(rt_qk, c + 1)
                nc.vector.tensor_reduce(rt_max, qk4, AX_X, ALU.max).then_inc(rt_peak, 1)

            def router_sum(c):
                dve.wait_ge(rt_exp, c + 1)
                nc.vector.tensor_reduce(rt_sum, qk4, AX_X, ALU.add).then_inc(rt_tot, 1)

            def router_dot(c):
                dve.wait_ge(rt_mul, c + 1)
                nc.vector.tensor_reduce(rt_dot, qk4, AX_X, ALU.add).then_inc(rt_dotted, 1)
                dve.wait_ge(rt_tot, c + 1)
                nc.vector.reciprocal(rt_sum, rt_sum).then_inc(rt_rec, 1)

            def slot(i, u):
                here, last, then = live(i, u), live(*before(i, u)), live(*after(i, u))
                li, lu = before(i, u)
                for p in range(NT):
                    if last:
                        turn_lo(li, lu, p)
                    if u == 2 and p == 2 and ok(i - 3):
                        router_peak(i - 3)
                    if here:
                        peak(i, u, p)
                    if u == 1 and p == 0 and ok(i - 3):
                        norm4(i - 3)
                    if p >= 1 and last:
                        weigh_lo(li, lu, p - 1)
                    if p >= 4 - EARLY and here:
                        total(i, u, p + EARLY - 4)
                if last:
                    weigh_lo(li, lu, 3)

                def stats2(c):
                    dve.wait_ge(y1_done, c + 1)
                    ln_stats(1, c, res)

                def stats3(c):
                    dve.wait_ge(y2_done, c + 1)
                    ln_stats(2, c, tmp)

                hooks = {0: ((3, 1, lambda c: ln_lo(c, 1)), (5, 1, context), (7, 3, after_glu)),
                         1: ((3, 2, after_attn2), (4, 2, stats3), (5, 3, lambda c: ln_lo(c, 3)), (6, 2, norm3), (8, -1, ln1_stats)),
                         2: ((2, 3, router_sum), (4, 3, router_dot), (3, 2, lambda c: ln_lo(c, 2)), (4, -1, ln1), (6, 2, lambda c: glu_mul(c, 0)), (7, 2, lambda c: glu_split_lo(c, 0)), (8, -1, lambda c: ln_lo(c, 0))),
                         3: ((3, 0, after_attn1), (4, 0, stats2), (7, 0, norm2))}[u]
                for h in range(HG + 1):
                    if u == 3 and ok(i - 2) and h in (3, 5, 7):
                        glu_mul(i - 2, h // 2)
                    if u == 3 and ok(i - 2) and h in (4, 6, 8):
                        glu_split_lo(i - 2, h // 2 - 1)
                    for at, lag, stage in hooks:
                        if at == h and ok(i - lag):
                            stage(i - lag)
                    if h < NT - EARLY and here:
                        total(i, u, h + EARLY)
                    if h < HG and then:
                        keys_lo(*after(i, u), h)

            ln1_stats(0)
            ln1(0)
            ln_lo(0, 0)
            for h in range(HG):
                keys_lo(0, 0, h)
            rounds(dve, lambda i: [slot(i, u) for u in range(4)])
            dve.drain().then_inc(a_end, 1)

            dve.wait_ge(a_end, 4)
            dve.wait_ge(ld_mx, 16)
            TTE = [P, TT, E]

            count = [0]

            def step(op):
                op.then_inc(rt, 1)
                count[0] += 1
                dve.wait_ge(rt, count[0])

            def over(ap):
                return ap.unsqueeze(2).broadcast_to(TTE)

            def pick(logits, mask, eq, top, first_eq):
                step(nc.vector.tensor_reduce(top, logits, AX_X, ALU.max))
                step(tensor(eq, logits, over(top), ALU.is_equal))
                step(tensor(eq, eq, pri[:].unsqueeze(1).broadcast_to(TTE), ALU.mult))
                step(nc.vector.tensor_reduce(first_eq, eq, AX_X, ALU.max))
                step(tensor(mask, eq, over(first_eq), ALU.is_equal))

            for e in range(E):
                step(nc.vector.memset(pri[:, e:e + 1], float(E - e)))
            pick(rr[3][:], rr[1][:], rr[0][:], r1[0][:], r1[1][:])
            step(nc.vector.scalar_tensor_tensor(rr[2][:], rr[1][:], -3e38, rr[3][:], ALU.mult, ALU.add))
            pick(rr[2][:], rr[4][:], rr[0][:], r1[2][:], r1[1][:])
            step(tensor(r1[3][:], r1[2][:], r1[0][:], ALU.subtract))
            assert count[0] == RT_DIFF
            dve.wait_ge(rt_act, 1)
            step(nc.vector.tensor_scalar(r1[0][:], r1[3][:], 1.0, None, ALU.add))
            step(nc.vector.reciprocal(r1[0][:], r1[0][:]))
            step(tensor(r1[3][:], r1[3][:], r1[0][:], ALU.mult))
            step(tensor(rr[1][:], rr[1][:], over(r1[0][:]), ALU.mult))
            step(tensor(rr[4][:], rr[4][:], over(r1[3][:]), ALU.mult))
            step(tensor(rr[5][:], rr[1][:], rr[4][:], ALU.add))
            assert count[0] == RT_LAST
            for n, (k, g) in enumerate(EU):
                dve.wait_ge(eu_act, n + 1)
                w = min(4, MT - 4 * g)
                hi, lo = (WE[:, k, i, 4 * g:4 * g + w, :].rearrange("p a b -> p (a b)") for i in range(2))
                tensor(lo, SR[n % 4][:, 0:w * P], f32(hi), ALU.subtract).then_inc(eu_dve, 1)
            dve.wait_ge(gt_pe, 1)
            nc.vector.tensor_copy(gT[:].rearrange("p a b -> p (a b)"), psum[7][:]).then_inc(gt_cp, 1)

            def gate_mul(c, i, j, first=False):
                m = c * MT + j
                r = (i * MT + j) % 4
                dve.wait_ge(sil_done, m + 1)
                if not (first and j < 4):
                    dve.wait_ge(uh_done, m - 3)
                    dve.wait_ge(ul_done, m - 3)
                tensor(ug[:, r, :], psum[3 + (j + i) % 3][:], sil[:, j % 2, :], ALU.mult).then_inc(ug_done, 1)

            def ulo(c, i, j):
                r = (i * MT + j) % UR
                dve.wait_ge(uh_done, c * MT + j + 1)
                tensor(uu[:, r, 1, :], ug[:, (i * MT + j) % 4, :], f32(uu[:, r, 0, :]), ALU.subtract).then_inc(ul_done, 1)

            def out_b(c, i):
                dve.wait_ge(mb_done, c + 1)
                dve.wait_ge(ld_xb[i], 16 * (c // 2 + 1) if isinstance(c, int) else 8 * (c - i) + 16)
                dve.wait_ge(st_out, 16 * (c + 1))
                tensor(ob[:], tiles3(psum[6 + i][:]), x1b[i][:], ALU.add).then_inc(ob_done, 1)

            def chunk(c, i, first=False):
                for j in range(MT):
                    gate_mul(c, i, j, first)
                    if j >= 2:
                        ulo(c, i, j - 2)
                    elif not first:
                        ulo(c - 1, 1 - i, MT + j - 2)
                    if j == LAG + 3 and not first:
                        out_b(c - 1, 1 - i)

            dve.wait_ge(gt_st, 16)
            chunk(0, 0, first=True)
            chunk(1, 1)
            with dve.Fori(1, NC // 2) as d:
                for i in range(2):
                    chunk(2 * d + i, i)
            for j in range(MT - 2, MT):
                ulo(NC - 1, 1, j)
            out_b(NC - 1, 1)

        @block.gpsimd
        def _(pool):
            nc.gpsimd.memset(ident[:], 0.0).then_inc(identity, 1)
            pool.wait_ge(identity, 1)
            nc.gpsimd.affine_select(out=ident[:], in_=ident[:], compare_op=ALU.not_equal, fill=1.0, base=0,
                                    pattern=[[-1, P]], channel_multiplier=1).then_inc(identity, 1)
            pool.wait_ge(consts, 3)
            pool.wait_ge(emb_w, 16)
            for a in range(2):
                nc.gpsimd.memset(f32(hq[a][:, :, :, 64:128]), 0.0).then_inc(pads, 1)
            tensor = nc.gpsimd.tensor_tensor

            def prob(i, u, p):
                pool.wait_ge(rec_done, 4 * seq(i, u) + p + 1)
                v = pr[:, p, :].rearrange("p (h k) -> p h k", h=HG)
                tensor(v, v, sm[:, p, :].unsqueeze(2).broadcast_to([P, HG, 64]), ALU.mult).then_inc(prob_done, 1)

            def weigh_lo(i, u, p):
                if p in POOL_TILES:
                    pool.wait_ge(tt_raw, t_count(i, u, p, True))
                    tensor(tt_tile(1, p, 1), heads4(tmp2), f32(tt_tile(0, p, 1)), ALU.subtract).then_inc(tt_lo[1], 1)

            def ln_rstd(k, c):
                pool.wait_ge(stat[k], 12 * c + 12)
                tensor(lv[k][:, 7, :], lv[k][:, 6, :], half[:], ALU.pow).then_inc(rstd[k], 1)

            def ln1_rstd(c):
                v = lv[0]
                pool.wait_ge(stat[0], 12 * c + 12)
                tensor(v[:, 7, :], v[:, 6, :], half[:], ALU.pow).then_inc(rstd[0], 1)
                pool.wait_ge(rstd[0], 5 * c + 1)
                tensor(v[:, 8, :], v[:, 5, :], v[:, 7, :], ALU.mult).then_inc(rstd[0], 1)
                pool.wait_ge(rstd[0], 5 * c + 2)
                tensor(v[:, 9, :], v[:, 8, :], v[:, 7, :], ALU.mult).then_inc(rstd[0], 1)
                pool.wait_ge(rstd[0], 5 * c + 3)
                tensor(v[:, 10, :], v[:, 9, :], eps[:], ALU.add).then_inc(rstd[0], 1)
                pool.wait_ge(rstd[0], 5 * c + 4)
                tensor(v[:, 11, :], v[:, 10, :], half[:], ALU.pow).then_inc(rstd[0], 1)

            def modulate(c, k):
                pool.wait_ge(nrm[k], c + 1)
                pool.wait_ge(ld_mod[k], 32 * c + 32)
                tensor(htm[:], htm[:], mod[:, :, 0:D], ALU.mult).then_inc(mods[k], 1)
                pool.wait_ge(mods[k], 2 * c + 1)
                tensor(htm[:], htm[:], mod[:, :, D:2 * D], ALU.add).then_inc(mods[k], 1)

            def add_x(c):
                pool.wait_ge(nrm[2], c + 1)
                pool.wait_ge(ld_xa, 16 * c + 16)
                tensor(tmp[:], tmp[:], res[:], ALU.add).then_inc(u_done, 1)

            def tm_lo_(c):
                pool.wait_ge(tm_hi, c + 1)
                tensor(h_tm[:, 1, 0], h1[:], f32(h_tm[:, 0, 0]), ALU.subtract).then_inc(tm_lo, 1)

            def cm_lo_(c):
                pool.wait_ge(cm_hi, c + 1)
                tensor(c_tm[:, 1, 0], c_in[:], f32(c_tm[:, 0, 0]), ALU.subtract).then_inc(cm_lo, 1)

            def pairs(ap, axis):
                return ap.unsqueeze(axis).broadcast_to([P, NT, E, E])

            def router_qk(c):
                pool.wait_ge(mix_cp, c + 1)
                tensor(qk4, pairs(mixed[:, :, 0:E], 3), pairs(mixed[:, :, E:2 * E], 2), ALU.mult).then_inc(rt_qk, 1)

            def router_sub(c):
                pool.wait_ge(rt_peak, c + 1)
                tensor(qk4, qk4, pairs(rt_max, 3), ALU.subtract).then_inc(rt_sub, 1)

            def router_mul(c):
                pool.wait_ge(rt_tot, c + 1)
                tensor(qk4, qk4, pairs(mixed[:, :, 2 * E:3 * E], 2), ALU.mult).then_inc(rt_mul, 1)

            def router_out(c):
                pool.wait_ge(rt_dotted, c + 1)
                pool.wait_ge(rt_rec, c + 1)
                if not first(c):
                    pool.wait_ge(st_mix, 16 * c)
                tensor(rt_o[:], rt_dot, rt_sum, ALU.mult).then_inc(rt_done, 1)

            def slot(i, u):
                here, last, then = live(i, u), live(*before(i, u)), live(*after(i, u))
                li, lu = before(i, u)
                for p in range(NT):
                    if last:
                        weigh_lo(li, lu, p)
                    if u == 2 and p == 1 and ok(i - 3):
                        router_sub(i - 3)
                hooks = {0: ((2, 0, tm_lo_), (8, 3, lambda c: ln_rstd(3, c))),
                         1: ((4, 2, lambda c: ln_rstd(2, c)), (7, 2, lambda c: modulate(c, 2)), (7, 2, add_x), (8, -1, ln1_rstd), (8, 3, router_qk)),
                         2: ((2, 3, router_mul), (2, 1, cm_lo_), (4, 3, router_out)),
                         3: ((5, 0, lambda c: ln_rstd(1, c)), (8, 0, lambda c: modulate(c, 1)))}[u]
                for h in range(HG + 1):
                    if h < NT and here:
                        prob(i, u, h)
                    for at, lag, stage in hooks:
                        if at == h and ok(i - lag):
                            stage(i - lag)

            ln1_rstd(0)
            rounds(pool, lambda i: [slot(i, u) for u in range(4)])
            pool.drain().then_inc(a_end, 1)

            def gate(c, i, j):
                r = (i * MT + j) % 4
                m = c * MT + j
                pool.wait_ge(ug_done, m + 1)
                tensor(ug[:, r, :], ug[:, r, :], gb[i][:], ALU.mult).then_inc(uc_done, 1)

            pool.wait_ge(a_end, 4)
            for i in range(2):
                pool.wait_ge(ld_gb[i], 16 * E)
                for j in range(MT):
                    gate(i, i, j)
            with pool.Fori(1, NC // 2) as d:
                for i in range(2):
                    pool.wait_ge(ld_gb[i], 16 * E * d + 16 * E)
                    for j in range(MT):
                        gate(2 * d + i, i, j)


_INS = ["x", "cond_1024", "ctx_1024", "L0_xcond_attn1_wq", "L0_xcond_attn1_wk", "L0_xcond_attn1_wv",
        "L0_xcond_attn1_wo", "L0_xcond_attn1_bo", "L0_xcond_attn2_wq", "L0_xcond_attn2_wk", "L0_xcond_attn2_wv",
        "L0_xcond_attn2_wo", "L0_xcond_attn2_bo", "L0_xcond_ff_w1", "L0_xcond_ff_b1", "L0_xcond_ff_w2",
        "L0_xcond_ff_b2", "L0_xcond_norm1_w", "L0_xcond_norm1_b", "L0_xcond_norm2_w", "L0_xcond_norm2_b",
        "L0_xcond_norm3_w", "L0_xcond_norm3_b", "L0_ffn_wqkv", "L0_ffn_w1", "L0_ffn_w2"]


def kernel(**inputs):
    import numpy as _np
    import concourse.bacc as _bacc
    from concourse import mybir as _mybir
    from concourse.bass_utils import run_bass_kernel_spmd as _run

    nc = _bacc.Bacc("TRN2", target_bir_lowering=False, num_devices=1)
    arrays, t_in = {}, {}
    for name in _INS:
        a = _np.ascontiguousarray(inputs[name])
        arrays[f"in_{name}_dram"] = a
        t_in[name] = nc.dram_tensor(f"in_{name}_dram", a.shape, _mybir.dt.from_np(a.dtype), kind="ExternalInput").ap()
    out = nc.dram_tensor("out_dram", inputs["x"].shape, _mybir.dt.float32, kind="ExternalOutput").ap()
    pixart_block_moe(nc, t_in, out)
    r = _run(nc, [arrays], core_ids=[0])
    return r.results[0]["out_dram"]
```
